# Optimizing a Trainium2 kernel written in Bass

```python
import numpy as np
import jax
import jax.numpy as jnp

def _softmax(x, axis=-1):
    return jax.nn.softmax(x, axis=axis)

def _gelu(x):
    return jax.nn.gelu(x, approximate=True)

def _silu(x):
    return jax.nn.silu(x)

def _sigmoid(x):
    return jax.nn.sigmoid(x)

def _layernorm(x, axis=-1, eps=1e-05):
    m = jnp.mean(x, axis=axis, keepdims=True)
    v = jnp.var(x, axis=axis, keepdims=True)
    return (x - m) / jnp.sqrt(v + eps)

def _scatter_add(tgt, idx, src, axis=0):
    return tgt.at[idx].add(src)

def _segment_sum(src, seg, n):
    return jax.ops.segment_sum(src, seg, n)
kernel_name = 'mk_gnn_preln_d4_gnn_r32_7e2ba3'

def setup_inputs(seed: int=0):
    np.random.seed(seed)
    _w = jnp.asarray

    def _rec_inputs():
        import jax
        import jax.numpy as jnp
        _gk = jax.random.key(seed)
        x = -0.0003713 + 1 * jax.random.normal(jax.random.fold_in(_gk, 1), (3125, 128), jnp.float32)
        src = jax.random.randint(jax.random.fold_in(_gk, 2), (100000,), 0, 3125, jnp.int32)
        dst = jax.random.randint(jax.random.fold_in(_gk, 3), (100000,), 0, 3125, jnp.int32)
        _o = jnp.argsort(dst, stable=True)
        src = src[_o]
        dst = dst[_o]
        edge_attr_16 = 0.000268479 + 0.999861 * jax.random.normal(jax.random.fold_in(_gk, 11), (100000, 16), jnp.float32)
        return (x, src, dst, edge_attr_16)
    x, src, dst, edge_attr_16 = _rec_inputs()

    def _L0_gnn_setup():
        import jax, jax.numpy as jnp
        import numpy as np
        N = 3125
        E = 25000
        D = 128
        OUT = 128
        key = jax.random.key(seed)
        k = jax.random.split(key, 6)
        x = jax.random.normal(k[0], (N, D), dtype=jnp.float32)
        edge_index = jax.random.randint(k[1], (2, E), 0, N, dtype=jnp.int64)
        Wl = jax.random.normal(k[2], (D, OUT), dtype=jnp.float32) / np.sqrt(D)
        bl = jax.random.normal(k[3], (OUT,), dtype=jnp.float32) * 0.01
        Wr = jax.random.normal(k[4], (D, OUT), dtype=jnp.float32) / np.sqrt(D)
        br = jax.random.normal(k[5], (OUT,), dtype=jnp.float32) * 0.01
        return {'x': x, 'edge_index': edge_index, 'Wl': Wl, 'bl': bl, 'Wr': Wr, 'br': br}
    _L0_gnn_all = _L0_gnn_setup()
    _L0_gnn_in = {k: v for k, v in _L0_gnn_all.items() if k in ('Wl', 'bl', 'Wr', 'br')}
    del _L0_gnn_all

    def _L1_gnn_setup():
        import jax, jax.numpy as jnp
        import numpy as np
        HEADS = 4
        OUT_F = 32
        EDGE_F = 16
        ALPHA = 0.2
        key = jax.random.key(seed)
        k1, k2, k3, k4, k5 = jax.random.split(key, 5)
        N, E, IN_F = (625, 20000, 128)
        h = jax.random.normal(k1, (N, IN_F), dtype=jnp.float32)
        edge_index = jax.random.randint(k2, (2, E), 0, N, dtype=jnp.int64)
        edge_attr = jax.random.normal(k3, (E, EDGE_F), dtype=jnp.float32)
        W = jax.random.normal(k4, (IN_F, HEADS * OUT_F), dtype=jnp.float32) * 0.1
        a = jax.random.normal(k5, (HEADS, 2 * OUT_F + EDGE_F), dtype=jnp.float32) * 0.1
        return {'h': h, 'edge_index': edge_index, 'edge_attr': edge_attr, 'W': W, 'a': a}
    _L1_gnn_all = _L1_gnn_setup()
    _L1_gnn_in = {k: v for k, v in _L1_gnn_all.items() if k in ('W', 'a')}
    del _L1_gnn_all

    def _L2_gnn_setup():
        import jax, jax.numpy as jnp
        import numpy as np
        N_NODES = 50000
        N_EDGES = 25000
        D = 128
        N_LAYERS = 5

        def _max_agg_conv(x, src, dst, W, b, n_nodes):
            h = jnp.einsum('nd,od->no', x, W) + b
            m = jax.ops.segment_max(h[src], dst, num_segments=n_nodes)
            return jnp.where(jnp.isneginf(m), 0.0, m)
        key = jax.random.key(seed)
        k1, k2, k3, k4 = jax.random.split(key, 4)
        x = jax.random.normal(k1, (N_NODES, D), dtype=jnp.float32)
        edge_index = jax.random.randint(k2, (2, N_EDGES), 0, N_NODES, dtype=jnp.int64)
        Ws = jax.random.normal(k3, (N_LAYERS, D, D), dtype=jnp.float32) * (1.0 / np.sqrt(D))
        bs = jax.random.normal(k4, (N_LAYERS, D), dtype=jnp.float32) * 0.01
        return {'x': x, 'edge_index': edge_index, 'Ws': Ws, 'bs': bs}
    _L2_gnn_all = _L2_gnn_setup()
    _L2_gnn_in = {k: v for k, v in _L2_gnn_all.items() if k in ('Ws', 'bs')}
    del _L2_gnn_all

    def _L3_gnn_setup():
        import jax, jax.numpy as jnp
        import numpy as np
        N, D, E = (50000, 128, 25000)
        key = jax.random.key(seed)
        k1, k2, k3, k4 = jax.random.split(key, 4)
        x = jax.random.normal(k1, (N, D), dtype=jnp.float32)
        edge_index = jax.random.randint(k2, (2, E), 0, N, dtype=jnp.int64)
        lim = 1.0 / np.sqrt(D)
        W = jax.random.uniform(k3, (D, D), minval=-lim, maxval=lim, dtype=jnp.float32)
        b = jax.random.uniform(k4, (D,), minval=-lim, maxval=lim, dtype=jnp.float32)
        return {'x': x, 'edge_index': edge_index, 'W': W, 'b': b}
    _L3_gnn_all = _L3_gnn_setup()
    _L3_gnn_in = {k: v for k, v in _L3_gnn_all.items() if k in ('W', 'b')}
    del _L3_gnn_all
    return {'x': x, 'src': src, 'dst': dst, 'edge_attr_16': edge_attr_16, 'L0_gnn_Wl': _L0_gnn_in['Wl'], 'L0_gnn_bl': _L0_gnn_in['bl'], 'L0_gnn_Wr': _L0_gnn_in['Wr'], 'L0_gnn_br': _L0_gnn_in['br'], 'L1_gnn_W': _L1_gnn_in['W'], 'L1_gnn_a': _L1_gnn_in['a'], 'L2_gnn_Ws': _L2_gnn_in['Ws'], 'L2_gnn_bs': _L2_gnn_in['bs'], 'L3_gnn_W': _L3_gnn_in['W'], 'L3_gnn_b': _L3_gnn_in['b']}

def reference(x, src, dst, edge_attr_16, L0_gnn_Wl, L0_gnn_bl, L0_gnn_Wr, L0_gnn_br, L1_gnn_W, L1_gnn_a, L2_gnn_Ws, L2_gnn_bs, L3_gnn_W, L3_gnn_b):
    import jax
    import jax.numpy as jnp

    def _L0_gnn_ref(x, edge_index, Wl, bl, Wr, br):
        import jax, jax.numpy as jnp
        import numpy as np
        N = 3125
        E = 25000
        D = 128
        OUT = 128
        n = x.shape[0]
        tgt = edge_index[0]
        nbr = edge_index[1]
        agg_sum = jax.ops.segment_sum(x[nbr], tgt, num_segments=n)
        deg = jax.ops.segment_sum(jnp.ones((edge_index.shape[1],), x.dtype), tgt, num_segments=n)
        agg = agg_sum / jnp.maximum(deg, 1.0)[:, None]
        out = jax.nn.relu(x @ Wl + bl + agg @ Wr + br)
        norm = jnp.linalg.norm(out, axis=1, keepdims=True) + 1e-06
        return out / norm

    def _L1_gnn_ref(h, edge_index, edge_attr, W, a):
        import jax, jax.numpy as jnp
        import numpy as np
        HEADS = 4
        OUT_F = 32
        EDGE_F = 16
        ALPHA = 0.2
        N = h.shape[0]
        Wh = (h @ W).reshape(N, HEADS, OUT_F)
        src = edge_index[0]
        dst = edge_index[1]
        a_src = a[:, :OUT_F]
        a_dst = a[:, OUT_F:2 * OUT_F]
        a_edge = a[:, 2 * OUT_F:]
        e = jnp.einsum('ehd,hd->eh', Wh[src], a_src) + jnp.einsum('ehd,hd->eh', Wh[dst], a_dst) + edge_attr @ a_edge.T
        e = jnp.where(e >= 0, e, ALPHA * e)
        attention = jax.nn.softmax(e, axis=1)
        msg = attention[:, :, None] * Wh[dst]
        h_prime = jnp.zeros_like(Wh).at[src].add(msg)
        out = h_prime.reshape(N, HEADS * OUT_F)
        return jax.nn.elu(out)

    def _L2_gnn_ref(x, edge_index, Ws, bs):
        import jax, jax.numpy as jnp
        import numpy as np
        N_NODES = 50000
        N_EDGES = 25000
        D = 128
        N_LAYERS = 5

        def _max_agg_conv(x, src, dst, W, b, n_nodes):
            h = jnp.einsum('nd,od->no', x, W) + b
            m = jax.ops.segment_max(h[src], dst, num_segments=n_nodes)
            return jnp.where(jnp.isneginf(m), 0.0, m)
        src = edge_index[0]
        dst = edge_index[1]
        n = x.shape[0]
        for i in range(N_LAYERS - 1):
            x = _max_agg_conv(x, src, dst, Ws[i], bs[i], n)
            x = jax.nn.silu(x)
        x = _max_agg_conv(x, src, dst, Ws[N_LAYERS - 1], bs[N_LAYERS - 1], n)
        return x

    def _L3_gnn_ref(x, edge_index, W, b):
        import jax, jax.numpy as jnp
        import numpy as np
        N, D, E = (50000, 128, 25000)
        src, dst = (edge_index[0], edge_index[1])
        full_src = jnp.concatenate([src, dst], axis=0)
        full_dst = jnp.concatenate([dst, src], axis=0)
        msg = x[full_src]
        agg = jax.ops.segment_sum(msg, full_dst, num_segments=x.shape[0])
        deg = jax.ops.segment_sum(jnp.ones((full_dst.shape[0],), dtype=x.dtype), full_dst, num_segments=x.shape[0])
        deg = jnp.sqrt(jnp.maximum(deg, 1.0))[:, None]
        out = agg / deg
        out = out @ W.T + b
        out = out + x
        out = jax.nn.gelu(out, approximate=False)
        return out
    edge_index = jnp.stack([src, dst])
    h = jnp.maximum(_layernorm(x, axis=-1), 0.0)
    x = x + _L0_gnn_ref(h, edge_index, L0_gnn_Wl, L0_gnn_bl, L0_gnn_Wr, L0_gnn_br)
    h = jnp.maximum(_layernorm(x, axis=-1), 0.0)
    x = x + _L1_gnn_ref(h, edge_index, edge_attr_16, L1_gnn_W, L1_gnn_a)
    h = jnp.maximum(_layernorm(x, axis=-1), 0.0)
    x = x + _L2_gnn_ref(h, edge_index, L2_gnn_Ws, L2_gnn_bs)
    h = jnp.maximum(_layernorm(x, axis=-1), 0.0)
    x = x + _L3_gnn_ref(h, edge_index, L3_gnn_W, L3_gnn_b)
    return x

_drawn_inputs = setup_inputs


def setup_inputs(seed=0):
    import zlib

    import numpy as np

    out = dict(_drawn_inputs(seed))
    spreads = {}
    factors = {'L0_gnn_bl': 64.0, 'L0_gnn_br': 45.94, 'L2_gnn_bs': 22.75, 'L3_gnn_b': 7.62}
    for name, (base, spread) in spreads.items():
        noise = np.random.default_rng([zlib.crc32(name.encode()), seed]).standard_normal(out[name].shape)
        drawn = base * np.exp(spread * noise) if base else spread * noise
        out[name] = jnp.asarray(drawn.astype(out[name].dtype))
    for name, factor in factors.items():
        out[name] = (out[name] * factor).astype(out[name].dtype)
    return out
```

```python
import concourse.bass as bass
from concourse import mybir
from concourse.alu_op_type import AluOpType as ALU
from contextlib import ExitStack

F32 = mybir.dt.float32
F16 = mybir.dt.float16
I32 = mybir.dt.int32
ACT = mybir.ActivationFunctionType
AX = mybir.AxisListType

P = 128
NODES = 3125
EDGES = 100000
D = 128
TILES = -(-NODES // P)
PAD_NODES = P * TILES
STEPS = -(-EDGES // P)
PAD_EDGES = P * STEPS
HEADS, HEAD_D, EDGE_F = 4, 32, 16
ROUNDS = 5
RING = 2
K = 17
CHUNKS = STEPS // K
LOOPS = CHUNKS // RING
assert K * CHUNKS == STEPS and LOOPS * RING == CHUNKS
BIG = 3.4028234e38
HALF = PAD_EDGES // 2
ZERO_ROW = PAD_EDGES
SPARE = PAD_EDGES + 1
SCAN_ROWS = SPARE + P
WIDE = D + HEADS
PAYLOAD = 2 + HEADS

GROUP = 4
STEP_GROUPS = [(a, min(GROUP, K - a)) for a in range(0, K, GROUP)]
NSG = len(STEP_GROUPS)
TILE_GROUPS = [(a, min(GROUP, TILES - a)) for a in range(0, TILES, GROUP)]
NTG = len(TILE_GROUPS)

P_SAGE, P_ATT, P_MAX, P_GCN_S, P_GCN_D = 0, 1, 2, 2 + ROUNDS, 3 + ROUNDS
J_L, J_R, J_WH, J_CONV, J_GCN = 0, 1, 2, 3, 3 + ROUNDS


class Steps:

    def __init__(self, eng, sem):
        self.eng, self.sem, self.n, self.at, self.outer = eng, sem, 0, None, []

    def __call__(self, ins):
        self.begin(ins)
        self.wait()

    def begin(self, ins):
        ins.then_inc(self.sem, 1)
        self.n += 1

    def wait(self):
        self.eng.wait_ge(self.sem, self.value())

    def value(self):
        return self.n if self.at is None else self.at + self.n

    def enter(self, turn, per):
        self.outer.append((self.n, self.at, per))
        self.at, self.n = turn * per + self.value(), 0

    def leave(self, turns):
        n, at, per = self.outer.pop()
        assert self.n == per, (self.n, per)
        self.n, self.at = n + per * turns, at


def build(nc, x, src, dst, edge_attr, Wl, Wr, W1, W2T, W3T, bl, br, b2, b3, att, out):
    es = ExitStack()
    with es:
        def sb(name, shape, dt=F32):
            return es.enter_context(nc.sbuf_tensor(name, shape, dt))

        def sem(name):
            return es.enter_context(nc.semaphore(name))

        table = nc.dram_tensor("table", (PAD_NODES, D), F32).ap()
        wide_table = nc.dram_tensor("wide_table", (PAD_NODES, WIDE), F32).ap()
        src_term_table = nc.dram_tensor("src_term_table", (PAD_NODES, HEADS), F32).ap()
        end_table = [nc.dram_tensor(f"end_table_{o}", (PAD_NODES, 1), F32).ap() for o in "sd"]
        payload_sorted = nc.dram_tensor("payload_sorted", (PAD_EDGES, PAYLOAD), F32).ap()
        src_term_at_start = nc.dram_tensor("src_term_at_start", (PAD_EDGES + PAD_NODES, HEADS), F32).ap()
        running = [nc.dram_tensor(f"running_{o}", (SCAN_ROWS, D), F32).ap() for o in "sd"]
        running_pk = [r[0:PAD_EDGES, :].rearrange("(p s) d -> p (s d)", s=STEPS) for r in running]

        X = sb("X", [P, TILES, D])
        H = sb("H", [P, TILES, D])
        R = sb("R", [P, TILES, D])
        U = sb("U", [P, TILES, D])
        V = sb("V", [P, TILES, D])
        src_i = sb("src_i", [P, STEPS], I32)
        dst_i = sb("dst_i", [P, STEPS], I32)
        ids = [dst_i, src_i]
        key = sb("key", [P, STEPS])
        dst_f = sb("dst_f", [P, STEPS])
        src_hi = sb("src_hi", [P, STEPS + K])
        src_lo = sb("src_lo", [P, STEPS + K])
        dst_hi = sb("dst_hi", [P, STEPS + K])
        dst_lo = sb("dst_lo", [P, STEPS + K])
        cont = [sb("cont_s", [P, STEPS]), sb("cont_d", [P, STEPS])]
        limit = sb("limit", [P, STEPS])
        sorted_sb = sb("sorted_sb", [P, STEPS, PAYLOAD])
        terms = sb("terms", [P, STEPS, HEADS])
        gathered = [sb(f"gathered{s}", [P, K, WIDE]) for s in range(RING)]
        scanned = [sb(f"scanned{s}", [P, K, D]) for s in range(RING)]
        index_ring = [sb(f"index_ring{s}", [P, K], I32) for s in range(RING)]
        hi_hot = [scanned[s][:].rearrange("p k d -> p (k d)").bitcast(F16)[:, 0:K * P]
                  .rearrange("p (k n) -> p k n", k=K) for s in range(RING)]
        lo_hot = [sb(f"lo_hot{s}", [P, K, TILES], F16)[:] for s in range(RING)]
        in_r = R[:].rearrange("p t d -> p (t d)").bitcast(F16)
        dhi_hot = [in_r[:, s * K * P:(s + 1) * K * P].rearrange("p (k n) -> p k n", k=K) for s in range(RING)]
        dlo_hot = [in_r[:, RING * K * P + s * K * TILES:RING * K * P + (s + 1) * K * TILES]
                   .rearrange("p (k n) -> p k n", k=K) for s in range(RING)]
        place_tables = [sb(f"place_tables{s}", [P, TILES, K + 1]) for s in range(RING)]
        place_parts = [sb(f"place_parts{s}", [P, 2, TILES, K + 1], F16) for s in range(RING)]
        hi_hot_T = [sb(f"hi_hot_T{s}", [P, GROUP, P], F16) for s in range(RING)]
        same_hi = [sb(f"same_hi{s}", [P, GROUP, P], F16) for s in range(RING)]
        attr = [sb(f"attr{s}", [P, K, EDGE_F]) for s in range(RING)]
        payload = [sb(f"payload{s}", [P, K, PAYLOAD]) for s in range(RING)]
        hT = [sb(f"hT{s}", [P, GROUP, P]) for s in range(RING)]
        iota_i = sb("iota_i", [P, P], I32)
        row_i = sb("row_i", [P, 1], I32)
        iota = sb("iota", [P, P])
        row = sb("row", [P, 1])
        ident = sb("ident", [P, P])
        ident_b = sb("ident_b", [P, P], F16)
        later = sb("later", [P, P])
        ones = sb("ones", [P, P])
        zeros_b = sb("zeros_b", [P, P], F16)
        not_first = sb("not_first", [P, TILES, K + 1])
        place_next = sb("place_next", [P, TILES])
        place_products = gathered[0][:].rearrange("p k w -> p (k w)")[:, 0:K * TILES]\
            .rearrange("p (k t) -> p k t", k=K)
        attr_products = gathered[1][:].rearrange("p k w -> p (k w)")[:, 0:K * HEADS * EDGE_F]\
            .rearrange("p (k h f) -> p k h f", k=K, h=HEADS)
        degree = [sb("degree_s", [P, TILES]), sb("degree_d", [P, TILES])]
        start = [sb("start_s", [P, TILES]), sb("start_d", [P, TILES])]
        end = [sb("end_s", [P, TILES]), sb("end_d", [P, TILES])]
        has_edges = [sb("has_edges_s", [P, TILES]), sb("has_edges_d", [P, TILES])]
        place_sums = sb("place_sums", [P, K])
        last_row = [sb("last_row_s", [P, TILES], I32), sb("last_row_d", [P, TILES], I32)]
        start_row = sb("start_row", [P, TILES], I32)
        spare_row = sb("spare_row", [P, TILES])
        tmp_t = sb("tmp_t", [P, TILES])
        tmp_u = sb("tmp_u", [P, TILES])
        key0_i = [sb("key0_s", [P, 1], I32), sb("key0_d", [P, 1], I32)]
        key_before_f = sb("key_before_f", [P, 1])
        key_before_i = sb("key_before_i", [P, 1], I32)
        end_of_first = [sb("end_of_first_s", [P, 1]), sb("end_of_first_d", [P, 1])]
        fix_row = [sb("fix_row_s", [P, 1], I32), sb("fix_row_d", [P, 1], I32)]
        unbroken = [sb("unbroken_s", [P, P]), sb("unbroken_d", [P, P])]
        unbroken_limit = sb("unbroken_limit", [P, P])
        tmp_1 = sb("tmp_1", [P, 1])
        tmp_2 = sb("tmp_2", [P, 1])
        tmp_3 = sb("tmp_3", [P, 1])
        diag = sb("diag", [P, P])
        state = sb("state", [P, D])
        joined_T = sb("joined_T", [P, P + 1])
        fix_rows = sb("fix_rows", [P, D])
        logit = sb("logit", [P, K, HEADS])
        top = sb("top", [P, K])
        stat = sb("stat", [P, TILES])
        stat2 = sb("stat2", [P, TILES])
        dst_term = sb("dst_term", [P, TILES, HEADS])
        src_term = sb("src_term", [P, TILES, HEADS])
        w_l, w_r, w_1, w_3 = (sb(n, [P, D]) for n in ("w_l", "w_r", "w_1", "w_3"))
        w_2 = sb("w_2", [P, ROUNDS, D])
        bias_l, bias_r, bias_3 = (sb(n, [P, D]) for n in ("bias_l", "bias_r", "bias_3"))
        bias_2 = sb("bias_2", [P, ROUNDS, D])
        att_w = sb("att_w", [P, HEADS, 2 * HEAD_D + EDGE_F])
        bank = [es.enter_context(nc.psum_tensor(f"bank{b}", [P, 512], F32)) for b in range(8)]

        delta_ps = bank[0][:, 0:TILES * (K + 1)].rearrange("p (t k) -> p t k", k=K + 1)
        place_ps = bank[1][:, 0:K * TILES].rearrange("p (k t) -> p k t", k=K)
        same_ps = [bank[3 + s][:, :].rearrange("p (j e) -> p j e", j=GROUP) for s in range(RING)]
        hot_T_ps = [bank[b][:, 0:256].bitcast(F16).rearrange("p (j e) -> p j e", j=GROUP) for b in (2, 5)]
        count_ps = [bank[6][:, 0:TILES], bank[7][:, 0:TILES]]
        offset_ps = bank[6][:, 32:33]
        hT_ps = [bank[s][:, :].rearrange("p (j n) -> p j n", j=GROUP) for s in range(RING)]
        prod_ps = [bank[2 + s][:, :].rearrange("p (j o) -> p j o", j=GROUP) for s in range(RING)]
        state_T_ps = bank[4][:, 0:P]
        joined_ps = bank[5][:, 0:P]
        unbroken_ps = bank[6][:, 0:P]

        iota_made = sem("iota_made")
        edges_loaded = sem("edges_loaded")
        x_loaded = sem("x_loaded")
        weights_loaded = sem("weights_loaded")
        vec = sem("vec")
        constants_made = sem("constants_made")
        zeros_made = sem("zeros_made")
        zeros_stored = sem("zeros_stored")
        count_hot_made = sem("count_hot_made")
        count_hot_used = sem("count_hot_used")
        counted = sem("counted")
        totals_made = sem("totals_made")
        offsets_made = sem("offsets_made")
        hot_made = sem("hot_made")
        deltas_made = sem("deltas_made")
        tables_made = sem("tables_made")
        hot_T_made = sem("hot_T_made")
        hot_T_copied = sem("hot_T_copied")
        same_made = sem("same_made")
        same_masked = sem("same_masked")
        group_placed = sem("group_placed")
        places_read = sem("places_read")
        attr_loaded = [sem(f"attr_loaded{s}") for s in range(RING)]
        attr_used = sem("attr_used")
        payload_made = sem("payload_made")
        scattered = [sem(f"scattered{s}") for s in range(RING)]
        payload_free = sem("payload_free")
        scattering = sem("scattering")
        sorted_loaded = sem("sorted_loaded")
        ends_made = sem("ends_made")
        ends_stored = sem("ends_stored")
        key0_made = sem("key0_made")
        first_ends_read = sem("first_ends_read")
        diag_made = sem("diag_made")
        unbroken_read = sem("unbroken_read")
        rows_free = sem("rows_free")
        index_copied = sem("index_copied")
        gathering = sem("gathering")
        rows_gathered = [sem(f"rows_gathered{s}") for s in range(RING)]
        chunk_scanned = sem("chunk_scanned")
        running_stored = sem("running_stored")
        scan_slot_free = sem("scan_slot_free")
        logits_shifted = sem("logits_shifted")
        exps_made = sem("exps_made")
        state_ready = sem("state_ready")
        state_T_made = sem("state_T_made")
        joined_T_made = sem("joined_T_made")
        joined_made = sem("joined_made")
        fix_read = sem("fix_read")
        fix_made = sem("fix_made")
        fix_written = sem("fix_written")
        nodes_read = [sem(f"nodes_read{g}") for g in range(NTG)]
        product_input = sem("product_input")
        tiles_T_made = sem("tiles_T_made")
        tiles_T_copied = sem("tiles_T_copied")
        product_made = sem("product_made")
        product_read = sem("product_read")
        silu_made = sem("silu_made")
        squares_summed = sem("squares_summed")
        roots_made = sem("roots_made")
        table_ready = sem("table_ready")
        table_stored = sem("table_stored")
        wide_stored = sem("wide_stored")
        src_terms_ready = sem("src_terms_ready")
        src_terms_stored = sem("src_terms_stored")
        src_terms_scattered = sem("src_terms_scattered")
        src_terms_loaded = sem("src_terms_loaded")
        first_terms_read = sem("first_terms_read")
        elu_input = sem("elu_input")
        elu_exp = sem("elu_exp")
        gelu_input = sem("gelu_input")
        gelu_made = sem("gelu_made")
        out_ready = sem("out_ready")
        out_stored = sem("out_stored")
        block = es.enter_context(nc.Block())

        by_node = lambda t: t.rearrange("(p t) d -> p t d", t=TILES)
        chunk = lambda n: bass.ds(n * K, K)

        @block.sync
        def _(sp):
            per_edge = lambda a: a.rearrange("(p s) -> p s", s=STEPS)
            sp.dma_start(src_i[:], per_edge(src)).then_inc(edges_loaded, 16)
            sp.dma_start(dst_i[:], per_edge(dst)).then_inc(edges_loaded, 16)
            sp.wait_ge(zeros_made, 1)
            with nc.allow_non_contiguous_dma(reason="one word of each partition"):
                sp.dma_start(key_before_i[1:P, :], per_edge(dst)[0:P - 1, STEPS - 1:STEPS]).then_inc(edges_loaded, 16)
            sp.dma_start(X[:], by_node(x)).then_inc(x_loaded, 16)
            for tile, a in ((w_l[:], Wl), (w_r[:], Wr), (w_1[:], W1), (w_3[:], W3T),
                            (w_2[:], W2T.rearrange("r i o -> i r o")),
                            (bias_l[:], bl.broadcast_to([P, D])), (bias_r[:], br.broadcast_to([P, D])),
                            (bias_3[:], b3.broadcast_to([P, D])),
                            (bias_2[:].rearrange("p r d -> p (r d)"), b2.broadcast_to([P, ROUNDS * D])),
                            (att_w[:].rearrange("p h a -> p (h a)"),
                             att.broadcast_to([P, HEADS * (2 * HEAD_D + EDGE_F)]))):
                sp.dma_start(tile, a).then_inc(weights_loaded, 16)
            sp.dma_start(src_term_at_start[0:PAD_EDGES, :].rearrange("(p s) h -> p (s h)", s=STEPS),
                         terms[:].rearrange("p s h -> p (s h)")).then_inc(zeros_stored, 16)
            for r in running:
                sp.dma_start(r[ZERO_ROW:ZERO_ROW + 1, :], terms[0:1, 0:D // HEADS, :].rearrange("p s h -> p (s h)"))\
                    .then_inc(zeros_stored, 16)
                sp.dma_start(r[SPARE:SCAN_ROWS, :], terms[:, 0:D // HEADS, :].rearrange("p s h -> p (s h)"))\
                    .then_inc(zeros_stored, 16)

            sp.sem_inc(payload_free, RING)
            with sp.Fori(0, LOOPS) as i:
                for s in range(RING):
                    sp.wait_ge(scattered[s], (i + 1) * (16 * K))
                    sp.sem_inc(payload_free, 1)
            sorted_pk = payload_sorted.rearrange("(p s) c -> p s c", s=STEPS)
            sp.dma_start(sorted_sb[:], sorted_pk).then_inc(sorted_loaded, 16)
            with nc.allow_non_contiguous_dma(reason="one word of each partition"):
                sp.dma_start(key_before_f[1:P, :], sorted_pk[0:P - 1, STEPS - 1, 1:2]).then_inc(sorted_loaded, 16)

            def store_ends(order):
                sp.wait_ge(ends_made, order + 1)
                with nc.allow_non_contiguous_dma(reason="a word of each node"):
                    sp.dma_start(by_node(end_table[order]), end[order][:].unsqueeze(2)).then_inc(ends_stored, 16)

            store_ends(0)

            def store_table(groups_before, rows):
                for g, (a, m) in enumerate(TILE_GROUPS):
                    sp.wait_ge(table_ready, groups_before + g + 1)
                    sp.dma_start(by_node(table)[:, a:a + m, :], rows[:, a:a + m, :]).then_inc(table_stored, 16)

            def store_running(pass_no, order):
                with sp.Fori(0, LOOPS) as i:
                    for s in range(RING):
                        n = i * RING + s + pass_no * CHUNKS
                        sp.wait_ge(chunk_scanned, n + 1)
                        sp.dma_start(running_pk[order][:, bass.ds((i * RING + s) * (K * D), K * D)],
                                     scanned[s][:].rearrange("p k d -> p (k d)")).then_inc(running_stored, 16)
                        sp.wait_ge(running_stored, (n + 1) * 16)
                        sp.sem_inc(scan_slot_free, 1)

            sp.sem_inc(scan_slot_free, RING)
            store_table(0, H)
            store_running(P_SAGE, 0)
            sp.wait_ge(src_terms_ready, 1)
            with nc.allow_non_contiguous_dma(reason="four words of each node"):
                sp.dma_start(by_node(src_term_table), src_term[:]).then_inc(src_terms_stored, 16)
                sp.dma_start(by_node(wide_table)[:, :, 0:D], U[:]).then_inc(wide_stored, 16)
                sp.dma_start(by_node(wide_table)[:, :, D:WIDE], dst_term[:]).then_inc(wide_stored, 16)
            store_ends(1)
            sp.wait_ge(src_terms_scattered, 16 * TILES)
            sp.dma_start(terms[:].rearrange("p s h -> p (s h)"),
                         src_term_at_start[0:PAD_EDGES, :].rearrange("(p s) h -> p (s h)", s=STEPS))\
                .then_inc(src_terms_loaded, 16)
            store_running(P_ATT, 0)
            store_table(NTG, U)
            with sp.Fori(0, ROUNDS - 1) as r:
                store_running(r + P_MAX, 1)
                store_table((r + 2) * NTG, U)
            store_running(P_MAX + ROUNDS - 1, 1)
            store_table((ROUNDS + 1) * NTG, H)
            store_running(P_GCN_S, 0)
            store_running(P_GCN_D, 1)
            sp.wait_ge(out_ready, 1)
            sp.dma_start(by_node(out), X[:]).then_inc(out_stored, 16)
            sp.wait_ge(out_stored, 16)
            sp.wait_ge(zeros_stored, 16 * 5)
            sp.wait_ge(table_stored, 16 * NTG * (ROUNDS + 2))

        @block.gpsimd
        def _(pool):
            pool.iota(iota_i[:], pattern=[[1, P]], base=0, channel_multiplier=0).then_inc(iota_made, 1)
            pool.iota(row_i[:], pattern=[[0, 1]], base=0, channel_multiplier=1).then_inc(iota_made, 1)

            def gather(out_, table_, index, done):
                pool.indirect_dma_start(out=out_, out_offset=None, in_=table_,
                                        in_offset=bass.IndirectOffsetOnAxis(ap=index, axis=0)).then_inc(done, 16)

            def scatter(table_, index, rows, done):
                pool.indirect_dma_start(out=table_, out_offset=bass.IndirectOffsetOnAxis(ap=index, axis=0),
                                        in_=rows, in_offset=None).then_inc(done, 16)

            with pool.Fori(0, LOOPS) as i:
                for s in range(RING):
                    n = i * RING + s
                    pool.wait_ge(payload_made, n + 1)
                    pool.sem_inc(scattering, 1)
                    for k in range(K):
                        scatter(payload_sorted, index_ring[s][:, k:k + 1], payload[s][:, k, :], scattered[s])

            def read_first_ends(order):
                pool.wait_ge(ends_stored, 16 * (order + 1))
                pool.wait_ge(key0_made, order + 1)
                gather(end_of_first[order][:], end_table[order], key0_i[order][:], first_ends_read)

            def gather_edges(pass_no, order, table_, width):
                with pool.Fori(0, LOOPS) as i:
                    for s in range(RING):
                        n = i * RING + s + pass_no * CHUNKS
                        pool.wait_ge(rows_free, n + 1)
                        pool.tensor_copy(index_ring[s][:], ids[order][:, chunk(i * RING + s)]).then_inc(index_copied, 1)
                        pool.wait_ge(index_copied, n + 1)
                        pool.sem_inc(gathering, 1)
                        for k in range(K):
                            to = gathered[s][:].rearrange("p k w -> p (k w)")[:, k * width:(k + 1) * width]
                            gather(to, table_, index_ring[s][:, k:k + 1], rows_gathered[s])

            def read_nodes(pass_no, order):
                pool.wait_ge(scan_slot_free, (pass_no + 1) * CHUNKS + RING)
                pool.sem_inc(gathering, 1)
                gather(fix_rows[:], running[order], fix_row[order][:], fix_read)
                pool.wait_ge(fix_made, pass_no + 1)
                pool.sem_inc(gathering, 1)
                scatter(running[order], fix_row[order][:], fix_rows[:], fix_written)
                pool.wait_ge(fix_written, (pass_no + 1) * 16)
                pool.sem_inc(gathering, 1)
                for g, (a, m) in enumerate(TILE_GROUPS):
                    for t in range(a, a + m):
                        gather(R[:, t, :], running[order], last_row[order][:, t:t + 1], nodes_read[g])

            pool.wait_ge(zeros_stored, 16 * 5)
            read_first_ends(0)
            pool.wait_ge(table_stored, 16 * NTG)
            gather_edges(P_SAGE, 0, table, D)
            read_nodes(P_SAGE, 0)
            pool.wait_ge(src_terms_ready, 1)
            for t in range(TILES):
                scatter(src_term_at_start, start_row[:, t:t + 1], src_term[:, t, :], src_terms_scattered)
            pool.wait_ge(src_terms_stored, 16)
            pool.wait_ge(src_terms_loaded, 16)
            gather(terms[:, 0, :], src_term_table, key0_i[0][:], first_terms_read)
            read_first_ends(1)
            pool.wait_ge(wide_stored, 32)
            gather_edges(P_ATT, 0, wide_table, WIDE)
            read_nodes(P_ATT, 0)
            pool.wait_ge(table_stored, 16 * NTG * 2)
            with pool.Fori(0, ROUNDS - 1) as r:
                gather_edges(r + P_MAX, 1, table, D)
                read_nodes(r + P_MAX, 1)
                pool.wait_ge(table_stored, r * (16 * NTG) + 16 * NTG * 3)
            gather_edges(P_MAX + ROUNDS - 1, 1, table, D)
            read_nodes(P_MAX + ROUNDS - 1, 1)
            pool.wait_ge(table_stored, 16 * NTG * (ROUNDS + 2))
            gather_edges(P_GCN_S, 0, table, D)
            read_nodes(P_GCN_S, 0)
            gather_edges(P_GCN_D, 1, table, D)
            read_nodes(P_GCN_D, 1)

        @block.tensor
        def _(pe):
            def count(order, his, los):
                nc.tensor.matmul(count_ps[order], zeros_b[:], zeros_b[:, 0:TILES], start=True, stop=False)
                with pe.Fori(0, LOOPS) as i:
                    for s in range(RING):
                        pe.wait_ge(count_hot_made, i * RING + s + 1 + order * CHUNKS)
                        for k in range(K):
                            last = nc.tensor.matmul(count_ps[order], his[s][:, k, :], los[s][:, k, :],
                                                    start=False, stop=False)
                        last.then_inc(count_hot_used, 1)
                nc.tensor.matmul(count_ps[order], zeros_b[:], zeros_b[:, 0:TILES], start=False, stop=True)\
                    .then_inc(counted, 1)

            pe.wait_ge(constants_made, 1)
            pe.sem_inc(count_hot_used, RING)
            count(0, hi_hot, lo_hot)

            def offsets(n):
                pe.wait_ge(totals_made, n)
                nc.tensor.matmul(offset_ps, later[:], tmp_1[:], start=True, stop=True).then_inc(offsets_made, 1)

            offsets(1)
            pe.sem_inc(group_placed, RING)
            with pe.Fori(0, LOOPS) as i:
                for s in range(RING):
                    n = i * RING + s
                    pe.wait_ge(hot_made, n + 1)
                    pe.wait_ge(tables_made, n + 1)
                    for k in range(K):
                        last = nc.tensor.matmul(delta_ps[:, :, k + 1], hi_hot[s][:, k, :], lo_hot[s][:, k, :],
                                                start=True, stop=True)
                    last.then_inc(deltas_made, 1)
                    for g in range(NSG + 2):
                        if g < NSG:
                            a, m = STEP_GROUPS[g]
                            c, r = n * NSG + g, (s * NSG + g) % RING
                            pe.wait_ge(hot_T_copied, c + 1)
                            for j in range(m):
                                last = nc.tensor.transpose(hot_T_ps[r][:, j, :], hi_hot[s][:, a + j, :], ident_b[:])
                            last.then_inc(hot_T_made, 1)
                        if 1 <= g <= NSG:
                            a, m = STEP_GROUPS[g - 1]
                            c, r = n * NSG + g - 1, (s * NSG + g - 1) % RING
                            pe.wait_ge(hot_T_copied, c + 1 + RING)
                            pe.wait_ge(same_masked, c + 1)
                            for j in range(m):
                                last = nc.tensor.matmul(same_ps[r][:, j, :], hi_hot_T[r][:, j, :], hi_hot_T[r][:, j, :],
                                                        start=True, stop=True)
                            last.then_inc(same_made, 1)
                        if g >= 2:
                            a, m = STEP_GROUPS[g - 2]
                            c, r = n * NSG + g - 2, (s * NSG + g - 2) % RING
                            if g == 2:
                                pe.wait_ge(tables_made, n + 2)
                                pe.wait_ge(places_read, n + 1)
                            pe.wait_ge(same_masked, c + 1 + RING)
                            for j in range(m):
                                for part in range(2):
                                    nc.tensor.matmul(place_ps[:, a + j, :], hi_hot_T[r][:, j, :],
                                                     place_parts[s][:, part, :, a + j], start=part == 0, stop=False)
                                last = nc.tensor.matmul(place_ps[:, a + j, :], same_hi[r][:, j, :],
                                                        lo_hot[s][:, a + j, :], start=False, stop=True)
                            last.then_inc(group_placed, 1)

            def spread_unbroken(order):
                pe.wait_ge(diag_made, order + 1)
                nc.tensor.matmul(unbroken_ps, ones[:], diag[:], start=True, stop=True).then_inc(unbroken_read, 1)

            spread_unbroken(0)

            def product(job, tiles, weight, ready):
                def transposes(g):
                    a, m = TILE_GROUPS[g]
                    ready(g)
                    if not (isinstance(job, int) and job == 0 and g < RING):
                        pe.wait_ge(tiles_T_copied, job * NTG + max(g - RING + 1, 0))
                    for j in range(m):
                        last = nc.tensor.transpose(hT_ps[g % RING][:, j, :], tiles[:, a + j, :], ident[:])
                    last.then_inc(tiles_T_made, 1)

                def products(g):
                    a, m = TILE_GROUPS[g]
                    pe.wait_ge(tiles_T_copied, job * NTG + g + 1)
                    if not (isinstance(job, int) and job == 0 and g < RING):
                        pe.wait_ge(product_read, job * NTG + max(g - RING + 1, 0))
                    for j in range(m):
                        last = nc.tensor.matmul(prod_ps[g % RING][:, j, :], hT[g % RING][:, j, :], weight,
                                                start=True, stop=True)
                    last.then_inc(product_made, 1)

                for g in range(NTG + 1):
                    if g < NTG:
                        transposes(g)
                    if g >= 1:
                        products(g - 1)

            def join(pass_no):
                pe.wait_ge(state_ready, pass_no + 1)
                nc.tensor.transpose(state_T_ps, state[:], ident[:]).then_inc(state_T_made, 1)
                pe.wait_ge(joined_T_made, pass_no + 1)
                nc.tensor.transpose(joined_ps, joined_T[:, 0:P], ident[:]).then_inc(joined_made, 1)

            inputs = lambda n: (lambda g: pe.wait_ge(product_input, n) if g == 0 else None)
            pe.wait_ge(weights_loaded, 160)
            product(J_L, H, w_l[:], inputs(1))
            count(1, dhi_hot, dlo_hot)
            join(P_SAGE)
            product(J_R, R, w_r[:], inputs(2))
            product(J_WH, H, w_1[:], inputs(3))
            offsets(2)
            spread_unbroken(1)
            join(P_ATT)
            product(J_CONV, H, w_2[:, 0, :], inputs(4))
            with pe.Fori(0, ROUNDS - 1) as r:
                join(r + P_MAX)
                product(r + J_CONV + 1, R, w_2[:, bass.ds(r + 1, 1), :].rearrange("p a o -> p (a o)"),
                        lambda g: pe.wait_ge(silu_made, r * NTG + g + 1))
            join(P_MAX + ROUNDS - 1)
            join(P_GCN_S)
            join(P_GCN_D)
            product(J_GCN, R, w_3[:], inputs(5))

        @block.scalar
        def _(act):
            act.wait_ge(constants_made, 1)
            act.sem_inc(hot_T_copied, RING)
            with act.Fori(0, LOOPS) as i:
                for s in range(RING):
                    n = i * RING + s
                    act.wait_ge(attr_used, n + 1)
                    act.dma_start(attr[s][:].rearrange("p k f -> p (k f)"),
                                  edge_attr.rearrange("(p s) f -> p (s f)", s=STEPS)[:, bass.ds(n * (K * EDGE_F), K * EDGE_F)])\
                        .then_inc(attr_loaded[s], 16)
                    for g, (a, m) in enumerate(STEP_GROUPS):
                        c, r = n * NSG + g, (s * NSG + g) % RING
                        act.wait_ge(hot_T_made, c + 1)
                        act.wait_ge(group_placed, c + 1)
                        nc.scalar.activation(hi_hot_T[r][:, 0:m, :], hot_T_ps[r][:, 0:m, :], ACT.Copy)\
                            .then_inc(hot_T_copied, 1)

            def transposed(job, g):
                a, m = TILE_GROUPS[g]
                act.wait_ge(tiles_T_made, job * NTG + g + 1)
                if not (isinstance(job, int) and job == 0 and g < RING):
                    act.wait_ge(product_made, job * NTG + max(g - RING + 1, 0))
                nc.scalar.activation(hT[g % RING][:, 0:m, :], hT_ps[g % RING][:, 0:m, :], ACT.Copy)\
                    .then_inc(tiles_T_copied, 1)

            def product(job):
                for g in range(NTG):
                    transposed(job, g)

            def root(n):
                act.wait_ge(squares_summed, n)
                nc.scalar.activation(stat2[:], stat[:], ACT.Sqrt).then_inc(roots_made, 1)

            root(1)
            product(J_L)
            product(J_R)
            root(2)
            root(3)
            product(J_WH)
            with act.Fori(0, CHUNKS) as i:
                act.wait_ge(logits_shifted, i + 1)
                nc.scalar.activation(logit[:], logit[:], ACT.Exp).then_inc(exps_made, 1)
            act.wait_ge(elu_input, 1)
            nc.scalar.activation(V[:], V[:], ACT.Exp).then_inc(elu_exp, 1)
            root(4)
            product(J_CONV)
            with act.Fori(0, ROUNDS - 1) as r:
                for g in range(NTG + 1):
                    if g < NTG:
                        a, m = TILE_GROUPS[g]
                        act.wait_ge(nodes_read[g], r * (16 * m) + 16 * m * (P_MAX + 1))
                        nc.scalar.activation(R[:, a:a + m, :], R[:, a:a + m, :], ACT.Silu).then_inc(silu_made, 1)
                    if g >= 1:
                        transposed(r + J_CONV + 1, g - 1)
            root(5)
            root(6)
            product(J_GCN)
            act.wait_ge(gelu_input, 1)
            nc.scalar.activation(U[:], U[:], ACT.Gelu).then_inc(gelu_made, 1)

        @block.vector
        def _(dve):
            v = nc.vector
            step = Steps(dve, vec)
            tiles = lambda a: a[:].unsqueeze(2).broadcast_to([P, TILES, D])

            step(v.memset(terms[:], 0.0))
            step(v.memset(key_before_i[:], -1))
            dve.sem_inc(zeros_made, 1)
            step(v.memset(key_before_f[:], -1.0))
            step(v.memset(ones[:], 1.0))
            step(v.memset(zeros_b[:], 0.0))
            step(v.memset(joined_T[:], 0.0))
            for a in (src_hi, src_lo, dst_hi, dst_lo):
                step(v.memset(a[:, STEPS:], 0.0))
            step(v.memset(not_first[:], 1.0))
            step(v.memset(not_first[:, :, 0], 0.0))
            dve.wait_ge(iota_made, 2)
            step(v.tensor_copy(iota[:], iota_i[:]))
            step(v.tensor_copy(row[:], row_i[:]))
            step(v.tensor_scalar(ident[:], iota[:], row[:], None, ALU.is_equal))
            step(v.tensor_scalar(ident_b[:], iota[:], row[:], None, ALU.is_equal))
            step(v.tensor_scalar(later[:], iota[:], row[:], None, ALU.is_gt))
            dve.sem_inc(constants_made, 1)
            dve.wait_ge(edges_loaded, 48)

            def split(ids_i, ids_f, hi, lo):
                step(v.tensor_copy(ids_f[:], ids_i[:]))
                step(v.tensor_scalar(sorted_sb[:, :, 0].bitcast(I32), ids_f[:], 1.0 / TILES, -0.48, ALU.mult, ALU.add))
                step(v.tensor_copy(hi[:, 0:STEPS], sorted_sb[:, :, 0].bitcast(I32)))
                step(v.scalar_tensor_tensor(out=lo[:, 0:STEPS], in0=hi[:, 0:STEPS], scalar=-float(TILES), in1=ids_f[:],
                                            op0=ALU.mult, op1=ALU.add))

            split(src_i, key, src_hi, src_lo)

            def one_hot(hot, width, value, n):
                return v.tensor_tensor(hot, iota[:, 0:width].unsqueeze(1).broadcast_to([P, K, width]),
                                       value[:, chunk(n)].unsqueeze(2).broadcast_to([P, K, width]), ALU.is_equal)

            with dve.Fori(0, LOOPS) as i:
                for s in range(RING):
                    n = i * RING + s
                    dve.wait_ge(count_hot_used, n + 1)
                    one_hot(hi_hot[s], P, src_hi, n)
                    one_hot(lo_hot[s], TILES, src_lo, n).then_inc(count_hot_made, 1)
            split(dst_i, dst_f, dst_hi, dst_lo)

            def bounds(order):
                dve.wait_ge(counted, order + 1)
                step(v.tensor_copy(degree[order][:], count_ps[order]))
                step(v.tensor_tensor_scan(end[order][:], ones[:, 0:TILES], degree[order][:], 0.0, ALU.mult, ALU.add))
                step(v.tensor_copy(tmp_1[:], end[order][:, TILES - 1:TILES]))
                dve.sem_inc(totals_made, 1)
                dve.wait_ge(offsets_made, order + 1)
                step(v.tensor_copy(tmp_2[:], offset_ps))
                step(v.tensor_scalar(end[order][:], end[order][:], tmp_2[:], None, ALU.add))
                step(v.tensor_tensor(start[order][:], end[order][:], degree[order][:], ALU.subtract))
                step(v.tensor_scalar(has_edges[order][:], degree[order][:], 0.0, None, ALU.is_gt))
                step(v.tensor_scalar(tmp_t[:], end[order][:], -1.0 - ZERO_ROW, None, ALU.add))
                step(v.tensor_tensor(tmp_t[:], tmp_t[:], has_edges[order][:], ALU.mult))
                step(v.tensor_scalar(last_row[order][:], tmp_t[:], float(ZERO_ROW), None, ALU.add))
                dve.sem_inc(ends_made, 1)

            bounds(0)
            step(v.tensor_scalar(tmp_1[:], row[:], float(TILES), float(PAD_EDGES), ALU.mult, ALU.add))
            step(v.tensor_scalar(spare_row[:], iota[:, 0:TILES], tmp_1[:], None, ALU.add))
            step(v.tensor_tensor(tmp_t[:], start[0][:], spare_row[:], ALU.subtract))
            step(v.tensor_tensor(tmp_t[:], tmp_t[:], has_edges[0][:], ALU.mult))
            step(v.tensor_tensor(start_row[:], tmp_t[:], spare_row[:], ALU.add))
            step(v.tensor_scalar(place_next[:], start[0][:], -float(HALF), None, ALU.add))
            dve.wait_ge(weights_loaded, 160)

            def all_hots(s, n):
                one_hot(hi_hot[s], P, src_hi, n)
                one_hot(lo_hot[s], TILES, src_lo, n).then_inc(hot_made, 1)

            dve.sem_inc(tables_made, 1)
            dve.sem_inc(same_masked, RING)
            dve.sem_inc(places_read, 1)
            dve.sem_inc(attr_used, RING)
            all_hots(0, 0)
            with dve.Fori(0, LOOPS) as i:
                step.enter(i, 9 * RING)
                for s in range(RING):
                    n = i * RING + s
                    dve.wait_ge(deltas_made, n + 1)
                    step(v.tensor_copy(delta_ps[:, :, 0], place_next[:]))
                    step(v.tensor_tensor_scan(place_tables[s][:].rearrange("p t k -> p (t k)"),
                                              not_first[:].rearrange("p t k -> p (t k)"),
                                              bank[0][:, 0:TILES * (K + 1)], 0.0, ALU.mult, ALU.add))
                    step(v.tensor_copy(place_next[:], place_tables[s][:, :, K]))
                    step(v.tensor_copy(place_parts[s][:, 0], place_tables[s][:]))
                    step(v.tensor_tensor(place_parts[s][:, 1], place_tables[s][:], place_parts[s][:, 0], ALU.subtract))
                    dve.sem_inc(tables_made, 1)
                    dve.wait_ge(group_placed, n * NSG + RING)
                    all_hots((s + 1) % RING, n + 1)
                    dve.wait_ge(attr_loaded[s], (i + 1) * 16)
                    dve.wait_ge(payload_free, n + 1)
                    step(v.tensor_tensor(attr_products, attr[s][:].unsqueeze(2).broadcast_to([P, K, HEADS, EDGE_F]),
                                         att_w[:, :, 2 * HEAD_D:].unsqueeze(1).broadcast_to([P, K, HEADS, EDGE_F]),
                                         ALU.mult))
                    dve.sem_inc(attr_used, 1)
                    v.tensor_reduce(payload[s][:, :, 2:PAYLOAD], attr_products, AX.X, ALU.add)
                    v.tensor_copy(payload[s][:, :, 0], dst_f[:, chunk(n)])
                    v.tensor_copy(payload[s][:, :, 1], key[:, chunk(n)])
                    for g, (a, m) in enumerate(STEP_GROUPS):
                        c, r = n * NSG + g, (s * NSG + g) % RING
                        dve.wait_ge(same_made, c + 1)
                        dve.wait_ge(group_placed, c + 1)
                        v.tensor_tensor(same_hi[r][:, 0:m, :], same_ps[r][:, 0:m, :],
                                        later[:].unsqueeze(1).broadcast_to([P, m, P]), ALU.mult)\
                            .then_inc(same_masked, 1)
                    dve.wait_ge(group_placed, n * NSG + NSG + RING)
                    step(v.tensor_tensor(place_products, place_ps, lo_hot[s], ALU.mult))
                    dve.sem_inc(places_read, 1)
                    step(v.tensor_reduce(place_sums[:], place_products, AX.X, ALU.add))
                    step(v.tensor_scalar(index_ring[s][:], place_sums[:], float(HALF), None, ALU.add))
                    dve.sem_inc(payload_made, 1)
                step.leave(LOOPS)

            def normalise(n):
                step(v.tensor_reduce(stat[:], X[:], AX.X, ALU.add))
                step(v.tensor_scalar(stat[:], stat[:], 1.0 / D, None, ALU.mult))
                step(v.tensor_tensor(H[:], X[:], tiles(stat), ALU.subtract))
                step(v.tensor_tensor(V[:], H[:], H[:], ALU.mult))
                step(v.tensor_reduce(stat[:], V[:], AX.X, ALU.add))
                step(v.tensor_scalar(stat[:], stat[:], 1.0 / D, 1e-5, ALU.mult, ALU.add))
                dve.sem_inc(squares_summed, 1)
                dve.wait_ge(roots_made, n)
                step(v.reciprocal(stat[:], stat2[:]))
                step(v.scalar_tensor_tensor(out=H[:], in0=H[:], scalar=0.0, in1=tiles(stat), op0=ALU.max, op1=ALU.mult))

            def read_product(job, add):
                for g, (a, m) in enumerate(TILE_GROUPS):
                    dve.wait_ge(product_made, job * NTG + g + 1)
                    to, got = U[:, a:a + m, :], prod_ps[g % RING][:, 0:m, :]
                    (v.tensor_tensor(to, got, add(a, m), ALU.add) if add else v.tensor_copy(to, got))\
                        .then_inc(product_read, 1)
                    yield g

            def drained(generator):
                for _ in generator:
                    pass

            def product_done(job):
                dve.wait_ge(product_read, job * NTG + NTG)

            bias = lambda b: (lambda a, m: b.unsqueeze(1).broadcast_to([P, m, D]))

            dve.wait_ge(x_loaded, 16)
            normalise(1)
            dve.sem_inc(table_ready, NTG)
            dve.sem_inc(product_input, 1)

            def runs(order, before):
                v.tensor_tensor(cont[order][:, 1:], key[:, 1:], key[:, 0:STEPS - 1], ALU.is_equal)
                v.tensor_tensor(cont[order][:, 0:1], key[:, 0:1], before, ALU.is_equal)
                step(v.tensor_copy(key0_i[order][:], key[:, 0:1]))

            def fixes(order):
                dve.wait_ge(first_ends_read, 16 * (order + 1))
                step(v.tensor_scalar(tmp_1[:], row[:], float(STEPS), float(STEPS), ALU.mult, ALU.add))
                step(v.tensor_tensor(tmp_2[:], end_of_first[order][:], tmp_1[:], ALU.is_le))
                step(v.tensor_tensor(tmp_2[:], tmp_2[:], cont[order][:, 0:1], ALU.mult))
                step(v.tensor_scalar(tmp_1[:], row[:], float(SPARE), None, ALU.add))
                step(v.scalar_tensor_tensor(out=tmp_3[:], in0=end_of_first[order][:], scalar=-1.0,
                                            in1=tmp_1[:], op0=ALU.add, op1=ALU.subtract))
                step(v.tensor_tensor(tmp_3[:], tmp_3[:], tmp_2[:], ALU.mult))
                step(v.tensor_tensor(fix_row[order][:], tmp_3[:], tmp_1[:], ALU.add))
                step(v.tensor_reduce(tmp_1[:], cont[order][:], AX.X, ALU.min))
                step(v.tensor_scalar(diag[:], ident[:], tmp_1[:], None, ALU.mult))
                dve.sem_inc(diag_made, 1)
                dve.wait_ge(unbroken_read, order + 1)
                step(v.tensor_copy(unbroken[order][:], unbroken_ps))
                if order:
                    step(v.tensor_scalar(unbroken_limit[:], unbroken[1][:], -0.5, None, ALU.add))
                    step(v.tensor_scalar(unbroken_limit[:], unbroken_limit[:], BIG, 2.0, ALU.mult, ALU.mult))

            dve.wait_ge(sorted_loaded, 32)
            step(v.tensor_copy(dst_i[:], sorted_sb[:, :, 0]))
            dve.sem_inc(rows_free, RING)
            step(v.tensor_copy(key[:], sorted_sb[:, :, 1]))
            runs(0, key_before_f[:])
            dve.sem_inc(key0_made, 1)
            fixes(0)
            drained(read_product(J_L, bias(bias_l[:])))
            product_done(J_L)
            step(v.tensor_tensor(U[:], U[:], bias_r[:].unsqueeze(1).broadcast_to([P, TILES, D]), ALU.add))

            def attention(n, s, first):
                rows = gathered[s][:].rearrange("p k w -> p (k w)").rearrange("p (k w) -> p k w", w=WIDE)
                over = lambda a: a[:].unsqueeze(2).broadcast_to([P, K, HEADS])
                step(v.tensor_tensor(logit[:], rows[:, :, D:WIDE], terms[:, chunk(n), :], ALU.add))
                step(v.scalar_tensor_tensor(out=logit[:], in0=logit[:], scalar=0.2, in1=logit[:], op0=ALU.mult, op1=ALU.max))
                step(v.tensor_reduce(top[:], logit[:], AX.X, ALU.max))
                step(v.tensor_tensor(logit[:], logit[:], over(top), ALU.subtract))
                dve.sem_inc(logits_shifted, 1)
                dve.wait_ge(exps_made, n + 1)
                step(v.tensor_reduce(top[:], logit[:], AX.X, ALU.add))
                step(v.reciprocal(top[:], top[:]))
                step(v.tensor_tensor(logit[:], logit[:], over(top), ALU.mult))
                step(v.tensor_tensor(scanned[s][:].rearrange("p k (h e) -> p k h e", h=HEADS),
                                     rows[:, :, 0:D].rearrange("p k (h e) -> p k h e", h=HEADS),
                                     logit[:].unsqueeze(3).broadcast_to([P, K, HEADS, HEAD_D]), ALU.mult))

            def count_dst(m, s):
                dve.wait_ge(count_hot_used, m + 1 + CHUNKS)
                one_hot(dhi_hot[s], P, dst_hi, m)
                one_hot(dlo_hot[s], TILES, dst_lo, m).then_inc(count_hot_made, 1)

            def scan_edges(pass_no, order, op, gate, message=None, beside=None):
                reset, neutral = (ALU.mult, 0.0) if op == ALU.add else (ALU.min, -BIG)
                step.begin(v.memset(state[:], neutral))
                with dve.Fori(0, LOOPS) as i:
                    step.enter(i, RING * (K + 1 + (8 if message else 0)))
                    for s in range(RING):
                        m = i * RING + s
                        n = m + pass_no * CHUNKS
                        step.wait()
                        dve.wait_ge(rows_gathered[s], (i + 1) * (16 * K) + pass_no * (16 * K * LOOPS))
                        dve.wait_ge(scan_slot_free, n + 1)
                        if message:
                            message(m, s, None)
                        rows = scanned[s][:] if message else \
                            gathered[s][:].rearrange("p k w -> p (k w)")[:, 0:K * D].rearrange("p (k d) -> p k d", d=D)
                        for k in range(K):
                            before = scanned[s][:, k - 1, :] if k else state[:]
                            step(v.scalar_tensor_tensor(out=scanned[s][:, k, :], in0=before,
                                                        scalar=gate[:, bass.ds(m * K + k, 1)], in1=rows[:, k, :],
                                                        op0=reset, op1=op))
                        dve.sem_inc(chunk_scanned, 1)
                        dve.sem_inc(rows_free, 1)
                        if beside:
                            beside(m, s)
                        step.begin(v.tensor_copy(state[:], scanned[s][:, K - 1, :]))
                    step.leave(LOOPS)
                step.wait()
                dve.sem_inc(state_ready, 1)
                dve.wait_ge(state_T_made, pass_no + 1)
                across = unbroken[order] if op == ALU.add else unbroken_limit
                step(v.tensor_tensor_scan(joined_T[:, 1:], across[:], state_T_ps, neutral, reset, op))
                dve.sem_inc(joined_T_made, 1)
                dve.wait_ge(joined_made, pass_no + 1)
                dve.wait_ge(fix_read, (pass_no + 1) * 16)
                step(v.tensor_tensor(fix_rows[:], fix_rows[:], joined_ps, op))
                dve.sem_inc(fix_made, 1)

            def nodes(pass_no):
                for g, (a, m) in enumerate(TILE_GROUPS):
                    dve.wait_ge(nodes_read[g], 16 * m * (pass_no + 1))

            scan_edges(P_SAGE, 0, ALU.add, cont[0], beside=count_dst)
            nodes(P_SAGE)
            step(v.tensor_scalar(tmp_t[:], degree[0][:], 1.0, None, ALU.max))
            step(v.reciprocal(tmp_t[:], tmp_t[:]))
            step(v.tensor_tensor(R[:], R[:], tiles(tmp_t), ALU.mult))
            dve.sem_inc(product_input, 1)
            drained(read_product(J_R, lambda a, m: U[:, a:a + m, :]))
            product_done(J_R)
            step(v.tensor_scalar(U[:], U[:], 0.0, None, ALU.max))
            step(v.tensor_tensor(V[:], U[:], U[:], ALU.mult))
            step(v.tensor_reduce(stat[:], V[:], AX.X, ALU.add))
            dve.sem_inc(squares_summed, 1)
            dve.wait_ge(roots_made, 2)
            step(v.tensor_scalar(stat[:], stat2[:], 1e-6, None, ALU.add))
            step(v.reciprocal(stat[:], stat[:]))
            step(v.tensor_tensor(U[:], U[:], tiles(stat), ALU.mult))
            step(v.tensor_tensor(X[:], X[:], U[:], ALU.add))
            normalise(3)
            dve.sem_inc(product_input, 1)
            drained(read_product(J_WH, None))
            product_done(J_WH)
            for term, a0 in ((dst_term, HEAD_D), (src_term, 0)):
                for h in range(HEADS):
                    step(v.tensor_tensor(V[:, :, h * HEAD_D:(h + 1) * HEAD_D], U[:, :, h * HEAD_D:(h + 1) * HEAD_D],
                                         att_w[:, h, a0:a0 + HEAD_D].unsqueeze(1).broadcast_to([P, TILES, HEAD_D]),
                                         ALU.mult))
                step(v.tensor_reduce(term[:], V[:].rearrange("p t (h e) -> p t h e", h=HEADS), AX.X, ALU.add))
            dve.sem_inc(src_terms_ready, 1)
            bounds(1)
            step(v.tensor_copy(key[:], dst_f[:]))
            step(v.tensor_copy(tmp_1[:], key_before_i[:]))
            runs(1, tmp_1[:])
            dve.sem_inc(key0_made, 1)
            step(v.tensor_scalar(limit[:], cont[1][:], -0.5, None, ALU.add))
            step(v.tensor_scalar(limit[:], limit[:], BIG, 2.0, ALU.mult, ALU.mult))
            fixes(1)
            dve.wait_ge(first_terms_read, 16)
            for h in range(HEADS):
                step(v.tensor_tensor_scan(terms[:, :, h], cont[0][:], terms[:, :, h], 0.0, ALU.mult, ALU.add))
            step(v.tensor_tensor(terms[:], terms[:], sorted_sb[:, :, 2:PAYLOAD], ALU.add))
            scan_edges(P_ATT, 0, ALU.add, cont[0], attention)
            nodes(P_ATT)
            step(v.tensor_scalar(V[:], R[:], 0.0, None, ALU.min))
            dve.sem_inc(elu_input, 1)
            dve.wait_ge(elu_exp, 1)
            step(v.tensor_scalar(V[:], V[:], -1.0, None, ALU.add))
            step(v.scalar_tensor_tensor(out=R[:], in0=R[:], scalar=0.0, in1=V[:], op0=ALU.max, op1=ALU.add))
            step(v.tensor_tensor(X[:], X[:], R[:], ALU.add))
            normalise(4)
            dve.sem_inc(product_input, 1)
            for g in read_product(J_CONV, bias(bias_2[:, 0, :])):
                dve.wait_ge(product_read, J_CONV * NTG + g + 1)
                dve.sem_inc(table_ready, 1)
            with dve.Fori(0, ROUNDS - 1) as r:
                step.enter(r, 1 + CHUNKS * (K + 1) + 2)
                scan_edges(r + P_MAX, 1, ALU.max, limit)
                for g in read_product(r + J_CONV + 1,
                                      lambda a, m: bias_2[:, bass.ds(r + 1, 1), :].broadcast_to([P, m, D])):
                    dve.wait_ge(product_read, (r + J_CONV + 1) * NTG + g + 1)
                    dve.sem_inc(table_ready, 1)
                step.leave(ROUNDS - 1)
            scan_edges(P_MAX + ROUNDS - 1, 1, ALU.max, limit)
            nodes(P_MAX + ROUNDS - 1)
            step(v.tensor_tensor(X[:], X[:], R[:], ALU.add))
            normalise(5)
            dve.sem_inc(table_ready, NTG)
            scan_edges(P_GCN_S, 0, ALU.add, cont[0])
            nodes(P_GCN_S)
            step(v.tensor_copy(V[:], R[:]))
            scan_edges(P_GCN_D, 1, ALU.add, cont[1])
            nodes(P_GCN_D)
            step(v.tensor_tensor(R[:], R[:], V[:], ALU.add))
            step(v.tensor_tensor(stat[:], degree[0][:], degree[1][:], ALU.add))
            step(v.tensor_scalar(stat[:], stat[:], 1.0, None, ALU.max))
            dve.sem_inc(squares_summed, 1)
            dve.wait_ge(roots_made, 6)
            step(v.reciprocal(stat[:], stat2[:]))
            step(v.tensor_tensor(R[:], R[:], tiles(stat), ALU.mult))
            dve.sem_inc(product_input, 1)
            drained(read_product(J_GCN, bias(bias_3[:])))
            product_done(J_GCN)
            step(v.tensor_tensor(U[:], U[:], H[:], ALU.add))
            dve.sem_inc(gelu_input, 1)
            dve.wait_ge(gelu_made, 1)
            step(v.tensor_tensor(X[:], X[:], U[:], ALU.add))
            dve.sem_inc(out_ready, 1)


INPUTS = ["x", "src", "dst", "edge_attr_16", "L0_gnn_Wl", "L0_gnn_Wr", "L1_gnn_W", "L2_gnn_Ws", "L3_gnn_W",
          "L0_gnn_bl", "L0_gnn_br", "L2_gnn_bs", "L3_gnn_b", "L1_gnn_a"]


def kernel(**inputs):
    import numpy as np
    import concourse.bacc as bacc
    from concourse.bass_utils import run_bass_kernel_spmd

    a = {name: np.asarray(inputs[name]) for name in INPUTS}

    def padded(values, rows, fill):
        more = np.full((rows - values.shape[0],) + values.shape[1:], fill, values.dtype)
        return np.concatenate([values, more])

    a["x"] = padded(a["x"], PAD_NODES, 0)
    a["src"] = padded(a["src"], PAD_EDGES, PAD_NODES - 1)
    a["dst"] = padded(a["dst"], PAD_EDGES, PAD_NODES - 1)
    a["edge_attr_16"] = padded(a["edge_attr_16"], PAD_EDGES, 0)
    a["L2_gnn_Ws"] = a["L2_gnn_Ws"].transpose(0, 2, 1)
    a["L3_gnn_W"] = a["L3_gnn_W"].T
    for name in ("L0_gnn_bl", "L0_gnn_br", "L2_gnn_bs", "L3_gnn_b", "L1_gnn_a"):
        a[name] = a[name].reshape(1, -1)

    nc = bacc.Bacc("TRN2", target_bir_lowering=False, num_devices=1)
    arrays, args = {}, []
    for name in INPUTS:
        arrays[f"in_{name}"] = np.ascontiguousarray(a[name])
        args.append(nc.dram_tensor(f"in_{name}", a[name].shape, mybir.dt.from_np(a[name].dtype),
                                   kind="ExternalInput").ap())
    out = nc.dram_tensor("out_0", (PAD_NODES, D), F32, kind="ExternalOutput").ap()
    build(nc, *args, out)
    r = run_bass_kernel_spmd(nc, [arrays], core_ids=[0])
    return r.results[0]["out_0"][:NODES]
```

```python
import concourse.bass as bass
from concourse import mybir
from concourse.alu_op_type import AluOpType as ALU
from contextlib import ExitStack
import numpy as np

F32 = mybir.dt.float32
F16 = mybir.dt.float16
BF16 = mybir.dt.bfloat16
I32 = mybir.dt.int32
I16 = mybir.dt.int16
ACT = mybir.ActivationFunctionType
AX = mybir.AxisListType

P = 128
NODES = 3125
EDGES = 100000
D = 128
TILES = -(-NODES // P)
PAD_NODES = P * TILES
STEPS = -(-EDGES // P)
PAD_EDGES = P * STEPS
HEADS, HEAD_D, EDGE_F = 4, 32, 16
ROUNDS = 5
RING = 2
K = 17
CHUNKS = STEPS // K
LOOPS = CHUNKS // RING
assert K * CHUNKS == STEPS and LOOPS * RING == CHUNKS
KP = 3
KG = K - KP
PARTS = 3
HOT_TILES = 5
HOT_GROUPS = TILES // HOT_TILES
assert HOT_TILES * HOT_GROUPS == TILES
FETCHED = CHUNKS * KP
BIG = 3.4028234e38
HALF = PAD_EDGES // 2
ZERO_ROW = PAD_EDGES
SPARE = PAD_EDGES + 1
SCAN_ROWS = SPARE + P
WIDE = D + HEADS
PAYLOAD = 2 + HEADS

GROUP = 4
STEP_GROUPS = [(a, min(GROUP, K - a)) for a in range(0, K, GROUP)]
NSG = len(STEP_GROUPS)
TILE_GROUPS = [(a, min(GROUP, TILES - a)) for a in range(0, TILES, GROUP)]
NTG = len(TILE_GROUPS)

P_SAGE, P_ATT, P_MAX, P_GCN_S, P_GCN_D = 0, 1, 2, 2 + ROUNDS, 3 + ROUNDS
J_L, J_R, J_WH, J_CONV, J_GCN = 0, 1, 2, 3, 3 + ROUNDS


class Steps:

    def __init__(self, eng, sem):
        self.eng, self.sem, self.n, self.at, self.outer = eng, sem, 0, None, []

    def __call__(self, ins):
        self.begin(ins)
        self.wait()

    def begin(self, ins):
        ins.then_inc(self.sem, 1)
        self.n += 1

    def wait(self):
        self.eng.wait_ge(self.sem, self.value())

    def value(self):
        return self.n if self.at is None else self.at + self.n

    def enter(self, turn, per):
        self.outer.append((self.n, self.at, per))
        self.at, self.n = turn * per + self.value(), 0

    def leave(self, turns):
        n, at, per = self.outer.pop()
        assert self.n == per, (self.n, per)
        self.n, self.at = n + per * turns, at


def build(nc, x, src, dst, edge_attr, Wl, Wr, W1, W2T, W3T, bl, br, b2, b3, att, out):
    es = ExitStack()
    with es:
        def sb(name, shape, dt=F32):
            return es.enter_context(nc.sbuf_tensor(name, shape, dt))

        def sem(name):
            return es.enter_context(nc.semaphore(name))

        table = nc.dram_tensor("table", (PAD_NODES, D), F32).ap()
        wide_table = nc.dram_tensor("wide_table", (PAD_NODES, WIDE), F32).ap()
        src_term_table = nc.dram_tensor("src_term_table", (PAD_NODES, HEADS), F32).ap()
        end_table = [nc.dram_tensor(f"end_table_{o}", (PAD_NODES, 1), F32).ap() for o in "sd"]
        payload_sorted = nc.dram_tensor("payload_sorted", (PAD_EDGES, PAYLOAD), F32).ap()
        src_term_at_start = nc.dram_tensor("src_term_at_start", (PAD_EDGES + PAD_NODES, HEADS), F32).ap()
        fetched_ids = [nc.dram_tensor(f"fetched_ids_{o}", (FETCHED, P), I16).ap() for o in "sd"]
        running = [nc.dram_tensor(f"running_{o}", (SCAN_ROWS, D), F32).ap() for o in "sd"]
        running_pk = [r[0:PAD_EDGES, :].rearrange("(p s) d -> p (s d)", s=STEPS) for r in running]

        X = sb("X", [P, TILES, D])
        H = sb("H", [P, TILES, D])
        R = sb("R", [P, TILES, D])
        U = sb("U", [P, TILES, D])
        V = sb("V", [P, TILES, D])
        src_i = sb("src_i", [P, STEPS], I32)
        dst_i = sb("dst_i", [P, STEPS], I32)
        ids = [dst_i, src_i]
        key = sb("key", [P, STEPS])
        dst_f = sb("dst_f", [P, STEPS])
        cont = [sb("cont_s", [P, STEPS]), sb("cont_d", [P, STEPS])]
        limit = sb("limit", [P, STEPS])
        sorted_sb = sb("sorted_sb", [P, STEPS, PAYLOAD])
        terms = sb("terms", [P, STEPS, HEADS])
        dst_hi, dst_lo = (terms[:].rearrange("p s h -> p (s h)")[:, h * STEPS:(h + 1) * STEPS] for h in range(2))

        def carver(tile):
            at = [0]

            def take(shape, dt=F32):
                words = -(-int(np.prod(shape)) * mybir.dt.size(dt) // 4)
                view = tile[:, at[0]:at[0] + words].bitcast(dt)[:, 0:int(np.prod(shape))]
                at[0] += words
                names = "abcd"[:len(shape)]
                return view.rearrange(f"p ({' '.join(names)}) -> p {' '.join(names)}",
                                      **dict(zip(names, shape))) if len(shape) > 1 else view
            return take

        region = sb("region", [P, 6200])
        take = carver(region[:])
        src_hi = take([STEPS + K])
        src_lo = take([STEPS + K])
        lo_hot = [take([K, TILES], F16) for s in range(RING)]
        place_tables = [take([TILES, K + 1]) for s in range(RING)]
        place_parts = [take([2, TILES, K + 1], F16) for s in range(RING)]
        not_first = take([TILES, K + 1])
        hi_hot_T = [take([GROUP, P], F16) for s in range(RING)]
        same_hi = [take([GROUP, P], F16) for s in range(RING)]
        attr = [take([K, EDGE_F]) for s in range(RING)]
        payload = [take([K, PAYLOAD]) for s in range(RING)]
        take = carver(region[:])
        parts = take([TILES, PARTS, WIDE], BF16)
        fetched = take([KP, PARTS * WIDE])
        in_v = V[:].rearrange("p t d -> p (t d)").bitcast(BF16)
        HOT_SIZE = HOT_TILES * KP * P
        node_hot = [sb(f"node_hot{g}", [P, HOT_TILES, KP * P], BF16)[:] for g in range(2)] \
            + [in_v[:, g * HOT_SIZE:(g + 1) * HOT_SIZE].rearrange("p (t e) -> p t e", t=HOT_TILES)
               for g in range(HOT_GROUPS - 2)]
        ids_row = [sb(f"ids_row{s}", [P, KP * P], I16) for s in range(RING)]
        id_columns = sb("id_columns", [P, FETCHED])
        id_rows = sb("id_rows", [P, P], I16)
        node_id = sb("node_id", [P, TILES])
        gathered = [sb(f"gathered{s}", [P, K, WIDE]) for s in range(RING)]
        scanned = [sb(f"scanned{s}", [P, K, D]) for s in range(RING)]
        index_ring = [sb(f"index_ring{s}", [P, K], I32) for s in range(RING)]
        hi_hot = [scanned[s][:].rearrange("p k d -> p (k d)").bitcast(F16)[:, 0:K * P]
                  .rearrange("p (k n) -> p k n", k=K) for s in range(RING)]
        in_r = R[:].rearrange("p t d -> p (t d)").bitcast(F16)
        dhi_hot = [in_r[:, s * K * P:(s + 1) * K * P].rearrange("p (k n) -> p k n", k=K) for s in range(RING)]
        dlo_hot = [in_r[:, RING * K * P + s * K * TILES:RING * K * P + (s + 1) * K * TILES]
                   .rearrange("p (k n) -> p k n", k=K) for s in range(RING)]
        hT = [sb(f"hT{s}", [P, GROUP, P]) for s in range(RING)]
        iota_i = sb("iota_i", [P, P], I32)
        row_i = sb("row_i", [P, 1], I32)
        iota = sb("iota", [P, P])
        row = sb("row", [P, 1])
        ident = sb("ident", [P, P])
        ident_b = sb("ident_b", [P, P], F16)
        later = sb("later", [P, P])
        ones = sb("ones", [P, P])
        zeros_b = sb("zeros_b", [P, P], F16)
        place_next = sb("place_next", [P, TILES])
        place_products = gathered[0][:].rearrange("p k w -> p (k w)")[:, 0:K * TILES]\
            .rearrange("p (k t) -> p k t", k=K)
        attr_products = gathered[1][:].rearrange("p k w -> p (k w)")[:, 0:K * HEADS * EDGE_F]\
            .rearrange("p (k h f) -> p k h f", k=K, h=HEADS)
        degree = [sb("degree_s", [P, TILES]), sb("degree_d", [P, TILES])]
        start = [sb("start_s", [P, TILES]), sb("start_d", [P, TILES])]
        end = [sb("end_s", [P, TILES]), sb("end_d", [P, TILES])]
        has_edges = [sb("has_edges_s", [P, TILES]), sb("has_edges_d", [P, TILES])]
        place_sums = sb("place_sums", [P, K])
        last_row = [sb("last_row_s", [P, TILES], I32), sb("last_row_d", [P, TILES], I32)]
        start_row = sb("start_row", [P, TILES], I32)
        spare_row = sb("spare_row", [P, TILES])
        tmp_t = sb("tmp_t", [P, TILES])
        tmp_u = sb("tmp_u", [P, TILES])
        key0_i = [sb("key0_s", [P, 1], I32), sb("key0_d", [P, 1], I32)]
        key_before_f = sb("key_before_f", [P, 1])
        key_before_i = sb("key_before_i", [P, 1], I32)
        end_of_first = [sb("end_of_first_s", [P, 1]), sb("end_of_first_d", [P, 1])]
        fix_row = [sb("fix_row_s", [P, 1], I32), sb("fix_row_d", [P, 1], I32)]
        unbroken = [sb("unbroken_s", [P, P]), sb("unbroken_d", [P, P])]
        unbroken_limit = sb("unbroken_limit", [P, P])
        tmp_1 = sb("tmp_1", [P, 1])
        tmp_2 = sb("tmp_2", [P, 1])
        tmp_3 = sb("tmp_3", [P, 1])
        diag = sb("diag", [P, P])
        state = sb("state", [P, D])
        joined_T = sb("joined_T", [P, P + 1])
        fix_rows = sb("fix_rows", [P, D])
        logit = sb("logit", [P, K, HEADS])
        top = sb("top", [P, K])
        stat = sb("stat", [P, TILES])
        stat2 = sb("stat2", [P, TILES])
        dst_term = sb("dst_term", [P, TILES, HEADS])
        src_term = sb("src_term", [P, TILES, HEADS])
        w_l, w_r, w_1, w_3 = (sb(n, [P, D]) for n in ("w_l", "w_r", "w_1", "w_3"))
        w_2 = sb("w_2", [P, ROUNDS, D])
        bias_l, bias_r, bias_3 = (sb(n, [P, D]) for n in ("bias_l", "bias_r", "bias_3"))
        bias_2 = sb("bias_2", [P, ROUNDS, D])
        att_w = sb("att_w", [P, HEADS, 2 * HEAD_D + EDGE_F])
        bank = [es.enter_context(nc.psum_tensor(f"bank{b}", [P, 512], F32)) for b in range(8)]

        delta_ps = bank[0][:, 0:TILES * (K + 1)].rearrange("p (t k) -> p t k", k=K + 1)
        place_ps = bank[1][:, 0:K * TILES].rearrange("p (k t) -> p k t", k=K)
        same_ps = [bank[3 + s][:, :].rearrange("p (j e) -> p j e", j=GROUP) for s in range(RING)]
        hot_T_ps = [bank[b][:, 0:256].bitcast(F16).rearrange("p (j e) -> p j e", j=GROUP) for b in (2, 5)]
        count_ps = [bank[6][:, 0:TILES], bank[0][:, 0:TILES]]
        offset_ps = bank[4][:, 0:1]
        hT_ps = [bank[s][:, :].rearrange("p (j n) -> p j n", j=GROUP) for s in range(RING)]
        prod_ps = [bank[2 + s][:, :].rearrange("p (j o) -> p j o", j=GROUP) for s in range(RING)]
        state_T_ps = bank[4][:, 0:P]
        joined_ps = bank[4][:, 0:P]
        unbroken_ps = bank[4][:, 0:P]
        id_rows_ps = bank[4][:, 0:P]
        fetched_ps = [[bank[b + j] for j in range(KP)] for b in (5, 1)]

        iota_made = sem("iota_made")
        edges_loaded = sem("edges_loaded")
        x_loaded = sem("x_loaded")
        weights_loaded = sem("weights_loaded")
        vec = sem("vec")
        constants_made = sem("constants_made")
        zeros_made = sem("zeros_made")
        zeros_stored = sem("zeros_stored")
        count_hot_made = sem("count_hot_made")
        count_hot_used = sem("count_hot_used")
        counted = sem("counted")
        totals_made = sem("totals_made")
        offsets_made = sem("offsets_made")
        hot_made = sem("hot_made")
        deltas_made = sem("deltas_made")
        tables_made = sem("tables_made")
        hot_T_made = sem("hot_T_made")
        hot_T_copied = sem("hot_T_copied")
        same_made = sem("same_made")
        same_masked = sem("same_masked")
        group_placed = sem("group_placed")
        places_read = sem("places_read")
        attr_loaded = [sem(f"attr_loaded{s}") for s in range(RING)]
        attr_used = sem("attr_used")
        payload_made = sem("payload_made")
        scattered = [sem(f"scattered{s}") for s in range(RING)]
        payload_free = sem("payload_free")
        scattering = sem("scattering")
        sorted_loaded = sem("sorted_loaded")
        ends_made = sem("ends_made")
        ends_stored = sem("ends_stored")
        key0_made = sem("key0_made")
        first_ends_read = sem("first_ends_read")
        diag_made = sem("diag_made")
        unbroken_read = sem("unbroken_read")
        rows_free = sem("rows_free")
        index_copied = sem("index_copied")
        gathering = sem("gathering")
        rows_gathered = [sem(f"rows_gathered{s}") for s in range(RING)]
        chunk_scanned = sem("chunk_scanned")
        running_stored = sem("running_stored")
        scan_slot_free = sem("scan_slot_free")
        logits_shifted = sem("logits_shifted")
        exps_made = sem("exps_made")
        state_ready = sem("state_ready")
        state_T_made = sem("state_T_made")
        joined_T_made = sem("joined_T_made")
        joined_made = sem("joined_made")
        fix_read = sem("fix_read")
        fix_made = sem("fix_made")
        fix_written = sem("fix_written")
        nodes_read = [sem(f"nodes_read{g}") for g in range(NTG)]
        product_input = sem("product_input")
        tiles_T_made = sem("tiles_T_made")
        tiles_T_copied = sem("tiles_T_copied")
        product_made = sem("product_made")
        product_read = sem("product_read")
        silu_made = sem("silu_made")
        squares_summed = sem("squares_summed")
        roots_made = sem("roots_made")
        table_ready = sem("table_ready")
        table_stored = sem("table_stored")
        wide_stored = sem("wide_stored")
        src_terms_ready = sem("src_terms_ready")
        src_terms_stored = sem("src_terms_stored")
        src_terms_scattered = sem("src_terms_scattered")
        src_terms_loaded = sem("src_terms_loaded")
        first_terms_read = sem("first_terms_read")
        id_columns_made = sem("id_columns_made")
        id_rows_T_made = sem("id_rows_T_made")
        id_rows_made = sem("id_rows_made")
        ids_stored = sem("ids_stored")
        parts_ready = sem("parts_ready")
        ids_loaded = [sem(f"ids_loaded{s}") for s in range(RING)]
        node_hot_made = sem("node_hot_made")
        node_hot_used = sem("node_hot_used")
        fetched_copied = sem("fetched_copied")
        fetched_summed = sem("fetched_summed")
        elu_input = sem("elu_input")
        elu_exp = sem("elu_exp")
        gelu_input = sem("gelu_input")
        gelu_made = sem("gelu_made")
        out_ready = sem("out_ready")
        out_stored = sem("out_stored")
        block = es.enter_context(nc.Block())

        by_node = lambda t: t.rearrange("(p t) d -> p t d", t=TILES)
        chunk = lambda n: bass.ds(n * K, K)
        ID_SPANS = [(a, min(P, FETCHED - a)) for a in range(0, FETCHED, P)]

        @block.sync
        def _(sp):
            per_edge = lambda a: a.rearrange("(p s) -> p s", s=STEPS)
            sp.dma_start(src_i[:], per_edge(src)).then_inc(edges_loaded, 16)
            sp.dma_start(dst_i[:], per_edge(dst)).then_inc(edges_loaded, 16)
            sp.wait_ge(zeros_made, 1)
            with nc.allow_non_contiguous_dma(reason="one word of each partition"):
                sp.dma_start(key_before_i[1:P, :], per_edge(dst)[0:P - 1, STEPS - 1:STEPS]).then_inc(edges_loaded, 16)
            sp.dma_start(X[:], by_node(x)).then_inc(x_loaded, 16)
            for tile, a in ((w_l[:], Wl), (w_r[:], Wr), (w_1[:], W1), (w_3[:], W3T),
                            (w_2[:], W2T.rearrange("r i o -> i r o")),
                            (bias_l[:], bl.broadcast_to([P, D])), (bias_r[:], br.broadcast_to([P, D])),
                            (bias_3[:], b3.broadcast_to([P, D])),
                            (bias_2[:].rearrange("p r d -> p (r d)"), b2.broadcast_to([P, ROUNDS * D])),
                            (att_w[:].rearrange("p h a -> p (h a)"),
                             att.broadcast_to([P, HEADS * (2 * HEAD_D + EDGE_F)]))):
                sp.dma_start(tile, a).then_inc(weights_loaded, 16)
            sp.dma_start(src_term_at_start[0:PAD_EDGES, :].rearrange("(p s) h -> p (s h)", s=STEPS),
                         terms[:].rearrange("p s h -> p (s h)")).then_inc(zeros_stored, 16)
            for r in running:
                sp.dma_start(r[ZERO_ROW:ZERO_ROW + 1, :], terms[0:1, 0:D // HEADS, :].rearrange("p s h -> p (s h)"))\
                    .then_inc(zeros_stored, 16)
                sp.dma_start(r[SPARE:SCAN_ROWS, :], terms[:, 0:D // HEADS, :].rearrange("p s h -> p (s h)"))\
                    .then_inc(zeros_stored, 16)

            sp.sem_inc(payload_free, RING)
            with sp.Fori(0, LOOPS) as i:
                for s in range(RING):
                    sp.wait_ge(scattered[s], (i + 1) * (16 * K))
                    sp.sem_inc(payload_free, 1)
            sorted_pk = payload_sorted.rearrange("(p s) c -> p s c", s=STEPS)
            sp.dma_start(sorted_sb[:], sorted_pk).then_inc(sorted_loaded, 16)
            with nc.allow_non_contiguous_dma(reason="one word of each partition"):
                sp.dma_start(key_before_f[1:P, :], sorted_pk[0:P - 1, STEPS - 1, 1:2]).then_inc(sorted_loaded, 16)

            def store_ids(order):
                for c, (a, m) in enumerate(ID_SPANS):
                    sp.wait_ge(id_rows_made, order * len(ID_SPANS) + c + 1)
                    sp.dma_start(fetched_ids[order][a:a + m, :], id_rows[0:m, :]).then_inc(ids_stored, 16)

            def store_ends(order):
                sp.wait_ge(ends_made, order + 1)
                with nc.allow_non_contiguous_dma(reason="a word of each node"):
                    sp.dma_start(by_node(end_table[order]), end[order][:].unsqueeze(2)).then_inc(ends_stored, 16)

            store_ends(0)

            def store_table(groups_before, rows):
                for g, (a, m) in enumerate(TILE_GROUPS):
                    sp.wait_ge(table_ready, groups_before + g + 1)
                    sp.dma_start(by_node(table)[:, a:a + m, :], rows[:, a:a + m, :]).then_inc(table_stored, 16)

            def store_running(pass_no, order):
                with sp.Fori(0, LOOPS) as i:
                    for s in range(RING):
                        n = i * RING + s + pass_no * CHUNKS
                        sp.wait_ge(chunk_scanned, n + 1)
                        sp.dma_start(running_pk[order][:, bass.ds((i * RING + s) * (K * D), K * D)],
                                     scanned[s][:].rearrange("p k d -> p (k d)")).then_inc(running_stored, 16)
                        sp.wait_ge(running_stored, (n + 1) * 16)
                        sp.sem_inc(scan_slot_free, 1)

            sp.sem_inc(scan_slot_free, RING)
            store_ids(0)
            store_table(0, H)
            store_running(P_SAGE, 0)
            sp.wait_ge(src_terms_ready, 1)
            with nc.allow_non_contiguous_dma(reason="four words of each node"):
                sp.dma_start(by_node(src_term_table), src_term[:]).then_inc(src_terms_stored, 16)
                sp.dma_start(by_node(wide_table)[:, :, 0:D], U[:]).then_inc(wide_stored, 16)
                sp.dma_start(by_node(wide_table)[:, :, D:WIDE], dst_term[:]).then_inc(wide_stored, 16)
            store_ends(1)
            store_ids(1)
            sp.wait_ge(src_terms_scattered, 16 * TILES)
            sp.dma_start(terms[:].rearrange("p s h -> p (s h)"),
                         src_term_at_start[0:PAD_EDGES, :].rearrange("(p s) h -> p (s h)", s=STEPS))\
                .then_inc(src_terms_loaded, 16)
            store_running(P_ATT, 0)
            store_table(NTG, U)
            with sp.Fori(0, ROUNDS - 1) as r:
                store_running(r + P_MAX, 1)
                store_table((r + 2) * NTG, U)
            store_running(P_MAX + ROUNDS - 1, 1)
            store_table((ROUNDS + 1) * NTG, H)
            store_running(P_GCN_S, 0)
            store_running(P_GCN_D, 1)
            sp.wait_ge(out_ready, 1)
            sp.dma_start(by_node(out), X[:]).then_inc(out_stored, 16)
            sp.wait_ge(out_stored, 16)
            sp.wait_ge(zeros_stored, 16 * 5)
            sp.wait_ge(table_stored, 16 * NTG * (ROUNDS + 2))

        @block.gpsimd
        def _(pool):
            pool.iota(iota_i[:], pattern=[[1, P]], base=0, channel_multiplier=0).then_inc(iota_made, 1)
            pool.iota(row_i[:], pattern=[[0, 1]], base=0, channel_multiplier=1).then_inc(iota_made, 1)

            def gather(out_, table_, index, done):
                pool.indirect_dma_start(out=out_, out_offset=None, in_=table_,
                                        in_offset=bass.IndirectOffsetOnAxis(ap=index, axis=0)).then_inc(done, 16)

            def scatter(table_, index, rows, done):
                pool.indirect_dma_start(out=table_, out_offset=bass.IndirectOffsetOnAxis(ap=index, axis=0),
                                        in_=rows, in_offset=None).then_inc(done, 16)

            with pool.Fori(0, LOOPS) as i:
                for s in range(RING):
                    n = i * RING + s
                    pool.wait_ge(payload_made, n + 1)
                    pool.sem_inc(scattering, 1)
                    for k in range(K):
                        scatter(payload_sorted, index_ring[s][:, k:k + 1], payload[s][:, k, :], scattered[s])

            def read_first_ends(order):
                pool.wait_ge(ends_stored, 16 * (order + 1))
                pool.wait_ge(key0_made, order + 1)
                gather(end_of_first[order][:], end_table[order], key0_i[order][:], first_ends_read)

            def gather_edges(pass_no, order, table_, width):
                with pool.Fori(0, LOOPS) as i:
                    for s in range(RING):
                        n = i * RING + s + pass_no * CHUNKS
                        pool.wait_ge(rows_free, n + 1)
                        pool.tensor_copy(index_ring[s][:], ids[order][:, chunk(i * RING + s)]).then_inc(index_copied, 1)
                        pool.wait_ge(index_copied, n + 1)
                        pool.sem_inc(gathering, 1)
                        for k in range(KG):
                            gather(gathered[s][:, k, 0:width], table_, index_ring[s][:, k:k + 1], rows_gathered[s])

            def read_nodes(pass_no, order):
                pool.wait_ge(scan_slot_free, (pass_no + 1) * CHUNKS + RING)
                pool.sem_inc(gathering, 1)
                gather(fix_rows[:], running[order], fix_row[order][:], fix_read)
                pool.wait_ge(fix_made, pass_no + 1)
                pool.sem_inc(gathering, 1)
                scatter(running[order], fix_row[order][:], fix_rows[:], fix_written)
                pool.wait_ge(fix_written, (pass_no + 1) * 16)
                pool.sem_inc(gathering, 1)
                for g, (a, m) in enumerate(TILE_GROUPS):
                    for t in range(a, a + m):
                        gather(R[:, t, :], running[order], last_row[order][:, t:t + 1], nodes_read[g])

            pool.wait_ge(zeros_stored, 16 * 5)
            read_first_ends(0)
            pool.wait_ge(table_stored, 16 * NTG)
            gather_edges(P_SAGE, 0, table, D)
            read_nodes(P_SAGE, 0)
            pool.wait_ge(src_terms_ready, 1)
            for t in range(TILES):
                scatter(src_term_at_start, start_row[:, t:t + 1], src_term[:, t, :], src_terms_scattered)
            pool.wait_ge(src_terms_stored, 16)
            pool.wait_ge(src_terms_loaded, 16)
            gather(terms[:, 0, :], src_term_table, key0_i[0][:], first_terms_read)
            read_first_ends(1)
            pool.wait_ge(wide_stored, 32)
            gather_edges(P_ATT, 0, wide_table, WIDE)
            read_nodes(P_ATT, 0)
            pool.wait_ge(table_stored, 16 * NTG * 2)
            with pool.Fori(0, ROUNDS - 1) as r:
                gather_edges(r + P_MAX, 1, table, D)
                read_nodes(r + P_MAX, 1)
                pool.wait_ge(table_stored, r * (16 * NTG) + 16 * NTG * 3)
            gather_edges(P_MAX + ROUNDS - 1, 1, table, D)
            read_nodes(P_MAX + ROUNDS - 1, 1)
            pool.wait_ge(table_stored, 16 * NTG * (ROUNDS + 2))
            gather_edges(P_GCN_S, 0, table, D)
            read_nodes(P_GCN_S, 0)
            gather_edges(P_GCN_D, 1, table, D)
            read_nodes(P_GCN_D, 1)

        @block.tensor
        def _(pe):
            def count_begin(order):
                nc.tensor.matmul(count_ps[order], zeros_b[:], zeros_b[:, 0:TILES], start=True, stop=False)

            def count_chunk(order, m, s, his, los):
                pe.wait_ge(count_hot_made, m + 1 + order * CHUNKS)
                for k in range(K):
                    last = nc.tensor.matmul(count_ps[order], his[s][:, k, :], los[s][:, k, :], start=False, stop=False)
                last.then_inc(count_hot_used, 1)

            def count_end(order):
                nc.tensor.matmul(count_ps[order], zeros_b[:], zeros_b[:, 0:TILES], start=False, stop=True)\
                    .then_inc(counted, 1)

            pe.wait_ge(constants_made, 1)
            pe.sem_inc(count_hot_used, RING)
            count_begin(0)
            with pe.Fori(0, LOOPS) as i:
                for s in range(RING):
                    count_chunk(0, i * RING + s, s, hi_hot, lo_hot)
            count_end(0)

            def offsets(n):
                pe.wait_ge(totals_made, n)
                nc.tensor.matmul(offset_ps, later[:], tmp_1[:], start=True, stop=True).then_inc(offsets_made, 1)

            offsets(1)
            pe.sem_inc(group_placed, RING)
            with pe.Fori(0, LOOPS) as i:
                for s in range(RING):
                    n = i * RING + s
                    pe.wait_ge(hot_made, n + 1)
                    pe.wait_ge(tables_made, n + 1)
                    for k in range(K):
                        last = nc.tensor.matmul(delta_ps[:, :, k + 1], hi_hot[s][:, k, :], lo_hot[s][:, k, :],
                                                start=True, stop=True)
                    last.then_inc(deltas_made, 1)
                    for g in range(NSG + 2):
                        if g < NSG:
                            a, m = STEP_GROUPS[g]
                            c, r = n * NSG + g, (s * NSG + g) % RING
                            pe.wait_ge(hot_T_copied, c + 1)
                            for j in range(m):
                                last = nc.tensor.transpose(hot_T_ps[r][:, j, :], hi_hot[s][:, a + j, :], ident_b[:])
                            last.then_inc(hot_T_made, 1)
                        if 1 <= g <= NSG:
                            a, m = STEP_GROUPS[g - 1]
                            c, r = n * NSG + g - 1, (s * NSG + g - 1) % RING
                            pe.wait_ge(hot_T_copied, c + 1 + RING)
                            pe.wait_ge(same_masked, c + 1)
                            for j in range(m):
                                last = nc.tensor.matmul(same_ps[r][:, j, :], hi_hot_T[r][:, j, :], hi_hot_T[r][:, j, :],
                                                        start=True, stop=True)
                            last.then_inc(same_made, 1)
                        if g >= 2:
                            a, m = STEP_GROUPS[g - 2]
                            c, r = n * NSG + g - 2, (s * NSG + g - 2) % RING
                            if g == 2:
                                pe.wait_ge(tables_made, n + 2)
                                pe.wait_ge(places_read, n + 1)
                            pe.wait_ge(same_masked, c + 1 + RING)
                            for j in range(m):
                                for part in range(2):
                                    nc.tensor.matmul(place_ps[:, a + j, :], hi_hot_T[r][:, j, :],
                                                     place_parts[s][:, part, :, a + j], start=part == 0, stop=False)
                                last = nc.tensor.matmul(place_ps[:, a + j, :], same_hi[r][:, j, :],
                                                        lo_hot[s][:, a + j, :], start=False, stop=True)
                            last.then_inc(group_placed, 1)

            def spread_unbroken(order):
                pe.wait_ge(diag_made, order + 1)
                nc.tensor.matmul(unbroken_ps, ones[:], diag[:], start=True, stop=True).then_inc(unbroken_read, 1)

            def transpose_ids(order):
                for c, (a, m) in enumerate(ID_SPANS):
                    pe.wait_ge(id_columns_made, order * len(ID_SPANS) + c + 1)
                    nc.tensor.transpose(id_rows_ps[0:m, :], id_columns[:, a:a + m], ident[:]).then_inc(id_rows_T_made, 1)

            def fetch(pass_no, width, beside=None):
                def body(i, s):
                    n = i * RING + s + pass_no * CHUNKS
                    pe.wait_ge(fetched_copied, n + 1)
                    for g in range(HOT_GROUPS):
                        pe.wait_ge(node_hot_made, n * HOT_GROUPS + g + 1)
                        for b in range(HOT_TILES):
                            t = g * HOT_TILES + b
                            for j in range(KP):
                                last = nc.tensor.matmul(fetched_ps[s][j][:, 0:PARTS * width],
                                                        node_hot[g][:, b, j * P:(j + 1) * P], parts[:, t, :, 0:width],
                                                        start=t == 0, stop=t == TILES - 1)
                        last.then_inc(node_hot_used, 1)

                if beside:
                    pe.wait_ge(parts_ready, pass_no + 1)
                    for s in range(RING):
                        body(0, s)
                    with pe.Fori(0, LOOPS - 1) as i:
                        for s in range(RING):
                            beside(i * RING + s, s)
                            body(i + 1, s)
                    for s in range(RING):
                        beside((LOOPS - 1) * RING + s, s)
                    return
                with pe.Fori(0, LOOPS) as i:
                    pe.wait_ge(parts_ready, pass_no + 1)
                    for s in range(RING):
                        body(i, s)

            pe.sem_inc(node_hot_used, HOT_GROUPS)
            transpose_ids(0)
            spread_unbroken(0)

            def product(job, tiles, weight, ready):
                def transposes(g):
                    a, m = TILE_GROUPS[g]
                    ready(g)
                    if not (isinstance(job, int) and job == 0 and g < RING):
                        pe.wait_ge(tiles_T_copied, job * NTG + max(g - RING + 1, 0))
                    for j in range(m):
                        last = nc.tensor.transpose(hT_ps[g % RING][:, j, :], tiles[:, a + j, :], ident[:])
                    last.then_inc(tiles_T_made, 1)

                def products(g):
                    a, m = TILE_GROUPS[g]
                    pe.wait_ge(tiles_T_copied, job * NTG + g + 1)
                    if not (isinstance(job, int) and job == 0 and g < RING):
                        pe.wait_ge(product_read, job * NTG + max(g - RING + 1, 0))
                    for j in range(m):
                        last = nc.tensor.matmul(prod_ps[g % RING][:, j, :], hT[g % RING][:, j, :], weight,
                                                start=True, stop=True)
                    last.then_inc(product_made, 1)

                for g in range(NTG + 1):
                    if g < NTG:
                        transposes(g)
                    if g >= 1:
                        products(g - 1)

            def join(pass_no):
                pe.wait_ge(state_ready, pass_no + 1)
                nc.tensor.transpose(state_T_ps, state[:], ident[:]).then_inc(state_T_made, 1)
                pe.wait_ge(joined_T_made, pass_no + 1)
                nc.tensor.transpose(joined_ps, joined_T[:, 0:P], ident[:]).then_inc(joined_made, 1)

            inputs = lambda n: (lambda g: pe.wait_ge(product_input, n) if g == 0 else None)
            pe.wait_ge(weights_loaded, 160)
            product(J_L, H, w_l[:], inputs(1))
            count_begin(1)
            fetch(P_SAGE, D, lambda m, s: count_chunk(1, m, s, dhi_hot, dlo_hot))
            count_end(1)
            join(P_SAGE)
            product(J_R, R, w_r[:], inputs(2))
            product(J_WH, H, w_1[:], inputs(3))
            offsets(2)
            transpose_ids(1)
            spread_unbroken(1)
            fetch(P_ATT, WIDE)
            join(P_ATT)
            product(J_CONV, H, w_2[:, 0, :], inputs(4))
            with pe.Fori(0, ROUNDS - 1) as r:
                fetch(r + P_MAX, D)
                join(r + P_MAX)
                product(r + J_CONV + 1, R, w_2[:, bass.ds(r + 1, 1), :].rearrange("p a o -> p (a o)"),
                        lambda g: pe.wait_ge(silu_made, r * NTG + g + 1))
            for pass_no in (P_MAX + ROUNDS - 1, P_GCN_S, P_GCN_D):
                fetch(pass_no, D)
                join(pass_no)
            product(J_GCN, R, w_3[:], inputs(5))

        @block.scalar
        def _(act):
            act.wait_ge(constants_made, 1)
            act.sem_inc(hot_T_copied, RING)
            with act.Fori(0, LOOPS) as i:
                for s in range(RING):
                    n = i * RING + s
                    act.wait_ge(attr_used, n + 1)
                    act.dma_start(attr[s][:].rearrange("p k f -> p (k f)"),
                                  edge_attr.rearrange("(p s) f -> p (s f)", s=STEPS)[:, bass.ds(n * (K * EDGE_F), K * EDGE_F)])\
                        .then_inc(attr_loaded[s], 16)
                    for g, (a, m) in enumerate(STEP_GROUPS):
                        c, r = n * NSG + g, (s * NSG + g) % RING
                        act.wait_ge(hot_T_made, c + 1)
                        act.wait_ge(group_placed, c + 1)
                        nc.scalar.activation(hi_hot_T[r][:, 0:m, :], hot_T_ps[r][:, 0:m, :], ACT.Copy)\
                            .then_inc(hot_T_copied, 1)

            def transposed(job, g):
                a, m = TILE_GROUPS[g]
                act.wait_ge(tiles_T_made, job * NTG + g + 1)
                if not (isinstance(job, int) and job == 0 and g < RING):
                    act.wait_ge(product_made, job * NTG + max(g - RING + 1, 0))
                nc.scalar.activation(hT[g % RING][:, 0:m, :], hT_ps[g % RING][:, 0:m, :], ACT.Copy)\
                    .then_inc(tiles_T_copied, 1)

            def product(job):
                for g in range(NTG):
                    transposed(job, g)

            def root(n):
                act.wait_ge(squares_summed, n)
                nc.scalar.activation(stat2[:], stat[:], ACT.Sqrt).then_inc(roots_made, 1)

            def load_ids(pass_no, order, m, s):
                act.dma_start(ids_row[s][:], fetched_ids[order].rearrange("(a c) p -> a (c p)", a=1)
                              [:, bass.ds(m * (KP * P), KP * P)].broadcast_to([P, KP * P])).then_inc(ids_loaded[s], 16)

            def copy_fetched(pass_no, order, width, attend=False):
                act.wait_ge(ids_stored, 16 * len(ID_SPANS) * (order + 1))
                for s in range(RING):
                    load_ids(pass_no, order, s, s)

                def body(i, s, ahead):
                    m = i * RING + s
                    n = m + pass_no * CHUNKS
                    act.wait_ge(node_hot_used, n * HOT_GROUPS + 2 * HOT_GROUPS)
                    act.wait_ge(fetched_summed, n + 1)
                    for j in range(KP):
                        last = nc.scalar.activation(fetched[:, j, 0:PARTS * width], fetched_ps[s][j][:, 0:PARTS * width],
                                                    ACT.Copy)
                    last.then_inc(fetched_copied, 1)
                    if ahead:
                        load_ids(pass_no, order, m + RING, s)
                    if attend:
                        act.wait_ge(logits_shifted, m + 1)
                        nc.scalar.activation(logit[:], logit[:], ACT.Exp).then_inc(exps_made, 1)

                with act.Fori(0, LOOPS - 1) as i:
                    for s in range(RING):
                        body(i, s, True)
                for s in range(RING):
                    body(LOOPS - 1, s, False)

            act.sem_inc(fetched_copied, RING)
            root(1)
            product(J_L)
            copy_fetched(P_SAGE, 0, D)
            product(J_R)
            root(2)
            root(3)
            product(J_WH)
            copy_fetched(P_ATT, 0, WIDE, attend=True)
            act.wait_ge(elu_input, 1)
            nc.scalar.activation(V[:], V[:], ACT.Exp).then_inc(elu_exp, 1)
            root(4)
            product(J_CONV)
            with act.Fori(0, ROUNDS - 1) as r:
                copy_fetched(r + P_MAX, 1, D)
                for g in range(NTG + 1):
                    if g < NTG:
                        a, m = TILE_GROUPS[g]
                        act.wait_ge(nodes_read[g], r * (16 * m) + 16 * m * (P_MAX + 1))
                        nc.scalar.activation(R[:, a:a + m, :], R[:, a:a + m, :], ACT.Silu).then_inc(silu_made, 1)
                    if g >= 1:
                        transposed(r + J_CONV + 1, g - 1)
            copy_fetched(P_MAX + ROUNDS - 1, 1, D)
            root(5)
            copy_fetched(P_GCN_S, 0, D)
            copy_fetched(P_GCN_D, 1, D)
            root(6)
            product(J_GCN)
            act.wait_ge(gelu_input, 1)
            nc.scalar.activation(U[:], U[:], ACT.Gelu).then_inc(gelu_made, 1)

        @block.vector
        def _(dve):
            v = nc.vector
            step = Steps(dve, vec)
            tiles = lambda a: a[:].unsqueeze(2).broadcast_to([P, TILES, D])

            step(v.memset(terms[:], 0.0))
            step(v.memset(key_before_i[:], -1))
            dve.sem_inc(zeros_made, 1)
            step(v.memset(key_before_f[:], -1.0))
            step(v.memset(ones[:], 1.0))
            step(v.memset(zeros_b[:], 0.0))
            step(v.memset(joined_T[:], 0.0))
            for a in (src_hi, src_lo):
                step(v.memset(a[:, STEPS:], 0.0))
            step(v.memset(not_first[:], 1.0))
            step(v.memset(not_first[:, :, 0], 0.0))
            dve.wait_ge(iota_made, 2)
            step(v.tensor_copy(iota[:], iota_i[:]))
            step(v.tensor_copy(row[:], row_i[:]))
            step(v.tensor_scalar(ident[:], iota[:], row[:], None, ALU.is_equal))
            step(v.tensor_scalar(ident_b[:], iota[:], row[:], None, ALU.is_equal))
            step(v.tensor_scalar(later[:], iota[:], row[:], None, ALU.is_gt))
            dve.sem_inc(constants_made, 1)
            dve.wait_ge(edges_loaded, 48)

            def split(ids_i, ids_f, hi, lo):
                step(v.tensor_copy(ids_f[:], ids_i[:]))
                step(v.tensor_scalar(sorted_sb[:, :, 0].bitcast(I32), ids_f[:], 1.0 / TILES, -0.48, ALU.mult, ALU.add))
                step(v.tensor_copy(hi[:, 0:STEPS], sorted_sb[:, :, 0].bitcast(I32)))
                step(v.scalar_tensor_tensor(out=lo[:, 0:STEPS], in0=hi[:, 0:STEPS], scalar=-float(TILES), in1=ids_f[:],
                                            op0=ALU.mult, op1=ALU.add))

            split(src_i, key, src_hi, src_lo)

            def one_hot(hot, width, value, n):
                return v.tensor_tensor(hot, iota[:, 0:width].unsqueeze(1).broadcast_to([P, K, width]),
                                       value[:, chunk(n)].unsqueeze(2).broadcast_to([P, K, width]), ALU.is_equal)

            with dve.Fori(0, LOOPS) as i:
                for s in range(RING):
                    n = i * RING + s
                    dve.wait_ge(count_hot_used, n + 1)
                    one_hot(hi_hot[s], P, src_hi, n)
                    one_hot(lo_hot[s], TILES, src_lo, n).then_inc(count_hot_made, 1)
            dve.wait_ge(zeros_stored, 16 * 5)
            split(dst_i, dst_f, dst_hi, dst_lo)

            def bounds(order):
                step(v.tensor_tensor_scan(end[order][:], ones[:, 0:TILES], degree[order][:], 0.0, ALU.mult, ALU.add))
                step(v.tensor_copy(tmp_1[:], end[order][:, TILES - 1:TILES]))
                dve.sem_inc(totals_made, 1)
                dve.wait_ge(offsets_made, order + 1)
                step(v.tensor_copy(tmp_2[:], offset_ps))
                step(v.tensor_scalar(end[order][:], end[order][:], tmp_2[:], None, ALU.add))
                step(v.tensor_tensor(start[order][:], end[order][:], degree[order][:], ALU.subtract))
                step(v.tensor_scalar(has_edges[order][:], degree[order][:], 0.0, None, ALU.is_gt))
                step(v.tensor_scalar(tmp_t[:], end[order][:], -1.0 - ZERO_ROW, None, ALU.add))
                step(v.tensor_tensor(tmp_t[:], tmp_t[:], has_edges[order][:], ALU.mult))
                step(v.tensor_scalar(last_row[order][:], tmp_t[:], float(ZERO_ROW), None, ALU.add))
                dve.sem_inc(ends_made, 1)

            dve.wait_ge(counted, 1)
            step(v.tensor_copy(degree[0][:], count_ps[0]))
            bounds(0)
            step(v.tensor_scalar(tmp_1[:], row[:], float(TILES), float(PAD_EDGES), ALU.mult, ALU.add))
            step(v.tensor_scalar(spare_row[:], iota[:, 0:TILES], tmp_1[:], None, ALU.add))
            step(v.tensor_tensor(tmp_t[:], start[0][:], spare_row[:], ALU.subtract))
            step(v.tensor_tensor(tmp_t[:], tmp_t[:], has_edges[0][:], ALU.mult))
            step(v.tensor_tensor(start_row[:], tmp_t[:], spare_row[:], ALU.add))
            step(v.tensor_scalar(place_next[:], start[0][:], -float(HALF), None, ALU.add))
            dve.wait_ge(weights_loaded, 160)

            def all_hots(s, n):
                one_hot(hi_hot[s], P, src_hi, n)
                one_hot(lo_hot[s], TILES, src_lo, n).then_inc(hot_made, 1)

            dve.sem_inc(tables_made, 1)
            dve.sem_inc(same_masked, RING)
            dve.sem_inc(places_read, 1)
            dve.sem_inc(attr_used, RING)
            all_hots(0, 0)
            with dve.Fori(0, LOOPS) as i:
                step.enter(i, 9 * RING)
                for s in range(RING):
                    n = i * RING + s
                    dve.wait_ge(deltas_made, n + 1)
                    step(v.tensor_copy(delta_ps[:, :, 0], place_next[:]))
                    step(v.tensor_tensor_scan(place_tables[s][:].rearrange("p t k -> p (t k)"),
                                              not_first[:].rearrange("p t k -> p (t k)"),
                                              bank[0][:, 0:TILES * (K + 1)], 0.0, ALU.mult, ALU.add))
                    step(v.tensor_copy(place_next[:], place_tables[s][:, :, K]))
                    step(v.tensor_copy(place_parts[s][:, 0], place_tables[s][:]))
                    step(v.tensor_tensor(place_parts[s][:, 1], place_tables[s][:], place_parts[s][:, 0], ALU.subtract))
                    dve.sem_inc(tables_made, 1)
                    dve.wait_ge(group_placed, n * NSG + RING)
                    all_hots((s + 1) % RING, n + 1)
                    dve.wait_ge(attr_loaded[s], (i + 1) * 16)
                    dve.wait_ge(payload_free, n + 1)
                    step(v.tensor_tensor(attr_products, attr[s][:].unsqueeze(2).broadcast_to([P, K, HEADS, EDGE_F]),
                                         att_w[:, :, 2 * HEAD_D:].unsqueeze(1).broadcast_to([P, K, HEADS, EDGE_F]),
                                         ALU.mult))
                    dve.sem_inc(attr_used, 1)
                    v.tensor_reduce(payload[s][:, :, 2:PAYLOAD], attr_products, AX.X, ALU.add)
                    v.tensor_copy(payload[s][:, :, 0], dst_f[:, chunk(n)])
                    v.tensor_copy(payload[s][:, :, 1], key[:, chunk(n)])
                    for g, (a, m) in enumerate(STEP_GROUPS):
                        c, r = n * NSG + g, (s * NSG + g) % RING
                        dve.wait_ge(same_made, c + 1)
                        dve.wait_ge(group_placed, c + 1)
                        v.tensor_tensor(same_hi[r][:, 0:m, :], same_ps[r][:, 0:m, :],
                                        later[:].unsqueeze(1).broadcast_to([P, m, P]), ALU.mult)\
                            .then_inc(same_masked, 1)
                    dve.wait_ge(group_placed, n * NSG + NSG + RING)
                    step(v.tensor_tensor(place_products, place_ps, lo_hot[s], ALU.mult))
                    dve.sem_inc(places_read, 1)
                    step(v.tensor_reduce(place_sums[:], place_products, AX.X, ALU.add))
                    step(v.tensor_scalar(index_ring[s][:], place_sums[:], float(HALF), None, ALU.add))
                    dve.sem_inc(payload_made, 1)
                step.leave(LOOPS)

            def normalise(n):
                step(v.tensor_reduce(stat[:], X[:], AX.X, ALU.add))
                step(v.tensor_scalar(stat[:], stat[:], 1.0 / D, None, ALU.mult))
                step(v.tensor_tensor(H[:], X[:], tiles(stat), ALU.subtract))
                step(v.tensor_tensor(V[:], H[:], H[:], ALU.mult))
                step(v.tensor_reduce(stat[:], V[:], AX.X, ALU.add))
                step(v.tensor_scalar(stat[:], stat[:], 1.0 / D, 1e-5, ALU.mult, ALU.add))
                dve.sem_inc(squares_summed, 1)
                dve.wait_ge(roots_made, n)
                step(v.reciprocal(stat[:], stat2[:]))
                step(v.scalar_tensor_tensor(out=H[:], in0=H[:], scalar=0.0, in1=tiles(stat), op0=ALU.max, op1=ALU.mult))

            def read_product(job, add):
                for g, (a, m) in enumerate(TILE_GROUPS):
                    dve.wait_ge(product_made, job * NTG + g + 1)
                    to, got = U[:, a:a + m, :], prod_ps[g % RING][:, 0:m, :]
                    (v.tensor_tensor(to, got, add(a, m), ALU.add) if add else v.tensor_copy(to, got))\
                        .then_inc(product_read, 1)
                    yield g

            def drained(generator):
                for _ in generator:
                    pass

            def product_done(job):
                dve.wait_ge(product_read, job * NTG + NTG)

            bias = lambda b: (lambda a, m: b.unsqueeze(1).broadcast_to([P, m, D]))

            dve.wait_ge(x_loaded, 16)
            normalise(1)
            dve.sem_inc(table_ready, NTG)
            dve.sem_inc(product_input, 1)

            def node_rows_of_steps(order):
                step(v.tensor_copy(id_columns[:].rearrange("p (c j) -> p c j", j=KP),
                                   ids[order][:].rearrange("p (c k) -> p c k", k=K)[:, :, KG:K]))
                for c, (a, m) in enumerate(ID_SPANS):
                    n = order * len(ID_SPANS) + c
                    dve.sem_inc(id_columns_made, 1)
                    dve.wait_ge(id_rows_T_made, n + 1)
                    if n:
                        dve.wait_ge(ids_stored, 16 * n)
                    step(v.tensor_copy(id_rows[0:m, :], id_rows_ps[0:m, :]))
                    dve.sem_inc(id_rows_made, 1)

            def make_parts(pieces):
                for a, rows, rest in pieces:
                    part = lambda c: parts[:, :, c, a:a + rows.shape[-1]]
                    step(v.tensor_copy(part(0), rows))
                    step(v.tensor_tensor(rest, rows, part(0), ALU.subtract))
                    step(v.tensor_copy(part(1), rest))
                    step(v.tensor_tensor(rest, rest, part(1), ALU.subtract))
                    step(v.tensor_copy(part(2), rest))
                dve.sem_inc(parts_ready, 1)

            def runs(order, before):
                v.tensor_tensor(cont[order][:, 1:], key[:, 1:], key[:, 0:STEPS - 1], ALU.is_equal)
                v.tensor_tensor(cont[order][:, 0:1], key[:, 0:1], before, ALU.is_equal)
                step(v.tensor_copy(key0_i[order][:], key[:, 0:1]))

            def fixes(order):
                dve.wait_ge(first_ends_read, 16 * (order + 1))
                step(v.tensor_scalar(tmp_1[:], row[:], float(STEPS), float(STEPS), ALU.mult, ALU.add))
                step(v.tensor_tensor(tmp_2[:], end_of_first[order][:], tmp_1[:], ALU.is_le))
                step(v.tensor_tensor(tmp_2[:], tmp_2[:], cont[order][:, 0:1], ALU.mult))
                step(v.tensor_scalar(tmp_1[:], row[:], float(SPARE), None, ALU.add))
                step(v.scalar_tensor_tensor(out=tmp_3[:], in0=end_of_first[order][:], scalar=-1.0,
                                            in1=tmp_1[:], op0=ALU.add, op1=ALU.subtract))
                step(v.tensor_tensor(tmp_3[:], tmp_3[:], tmp_2[:], ALU.mult))
                step(v.tensor_tensor(fix_row[order][:], tmp_3[:], tmp_1[:], ALU.add))
                step(v.tensor_reduce(tmp_1[:], cont[order][:], AX.X, ALU.min))
                step(v.tensor_scalar(diag[:], ident[:], tmp_1[:], None, ALU.mult))
                dve.sem_inc(diag_made, 1)
                dve.wait_ge(unbroken_read, order + 1)
                step(v.tensor_copy(unbroken[order][:], unbroken_ps))
                if order:
                    step(v.tensor_scalar(unbroken_limit[:], unbroken[1][:], -0.5, None, ALU.add))
                    step(v.tensor_scalar(unbroken_limit[:], unbroken_limit[:], BIG, 2.0, ALU.mult, ALU.mult))

            dve.wait_ge(sorted_loaded, 32)
            step(v.tensor_copy(dst_i[:], sorted_sb[:, :, 0]))
            dve.sem_inc(rows_free, RING)
            step(v.tensor_copy(key[:], sorted_sb[:, :, 1]))
            runs(0, key_before_f[:])
            dve.sem_inc(key0_made, 1)
            node_rows_of_steps(0)
            step(v.tensor_scalar(node_id[:], spare_row[:], -float(PAD_EDGES), None, ALU.add))
            make_parts([(0, H[:], V[:])])
            fixes(0)
            drained(read_product(J_L, bias(bias_l[:])))
            product_done(J_L)
            step(v.tensor_tensor(U[:], U[:], bias_r[:].unsqueeze(1).broadcast_to([P, TILES, D]), ALU.add))

            def attention(n, s):
                over = lambda a: a[:].unsqueeze(2).broadcast_to([P, K, HEADS])
                step(v.tensor_tensor(logit[:], gathered[s][:, :, D:WIDE], terms[:, chunk(n), :], ALU.add))
                step(v.scalar_tensor_tensor(out=logit[:], in0=logit[:], scalar=0.2, in1=logit[:], op0=ALU.mult, op1=ALU.max))
                step(v.tensor_reduce(top[:], logit[:], AX.X, ALU.max))
                step(v.tensor_tensor(logit[:], logit[:], over(top), ALU.subtract))
                dve.sem_inc(logits_shifted, 1)
                dve.wait_ge(exps_made, n + 1)
                step(v.tensor_reduce(top[:], logit[:], AX.X, ALU.add))
                step(v.reciprocal(top[:], top[:]))
                step(v.tensor_tensor(logit[:], logit[:], over(top), ALU.mult))
                step(v.tensor_tensor(scanned[s][:].rearrange("p k (h e) -> p k h e", h=HEADS),
                                     gathered[s][:, :, 0:D].rearrange("p k (h e) -> p k h e", h=HEADS),
                                     logit[:].unsqueeze(3).broadcast_to([P, K, HEADS, HEAD_D]), ALU.mult))

            def count_dst(m, s):
                dve.wait_ge(count_hot_used, m + 1 + CHUNKS)
                one_hot(dhi_hot[s], P, dst_hi, m)
                one_hot(dlo_hot[s], TILES, dst_lo, m).then_inc(count_hot_made, 1)

            def scan_edges(pass_no, order, op, gate, message=None, beside=None):
                reset, neutral = (ALU.mult, 0.0) if op == ALU.add else (ALU.min, -BIG)
                width = WIDE if message else D

                def node_hots(i, s, rows):
                    n = i * RING + s + pass_no * CHUNKS
                    for t in rows:
                        g, b = divmod(t, HOT_TILES)
                        if t == 0:
                            dve.wait_ge(ids_loaded[s], (i + 1) * 16 + pass_no * (16 * LOOPS))
                        if b == 0:
                            dve.wait_ge(node_hot_used, n * HOT_GROUPS + g + 1)
                        made = v.tensor_scalar(node_hot[g][:, b, :], ids_row[s][:], node_id[:, t:t + 1], None, ALU.is_equal)
                        if b == HOT_TILES - 1:
                            made.then_inc(node_hot_made, 1)

                def body(i, s, ahead):
                    m = i * RING + s
                    n = m + pass_no * CHUNKS
                    dve.wait_ge(fetched_copied, n + 1 + RING)
                    rows = gathered[s][:, KG:K, 0:width]
                    part = lambda c: fetched[:, :, c * width:(c + 1) * width]
                    step(v.tensor_tensor(rows, part(0), part(1), ALU.add))
                    step(v.tensor_tensor(rows, rows, part(2), ALU.add))
                    dve.sem_inc(fetched_summed, 1)
                    if beside:
                        beside(m, s)
                    dve.wait_ge(rows_gathered[s], (i + 1) * (16 * KG) + pass_no * (16 * KG * LOOPS))
                    dve.wait_ge(scan_slot_free, n + 1)
                    if message:
                        message(m, s)
                    for k in range(K):
                        before = scanned[s][:, k - 1, :] if k else state[:]
                        row = (scanned if message else gathered)[s][:, k, 0:D]
                        step.wait()
                        step.begin(v.scalar_tensor_tensor(out=scanned[s][:, k, :], in0=before,
                                                          scalar=gate[:, bass.ds(m * K + k, 1)], in1=row,
                                                          op0=reset, op1=op))
                        if ahead:
                            node_hots(i + 1, s, range(TILES * k // K, TILES * (k + 1) // K))
                    step.wait()
                    dve.sem_inc(chunk_scanned, 1)
                    dve.sem_inc(rows_free, 1)
                    step.begin(v.tensor_copy(state[:], scanned[s][:, K - 1, :]))

                step.begin(v.memset(state[:], neutral))
                for s in range(RING):
                    node_hots(0, s, range(TILES))
                with dve.Fori(0, LOOPS - 1) as i:
                    step.enter(i, RING * (K + 3 + (8 if message else 0)))
                    for s in range(RING):
                        body(i, s, True)
                    step.leave(LOOPS - 1)
                for s in range(RING):
                    body(LOOPS - 1, s, False)
                step.wait()
                dve.sem_inc(state_ready, 1)
                dve.wait_ge(state_T_made, pass_no + 1)
                across = unbroken[order] if op == ALU.add else unbroken_limit
                step(v.tensor_tensor_scan(joined_T[:, 1:], across[:], state_T_ps, neutral, reset, op))
                dve.sem_inc(joined_T_made, 1)
                dve.wait_ge(joined_made, pass_no + 1)
                dve.wait_ge(fix_read, (pass_no + 1) * 16)
                step(v.tensor_tensor(fix_rows[:], fix_rows[:], joined_ps, op))
                dve.sem_inc(fix_made, 1)

            def nodes(pass_no):
                for g, (a, m) in enumerate(TILE_GROUPS):
                    dve.wait_ge(nodes_read[g], 16 * m * (pass_no + 1))

            dve.sem_inc(fetched_summed, 1)
            scan_edges(P_SAGE, 0, ALU.add, cont[0], beside=count_dst)
            dve.wait_ge(counted, 2)
            step(v.tensor_copy(degree[1][:], count_ps[1]))
            nodes(P_SAGE)
            step(v.tensor_scalar(tmp_t[:], degree[0][:], 1.0, None, ALU.max))
            step(v.reciprocal(tmp_t[:], tmp_t[:]))
            step(v.tensor_tensor(R[:], R[:], tiles(tmp_t), ALU.mult))
            dve.sem_inc(product_input, 1)
            drained(read_product(J_R, lambda a, m: U[:, a:a + m, :]))
            product_done(J_R)
            step(v.tensor_scalar(U[:], U[:], 0.0, None, ALU.max))
            step(v.tensor_tensor(V[:], U[:], U[:], ALU.mult))
            step(v.tensor_reduce(stat[:], V[:], AX.X, ALU.add))
            dve.sem_inc(squares_summed, 1)
            dve.wait_ge(roots_made, 2)
            step(v.tensor_scalar(stat[:], stat2[:], 1e-6, None, ALU.add))
            step(v.reciprocal(stat[:], stat[:]))
            step(v.tensor_tensor(U[:], U[:], tiles(stat), ALU.mult))
            step(v.tensor_tensor(X[:], X[:], U[:], ALU.add))
            normalise(3)
            dve.sem_inc(product_input, 1)
            drained(read_product(J_WH, None))
            product_done(J_WH)
            for term, a0 in ((dst_term, HEAD_D), (src_term, 0)):
                for h in range(HEADS):
                    step(v.tensor_tensor(V[:, :, h * HEAD_D:(h + 1) * HEAD_D], U[:, :, h * HEAD_D:(h + 1) * HEAD_D],
                                         att_w[:, h, a0:a0 + HEAD_D].unsqueeze(1).broadcast_to([P, TILES, HEAD_D]),
                                         ALU.mult))
                step(v.tensor_reduce(term[:], V[:].rearrange("p t (h e) -> p t h e", h=HEADS), AX.X, ALU.add))
            dve.sem_inc(src_terms_ready, 1)
            bounds(1)
            step(v.tensor_copy(key[:], dst_f[:]))
            step(v.tensor_copy(tmp_1[:], key_before_i[:]))
            runs(1, tmp_1[:])
            dve.sem_inc(key0_made, 1)
            step(v.tensor_scalar(limit[:], cont[1][:], -0.5, None, ALU.add))
            step(v.tensor_scalar(limit[:], limit[:], BIG, 2.0, ALU.mult, ALU.mult))
            node_rows_of_steps(1)
            make_parts([(0, U[:], V[:]), (D, dst_term[:], V[:, :, 0:HEADS])])
            fixes(1)
            dve.wait_ge(first_terms_read, 16)
            for h in range(HEADS):
                step(v.tensor_tensor_scan(terms[:, :, h], cont[0][:], terms[:, :, h], 0.0, ALU.mult, ALU.add))
            step(v.tensor_tensor(terms[:], terms[:], sorted_sb[:, :, 2:PAYLOAD], ALU.add))
            scan_edges(P_ATT, 0, ALU.add, cont[0], attention)
            nodes(P_ATT)
            step(v.tensor_scalar(V[:], R[:], 0.0, None, ALU.min))
            dve.sem_inc(elu_input, 1)
            dve.wait_ge(elu_exp, 1)
            step(v.tensor_scalar(V[:], V[:], -1.0, None, ALU.add))
            step(v.scalar_tensor_tensor(out=R[:], in0=R[:], scalar=0.0, in1=V[:], op0=ALU.max, op1=ALU.add))
            step(v.tensor_tensor(X[:], X[:], R[:], ALU.add))
            normalise(4)
            dve.sem_inc(product_input, 1)
            for g in read_product(J_CONV, bias(bias_2[:, 0, :])):
                dve.wait_ge(product_read, J_CONV * NTG + g + 1)
                dve.sem_inc(table_ready, 1)
            make_parts([(0, U[:], V[:])])
            with dve.Fori(0, ROUNDS - 1) as r:
                step.enter(r, 1 + CHUNKS * (K + 3) + 2 + 5)
                scan_edges(r + P_MAX, 1, ALU.max, limit)
                for g in read_product(r + J_CONV + 1,
                                      lambda a, m: bias_2[:, bass.ds(r + 1, 1), :].broadcast_to([P, m, D])):
                    dve.wait_ge(product_read, (r + J_CONV + 1) * NTG + g + 1)
                    dve.sem_inc(table_ready, 1)
                make_parts([(0, U[:], V[:])])
                step.leave(ROUNDS - 1)
            scan_edges(P_MAX + ROUNDS - 1, 1, ALU.max, limit)
            nodes(P_MAX + ROUNDS - 1)
            step(v.tensor_tensor(X[:], X[:], R[:], ALU.add))
            normalise(5)
            dve.sem_inc(table_ready, NTG)
            make_parts([(0, H[:], V[:])])
            scan_edges(P_GCN_S, 0, ALU.add, cont[0])
            nodes(P_GCN_S)
            step(v.tensor_copy(U[:], R[:]))
            dve.sem_inc(parts_ready, 1)
            scan_edges(P_GCN_D, 1, ALU.add, cont[1])
            nodes(P_GCN_D)
            step(v.tensor_tensor(R[:], R[:], U[:], ALU.add))
            step(v.tensor_tensor(stat[:], degree[0][:], degree[1][:], ALU.add))
            step(v.tensor_scalar(stat[:], stat[:], 1.0, None, ALU.max))
            dve.sem_inc(squares_summed, 1)
            dve.wait_ge(roots_made, 6)
            step(v.reciprocal(stat[:], stat2[:]))
            step(v.tensor_tensor(R[:], R[:], tiles(stat), ALU.mult))
            dve.sem_inc(product_input, 1)
            drained(read_product(J_GCN, bias(bias_3[:])))
            product_done(J_GCN)
            step(v.tensor_tensor(U[:], U[:], H[:], ALU.add))
            dve.sem_inc(gelu_input, 1)
            dve.wait_ge(gelu_made, 1)
            step(v.tensor_tensor(X[:], X[:], U[:], ALU.add))
            dve.sem_inc(out_ready, 1)


INPUTS = ["x", "src", "dst", "edge_attr_16", "L0_gnn_Wl", "L0_gnn_Wr", "L1_gnn_W", "L2_gnn_Ws", "L3_gnn_W",
          "L0_gnn_bl", "L0_gnn_br", "L2_gnn_bs", "L3_gnn_b", "L1_gnn_a"]


def kernel(**inputs):
    import numpy as np
    import concourse.bacc as bacc
    from concourse.bass_utils import run_bass_kernel_spmd

    a = {name: np.asarray(inputs[name]) for name in INPUTS}

    def padded(values, rows, fill):
        more = np.full((rows - values.shape[0],) + values.shape[1:], fill, values.dtype)
        return np.concatenate([values, more])

    a["x"] = padded(a["x"], PAD_NODES, 0)
    a["src"] = padded(a["src"], PAD_EDGES, PAD_NODES - 1)
    a["dst"] = padded(a["dst"], PAD_EDGES, PAD_NODES - 1)
    a["edge_attr_16"] = padded(a["edge_attr_16"], PAD_EDGES, 0)
    a["L2_gnn_Ws"] = a["L2_gnn_Ws"].transpose(0, 2, 1)
    a["L3_gnn_W"] = a["L3_gnn_W"].T
    for name in ("L0_gnn_bl", "L0_gnn_br", "L2_gnn_bs", "L3_gnn_b", "L1_gnn_a"):
        a[name] = a[name].reshape(1, -1)

    nc = bacc.Bacc("TRN2", target_bir_lowering=False, num_devices=1)
    arrays, args = {}, []
    for name in INPUTS:
        arrays[f"in_{name}"] = np.ascontiguousarray(a[name])
        args.append(nc.dram_tensor(f"in_{name}", a[name].shape, mybir.dt.from_np(a[name].dtype),
                                   kind="ExternalInput").ap())
    out = nc.dram_tensor("out_0", (PAD_NODES, D), F32, kind="ExternalOutput").ap()
    build(nc, *args, out)
    r = run_bass_kernel_spmd(nc, [arrays], core_ids=[0])
    return r.results[0]["out_0"][:NODES]
```

```python
import concourse.bass as bass
from concourse import mybir
from concourse.alu_op_type import AluOpType as ALU
from contextlib import ExitStack
import numpy as np

F32 = mybir.dt.float32
F16 = mybir.dt.float16
BF16 = mybir.dt.bfloat16
I32 = mybir.dt.int32
I16 = mybir.dt.int16
ACT = mybir.ActivationFunctionType
AX = mybir.AxisListType

P = 128
NODES = 3125
EDGES = 100000
D = 128
TILES = -(-NODES // P)
PAD_NODES = P * TILES
STEPS = -(-EDGES // P)
PAD_EDGES = P * STEPS
HEADS, HEAD_D, EDGE_F = 4, 32, 16
ROUNDS = 5
RING = 2
K = 17
CHUNKS = STEPS // K
LOOPS = CHUNKS // RING
assert K * CHUNKS == STEPS and LOOPS * RING == CHUNKS
KP = [3, 4]
KG = [K - kp for kp in KP]
GATHERS = [[range(0, kg // 2), range(kg // 2, kg)] for kg in KG]
KP_BEFORE = [sum(KP[:s]) for s in range(RING)]
PARTS = 3
HOT_TILES = 5
HOT_GROUPS = TILES // HOT_TILES
assert HOT_TILES * HOT_GROUPS == TILES
FETCHED = LOOPS * sum(KP)
BIG = 3.4028234e38
HALF = PAD_EDGES // 2
ZERO_ROW = PAD_EDGES
SPARE = PAD_EDGES + 1
SCAN_ROWS = SPARE + P
WIDE = D + HEADS
PAYLOAD = 2 + HEADS

GROUP = 4
STEP_GROUPS = [(a, min(GROUP, K - a)) for a in range(0, K, GROUP)]
NSG = len(STEP_GROUPS)
TILE_GROUPS = [(a, min(GROUP, TILES - a)) for a in range(0, TILES, GROUP)]
NTG = len(TILE_GROUPS)

P_SAGE, P_ATT, P_MAX, P_GCN_S, P_GCN_D = 0, 1, 2, 2 + ROUNDS, 3 + ROUNDS
J_L, J_R, J_WH, J_CONV, J_GCN = 0, 1, 2, 3, 3 + ROUNDS


class Steps:

    def __init__(self, eng, sem):
        self.eng, self.sem, self.n, self.at, self.outer = eng, sem, 0, None, []

    def __call__(self, ins):
        self.begin(ins)
        self.wait()

    def begin(self, ins):
        ins.then_inc(self.sem, 1)
        self.n += 1

    def wait(self):
        self.eng.wait_ge(self.sem, self.value())

    def value(self):
        return self.n if self.at is None else self.at + self.n

    def enter(self, turn, per):
        self.outer.append((self.n, self.at, per))
        self.at, self.n = turn * per + self.value(), 0

    def leave(self, turns):
        n, at, per = self.outer.pop()
        assert self.n == per, (self.n, per)
        self.n, self.at = n + per * turns, at


def build(nc, x, src, dst, edge_attr, Wl, Wr, W1, W2T, W3T, bl, br, b2, b3, att, out):
    es = ExitStack()
    with es:
        def sb(name, shape, dt=F32):
            return es.enter_context(nc.sbuf_tensor(name, shape, dt))

        def sem(name):
            return es.enter_context(nc.semaphore(name))

        table = nc.dram_tensor("table", (PAD_NODES, D), F32).ap()
        wide_table = nc.dram_tensor("wide_table", (PAD_NODES, WIDE), F32).ap()
        src_term_table = nc.dram_tensor("src_term_table", (PAD_NODES, HEADS), F32).ap()
        end_table = [nc.dram_tensor(f"end_table_{o}", (PAD_NODES, 1), F32).ap() for o in "sd"]
        payload_sorted = nc.dram_tensor("payload_sorted", (PAD_EDGES, PAYLOAD), F32).ap()
        src_term_at_start = nc.dram_tensor("src_term_at_start", (PAD_EDGES + PAD_NODES, HEADS), F32).ap()
        fetched_ids = [nc.dram_tensor(f"fetched_ids_{o}", (FETCHED, P), I16).ap() for o in "sd"]
        running = [nc.dram_tensor(f"running_{o}", (SCAN_ROWS, D), F32).ap() for o in "sd"]
        running_pk = [r[0:PAD_EDGES, :].rearrange("(p s) d -> p (s d)", s=STEPS) for r in running]

        X = sb("X", [P, TILES, D])
        H = sb("H", [P, TILES, D])
        R = sb("R", [P, TILES, D])
        U = sb("U", [P, TILES, D])
        src_i = sb("src_i", [P, STEPS], I32)
        dst_i = sb("dst_i", [P, STEPS], I32)
        ids = [dst_i, src_i]
        key = sb("key", [P, STEPS])
        dst_f = sb("dst_f", [P, STEPS])
        cont = [sb("cont_s", [P, STEPS]), sb("cont_d", [P, STEPS])]
        limit = key
        sorted_sb = sb("sorted_sb", [P, STEPS, PAYLOAD])
        terms = sb("terms", [P, STEPS, HEADS])
        dst_hi, dst_lo = (terms[:].rearrange("p s h -> p (s h)")[:, h * STEPS:(h + 1) * STEPS] for h in range(2))

        def carver(tile):
            at = [0]

            def take(shape, dt=F32):
                words = -(-int(np.prod(shape)) * mybir.dt.size(dt) // 4)
                view = tile[:, at[0]:at[0] + words].bitcast(dt)[:, 0:int(np.prod(shape))]
                at[0] += words
                names = "abcd"[:len(shape)]
                return view.rearrange(f"p ({' '.join(names)}) -> p {' '.join(names)}",
                                      **dict(zip(names, shape))) if len(shape) > 1 else view
            return take

        region = sb("region", [P, 6600])
        take = carver(region[:])
        src_hi = take([STEPS + K])
        src_lo = take([STEPS + K])
        lo_hot = [take([K, TILES], F16) for s in range(RING)]
        place_tables = [take([TILES, K + 1]) for s in range(RING)]
        place_parts = [take([2, TILES, K + 1], F16) for s in range(RING)]
        not_first = take([TILES, K + 1])
        hi_hot_T = [take([GROUP, P], F16) for s in range(RING)]
        same_hi = [take([GROUP, P], F16) for s in range(RING)]
        attr = [take([K, EDGE_F]) for s in range(RING)]
        payload = [take([K, PAYLOAD]) for s in range(RING)]
        take = carver(region[:])
        parts = take([TILES, PARTS, WIDE], BF16)
        fetched = take([max(KP), PARTS * WIDE])
        node_hot = [sb(f"node_hot{g}", [P, HOT_TILES, max(KP) * P], BF16) for g in range(HOT_GROUPS)]
        ids_row = [sb(f"ids_row{s}", [P, KP[s] * P], I16) for s in range(RING)]
        id_columns = sb("id_columns", [P, FETCHED])
        id_rows = sb("id_rows", [P, P], I16)
        node_id = sb("node_id", [P, TILES])
        gathered = [sb(f"gathered{s}", [P, K, WIDE]) for s in range(RING)]
        scanned = [sb(f"scanned{s}", [P, K, D]) for s in range(RING)]
        index_ring = [sb(f"index_ring{s}", [P, K], I32) for s in range(RING)]
        hi_hot = [scanned[s][:].rearrange("p k d -> p (k d)").bitcast(F16)[:, 0:K * P]
                  .rearrange("p (k n) -> p k n", k=K) for s in range(RING)]
        in_r = R[:].rearrange("p t d -> p (t d)").bitcast(F16)
        dhi_hot = [in_r[:, s * K * P:(s + 1) * K * P].rearrange("p (k n) -> p k n", k=K) for s in range(RING)]
        dlo_hot = [in_r[:, RING * K * P + s * K * TILES:RING * K * P + (s + 1) * K * TILES]
                   .rearrange("p (k n) -> p k n", k=K) for s in range(RING)]
        hT = [scanned[s][:, 0:GROUP, :] for s in range(RING)]
        iota_i = sb("iota_i", [P, P], I32)
        row_i = sb("row_i", [P, 1], I32)
        iota = sb("iota", [P, P])
        row = sb("row", [P, 1])
        ident = sb("ident", [P, P])
        ident_b = sb("ident_b", [P, P], F16)
        later = sb("later", [P, P])
        ones = sb("ones", [P, P])
        zeros_b = sb("zeros_b", [P, P], F16)
        place_next = sb("place_next", [P, TILES])
        place_products = gathered[0][:].rearrange("p k w -> p (k w)")[:, 0:K * TILES]\
            .rearrange("p (k t) -> p k t", k=K)
        attr_products = gathered[1][:].rearrange("p k w -> p (k w)")[:, 0:K * HEADS * EDGE_F]\
            .rearrange("p (k h f) -> p k h f", k=K, h=HEADS)
        degree = [sb("degree_s", [P, TILES]), sb("degree_d", [P, TILES])]
        start = [sb("start_s", [P, TILES]), sb("start_d", [P, TILES])]
        end = [sb("end_s", [P, TILES]), sb("end_d", [P, TILES])]
        has_edges = [sb("has_edges_s", [P, TILES]), sb("has_edges_d", [P, TILES])]
        place_sums = sb("place_sums", [P, K])
        last_row = [sb("last_row_s", [P, TILES], I32), sb("last_row_d", [P, TILES], I32)]
        start_row = sb("start_row", [P, TILES], I32)
        spare_row = sb("spare_row", [P, TILES])
        tmp_t = sb("tmp_t", [P, TILES])
        tmp_u = sb("tmp_u", [P, TILES])
        key0_i = [sb("key0_s", [P, 1], I32), sb("key0_d", [P, 1], I32)]
        key_before_f = sb("key_before_f", [P, 1])
        key_before_i = sb("key_before_i", [P, 1], I32)
        end_of_first = [sb("end_of_first_s", [P, 1]), sb("end_of_first_d", [P, 1])]
        fix_row = [sb("fix_row_s", [P, 1], I32), sb("fix_row_d", [P, 1], I32)]
        unbroken = [sb("unbroken_s", [P, P]), sb("unbroken_d", [P, P])]
        unbroken_limit = sb("unbroken_limit", [P, P])
        tmp_1 = sb("tmp_1", [P, 1])
        tmp_2 = sb("tmp_2", [P, 1])
        tmp_3 = sb("tmp_3", [P, 1])
        diag = sb("diag", [P, P])
        state = sb("state", [P, D])
        joined_T = sb("joined_T", [P, P + 1])
        fix_rows = sb("fix_rows", [P, D])
        logit = sb("logit", [P, K, HEADS])
        top = sb("top", [P, K])
        stat = sb("stat", [P, TILES])
        stat2 = sb("stat2", [P, TILES])
        dst_term = sb("dst_term", [P, TILES, HEADS])
        src_term = sb("src_term", [P, TILES, HEADS])
        first_terms = sb("first_terms", [P, HEADS])
        w_l, w_r, w_1, w_3 = (sb(n, [P, D]) for n in ("w_l", "w_r", "w_1", "w_3"))
        w_2 = sb("w_2", [P, ROUNDS, D])
        bias_l, bias_r, bias_3 = (sb(n, [P, D]) for n in ("bias_l", "bias_r", "bias_3"))
        bias_2 = sb("bias_2", [P, ROUNDS, D])
        att_w = sb("att_w", [P, HEADS, 2 * HEAD_D + EDGE_F])
        bank = [es.enter_context(nc.psum_tensor(f"bank{b}", [P, 512], F32)) for b in range(8)]

        delta_ps = bank[0][:, 0:TILES * (K + 1)].rearrange("p (t k) -> p t k", k=K + 1)
        place_ps = bank[1][:, 0:K * TILES].rearrange("p (k t) -> p k t", k=K)
        same_ps = [bank[3 + s][:, :].rearrange("p (j e) -> p j e", j=GROUP) for s in range(RING)]
        hot_T_ps = [bank[b][:, 0:256].bitcast(F16).rearrange("p (j e) -> p j e", j=GROUP) for b in (2, 5)]
        count_ps = [bank[6][:, 0:TILES], bank[4][:, 0:TILES]]
        offset_ps = bank[4][:, 0:1]
        hT_ps = [bank[s][:, :].rearrange("p (j n) -> p j n", j=GROUP) for s in range(RING)]
        prod_ps = [bank[2 + s][:, :].rearrange("p (j o) -> p j o", j=GROUP) for s in range(RING)]
        state_T_ps = bank[4][:, 0:P]
        joined_ps = bank[4][:, 0:P]
        unbroken_ps = bank[4][:, 0:P]
        id_rows_ps = bank[4][:, 0:P]
        fetched_ps = [[bank[b + j] for j in range(kp)] for b, kp in zip((5, 0), KP)]

        iota_made = sem("iota_made")
        edges_loaded = sem("edges_loaded")
        x_loaded = sem("x_loaded")
        weights_loaded = sem("weights_loaded")
        vec = sem("vec")
        constants_made = sem("constants_made")
        zeros_made = sem("zeros_made")
        zeros_stored = sem("zeros_stored")
        count_hot_made = sem("count_hot_made")
        count_hot_used = sem("count_hot_used")
        counted = sem("counted")
        totals_made = sem("totals_made")
        offsets_made = sem("offsets_made")
        hot_made = sem("hot_made")
        deltas_made = sem("deltas_made")
        tables_made = sem("tables_made")
        hot_T_made = sem("hot_T_made")
        hot_T_copied = sem("hot_T_copied")
        same_made = sem("same_made")
        same_masked = sem("same_masked")
        group_placed = sem("group_placed")
        places_read = sem("places_read")
        attr_loaded = [sem(f"attr_loaded{s}") for s in range(RING)]
        attr_used = sem("attr_used")
        payload_made = sem("payload_made")
        scattered = [sem(f"scattered{s}") for s in range(RING)]
        payload_free = sem("payload_free")
        scattering = sem("scattering")
        sorted_loaded = sem("sorted_loaded")
        ends_made = sem("ends_made")
        ends_stored = sem("ends_stored")
        key0_made = sem("key0_made")
        first_ends_read = sem("first_ends_read")
        diag_made = sem("diag_made")
        unbroken_read = sem("unbroken_read")
        rows_free = sem("rows_free")
        index_copied = sem("index_copied")
        gathering = sem("gathering")
        rows_gathered = [[sem(f"rows_gathered{s}_{h}") for h in range(2)] for s in range(RING)]
        chunk_scanned = sem("chunk_scanned")
        running_stored = sem("running_stored")
        scan_slot_free = sem("scan_slot_free")
        logits_shifted = sem("logits_shifted")
        exps_made = sem("exps_made")
        state_ready = sem("state_ready")
        state_T_made = sem("state_T_made")
        joined_T_made = sem("joined_T_made")
        joined_made = sem("joined_made")
        fix_read = sem("fix_read")
        fix_made = sem("fix_made")
        fix_written = sem("fix_written")
        nodes_read = [sem(f"nodes_read{g}") for g in range(NTG)]
        product_input = sem("product_input")
        tiles_T_made = sem("tiles_T_made")
        tiles_T_copied = sem("tiles_T_copied")
        product_made = sem("product_made")
        product_read = sem("product_read")
        silu_made = sem("silu_made")
        squares_summed = sem("squares_summed")
        roots_made = sem("roots_made")
        table_ready = sem("table_ready")
        table_stored = sem("table_stored")
        wide_stored = sem("wide_stored")
        src_terms_ready = sem("src_terms_ready")
        dst_terms_ready = sem("dst_terms_ready")
        src_terms_stored = sem("src_terms_stored")
        src_terms_scattered = sem("src_terms_scattered")
        src_terms_loaded = sem("src_terms_loaded")
        first_terms_read = sem("first_terms_read")
        id_columns_made = sem("id_columns_made")
        id_rows_T_made = sem("id_rows_T_made")
        id_rows_made = sem("id_rows_made")
        ids_stored = sem("ids_stored")
        parts_ready = sem("parts_ready")
        ids_loaded = [sem(f"ids_loaded{s}") for s in range(RING)]
        node_hot_made = sem("node_hot_made")
        node_hot_used = sem("node_hot_used")
        fetched_copied = sem("fetched_copied")
        fetched_summed = sem("fetched_summed")
        elu_input = sem("elu_input")
        elu_exp = sem("elu_exp")
        gelu_input = sem("gelu_input")
        gelu_made = sem("gelu_made")
        out_ready = sem("out_ready")
        out_stored = sem("out_stored")
        block = es.enter_context(nc.Block())

        by_node = lambda t: t.rearrange("(p t) d -> p t d", t=TILES)
        chunk = lambda n: bass.ds(n * K, K)
        ID_SPANS = [(a, min(P, FETCHED - a)) for a in range(0, FETCHED, P)]

        @block.sync
        def _(sp):
            per_edge = lambda a: a.rearrange("(p s) -> p s", s=STEPS)
            sp.dma_start(src_i[:], per_edge(src)).then_inc(edges_loaded, 16)
            sp.dma_start(dst_i[:], per_edge(dst)).then_inc(edges_loaded, 16)
            sp.wait_ge(zeros_made, 1)
            with nc.allow_non_contiguous_dma(reason="one word of each partition"):
                sp.dma_start(key_before_i[1:P, :], per_edge(dst)[0:P - 1, STEPS - 1:STEPS]).then_inc(edges_loaded, 16)
            sp.dma_start(X[:], by_node(x)).then_inc(x_loaded, 16)
            for tile, a in ((w_l[:], Wl), (w_r[:], Wr), (w_1[:], W1), (w_3[:], W3T),
                            (w_2[:], W2T.rearrange("r i o -> i r o")),
                            (bias_l[:], bl.broadcast_to([P, D])), (bias_r[:], br.broadcast_to([P, D])),
                            (bias_3[:], b3.broadcast_to([P, D])),
                            (bias_2[:].rearrange("p r d -> p (r d)"), b2.broadcast_to([P, ROUNDS * D])),
                            (att_w[:].rearrange("p h a -> p (h a)"),
                             att.broadcast_to([P, HEADS * (2 * HEAD_D + EDGE_F)]))):
                sp.dma_start(tile, a).then_inc(weights_loaded, 16)
            sp.dma_start(src_term_at_start[0:PAD_EDGES, :].rearrange("(p s) h -> p (s h)", s=STEPS),
                         terms[:].rearrange("p s h -> p (s h)")).then_inc(zeros_stored, 16)
            for r in running:
                sp.dma_start(r[ZERO_ROW:ZERO_ROW + 1, :], terms[0:1, 0:D // HEADS, :].rearrange("p s h -> p (s h)"))\
                    .then_inc(zeros_stored, 16)
                sp.dma_start(r[SPARE:SCAN_ROWS, :], terms[:, 0:D // HEADS, :].rearrange("p s h -> p (s h)"))\
                    .then_inc(zeros_stored, 16)

            sp.sem_inc(payload_free, RING)
            with sp.Fori(0, LOOPS) as i:
                for s in range(RING):
                    sp.wait_ge(scattered[s], (i + 1) * (16 * K))
                    sp.sem_inc(payload_free, 1)
            sorted_pk = payload_sorted.rearrange("(p s) c -> p s c", s=STEPS)
            sp.dma_start(sorted_sb[:], sorted_pk).then_inc(sorted_loaded, 16)
            with nc.allow_non_contiguous_dma(reason="one word of each partition"):
                sp.dma_start(key_before_f[1:P, :], sorted_pk[0:P - 1, STEPS - 1, 1:2]).then_inc(sorted_loaded, 16)

            def store_ids(order):
                for c, (a, m) in enumerate(ID_SPANS):
                    sp.wait_ge(id_rows_made, order * len(ID_SPANS) + c + 1)
                    sp.dma_start(fetched_ids[order][a:a + m, :], id_rows[0:m, :]).then_inc(ids_stored, 16)

            def store_ends(order):
                sp.wait_ge(ends_made, order + 1)
                with nc.allow_non_contiguous_dma(reason="a word of each node"):
                    sp.dma_start(by_node(end_table[order]), end[order][:].unsqueeze(2)).then_inc(ends_stored, 16)

            store_ends(0)

            def store_table(groups_before, rows):
                for g, (a, m) in enumerate(TILE_GROUPS):
                    sp.wait_ge(table_ready, groups_before + g + 1)
                    sp.dma_start(by_node(table)[:, a:a + m, :], rows[:, a:a + m, :]).then_inc(table_stored, 16)

            def store_running(pass_no, order):
                with sp.Fori(0, LOOPS) as i:
                    for s in range(RING):
                        n = i * RING + s + pass_no * CHUNKS
                        sp.wait_ge(chunk_scanned, n + 1)
                        sp.dma_start(running_pk[order][:, bass.ds((i * RING + s) * (K * D), K * D)],
                                     scanned[s][:].rearrange("p k d -> p (k d)")).then_inc(running_stored, 16)
                        sp.wait_ge(running_stored, (n + 1) * 16)
                        sp.sem_inc(scan_slot_free, 1)

            sp.sem_inc(scan_slot_free, RING)
            store_ids(0)
            store_table(0, H)
            store_running(P_SAGE, 0)
            store_ends(1)
            store_ids(1)
            sp.wait_ge(src_terms_ready, 1)
            with nc.allow_non_contiguous_dma(reason="four words of each node"):
                sp.dma_start(by_node(src_term_table), src_term[:]).then_inc(src_terms_stored, 16)
                sp.dma_start(by_node(wide_table)[:, :, 0:D], U[:]).then_inc(wide_stored, 16)
                sp.wait_ge(dst_terms_ready, 1)
                sp.dma_start(by_node(wide_table)[:, :, D:WIDE], dst_term[:]).then_inc(wide_stored, 16)
            sp.wait_ge(src_terms_scattered, 16 * TILES)
            sp.dma_start(terms[:].rearrange("p s h -> p (s h)"),
                         src_term_at_start[0:PAD_EDGES, :].rearrange("(p s) h -> p (s h)", s=STEPS))\
                .then_inc(src_terms_loaded, 16)
            store_running(P_ATT, 0)
            store_table(NTG, U)
            with sp.Fori(0, ROUNDS - 1) as r:
                store_running(r + P_MAX, 1)
                store_table((r + 2) * NTG, U)
            store_running(P_MAX + ROUNDS - 1, 1)
            store_table((ROUNDS + 1) * NTG, H)
            store_running(P_GCN_S, 0)
            store_running(P_GCN_D, 1)
            for g, (a, m) in enumerate(TILE_GROUPS):
                sp.wait_ge(out_ready, g + 1)
                sp.dma_start(by_node(out)[:, a:a + m, :], X[:, a:a + m, :]).then_inc(out_stored, 16)
            sp.wait_ge(out_stored, 16 * NTG)
            sp.wait_ge(zeros_stored, 16 * 5)
            sp.wait_ge(table_stored, 16 * NTG * (ROUNDS + 2))

        @block.gpsimd
        def _(pool):
            pool.iota(iota_i[:], pattern=[[1, P]], base=0, channel_multiplier=0).then_inc(iota_made, 1)
            pool.iota(row_i[:], pattern=[[0, 1]], base=0, channel_multiplier=1).then_inc(iota_made, 1)

            def gather(out_, table_, index, done):
                pool.indirect_dma_start(out=out_, out_offset=None, in_=table_,
                                        in_offset=bass.IndirectOffsetOnAxis(ap=index, axis=0)).then_inc(done, 16)

            def scatter(table_, index, rows, done):
                pool.indirect_dma_start(out=table_, out_offset=bass.IndirectOffsetOnAxis(ap=index, axis=0),
                                        in_=rows, in_offset=None).then_inc(done, 16)

            with pool.Fori(0, LOOPS) as i:
                for s in range(RING):
                    n = i * RING + s
                    pool.wait_ge(payload_made, n + 1)
                    pool.sem_inc(scattering, 1)
                    for k in range(K):
                        scatter(payload_sorted, index_ring[s][:, k:k + 1], payload[s][:, k, :], scattered[s])

            def read_first_ends(order):
                pool.wait_ge(ends_stored, 16 * (order + 1))
                pool.wait_ge(key0_made, order + 1)
                gather(end_of_first[order][:], end_table[order], key0_i[order][:], first_ends_read)

            def gather_edges(pass_no, order, table_, width):
                with pool.Fori(0, LOOPS) as i:
                    for s in range(RING):
                        n = i * RING + s + pass_no * CHUNKS
                        pool.wait_ge(rows_free, n + 1)
                        pool.tensor_copy(index_ring[s][:], ids[order][:, chunk(i * RING + s)]).then_inc(index_copied, 1)
                        pool.wait_ge(index_copied, n + 1)
                        pool.sem_inc(gathering, 1)
                        for h, steps in enumerate(GATHERS[s]):
                            for k in steps:
                                gather(gathered[s][:, k, 0:width], table_, index_ring[s][:, k:k + 1],
                                       rows_gathered[s][h])

            def read_nodes(pass_no, order):
                pool.wait_ge(state_ready, pass_no + 1)
                pool.wait_ge(scan_slot_free, (pass_no + 1) * CHUNKS + RING)
                pool.sem_inc(gathering, 1)
                gather(fix_rows[:], running[order], fix_row[order][:], fix_read)
                pool.wait_ge(fix_made, pass_no + 1)
                pool.sem_inc(gathering, 1)
                scatter(running[order], fix_row[order][:], fix_rows[:], fix_written)
                pool.wait_ge(fix_written, (pass_no + 1) * 16)
                pool.sem_inc(gathering, 1)
                for g, (a, m) in enumerate(TILE_GROUPS):
                    for t in range(a, a + m):
                        gather(R[:, t, :], running[order], last_row[order][:, t:t + 1], nodes_read[g])

            pool.wait_ge(zeros_stored, 16 * 5)
            pool.wait_ge(table_stored, 16 * NTG)
            gather_edges(P_SAGE, 0, table, D)
            read_first_ends(0)
            read_nodes(P_SAGE, 0)
            read_first_ends(1)
            pool.wait_ge(src_terms_ready, 1)
            for t in range(TILES):
                scatter(src_term_at_start, start_row[:, t:t + 1], src_term[:, t, :], src_terms_scattered)
            pool.wait_ge(src_terms_stored, 16)
            pool.sem_inc(gathering, 1)
            gather(first_terms[:], src_term_table, key0_i[0][:], first_terms_read)
            pool.wait_ge(wide_stored, 32)
            gather_edges(P_ATT, 0, wide_table, WIDE)
            read_nodes(P_ATT, 0)
            pool.wait_ge(table_stored, 16 * NTG * 2)
            with pool.Fori(0, ROUNDS - 1) as r:
                gather_edges(r + P_MAX, 1, table, D)
                read_nodes(r + P_MAX, 1)
                pool.wait_ge(table_stored, r * (16 * NTG) + 16 * NTG * 3)
            gather_edges(P_MAX + ROUNDS - 1, 1, table, D)
            read_nodes(P_MAX + ROUNDS - 1, 1)
            pool.wait_ge(table_stored, 16 * NTG * (ROUNDS + 2))
            gather_edges(P_GCN_S, 0, table, D)
            read_nodes(P_GCN_S, 0)
            gather_edges(P_GCN_D, 1, table, D)
            read_nodes(P_GCN_D, 1)

        @block.tensor
        def _(pe):
            def count_begin(order):
                nc.tensor.matmul(count_ps[order], zeros_b[:], zeros_b[:, 0:TILES], start=True, stop=False)

            def count_chunk(order, m, s, his, los):
                pe.wait_ge(count_hot_made, m + 1 + order * CHUNKS)
                for k in range(K):
                    last = nc.tensor.matmul(count_ps[order], his[s][:, k, :], los[s][:, k, :], start=False, stop=False)
                last.then_inc(count_hot_used, 1)

            def count_end(order):
                nc.tensor.matmul(count_ps[order], zeros_b[:], zeros_b[:, 0:TILES], start=False, stop=True)\
                    .then_inc(counted, 1)

            pe.wait_ge(constants_made, 1)
            pe.sem_inc(count_hot_used, RING)
            count_begin(0)
            with pe.Fori(0, LOOPS) as i:
                for s in range(RING):
                    count_chunk(0, i * RING + s, s, hi_hot, lo_hot)
            count_end(0)

            def offsets(n):
                pe.wait_ge(totals_made, n)
                nc.tensor.matmul(offset_ps, later[:], tmp_1[:], start=True, stop=True).then_inc(offsets_made, 1)

            offsets(1)
            pe.sem_inc(group_placed, RING)
            with pe.Fori(0, LOOPS) as i:
                for s in range(RING):
                    n = i * RING + s
                    pe.wait_ge(hot_made, n + 1)
                    pe.wait_ge(tables_made, n + 1)
                    for k in range(K):
                        last = nc.tensor.matmul(delta_ps[:, :, k + 1], hi_hot[s][:, k, :], lo_hot[s][:, k, :],
                                                start=True, stop=True)
                    last.then_inc(deltas_made, 1)
                    for g in range(NSG + 2):
                        if g < NSG:
                            a, m = STEP_GROUPS[g]
                            c, r = n * NSG + g, (s * NSG + g) % RING
                            pe.wait_ge(hot_T_copied, c + 1)
                            for j in range(m):
                                last = nc.tensor.transpose(hot_T_ps[r][:, j, :], hi_hot[s][:, a + j, :], ident_b[:])
                            last.then_inc(hot_T_made, 1)
                        if 1 <= g <= NSG:
                            a, m = STEP_GROUPS[g - 1]
                            c, r = n * NSG + g - 1, (s * NSG + g - 1) % RING
                            pe.wait_ge(hot_T_copied, c + 1 + RING)
                            pe.wait_ge(same_masked, c + 1)
                            for j in range(m):
                                last = nc.tensor.matmul(same_ps[r][:, j, :], hi_hot_T[r][:, j, :], hi_hot_T[r][:, j, :],
                                                        start=True, stop=True)
                            last.then_inc(same_made, 1)
                        if g >= 2:
                            a, m = STEP_GROUPS[g - 2]
                            c, r = n * NSG + g - 2, (s * NSG + g - 2) % RING
                            if g == 2:
                                pe.wait_ge(tables_made, n + 2)
                                pe.wait_ge(places_read, n + 1)
                            pe.wait_ge(same_masked, c + 1 + RING)
                            for j in range(m):
                                for part in range(2):
                                    nc.tensor.matmul(place_ps[:, a + j, :], hi_hot_T[r][:, j, :],
                                                     place_parts[s][:, part, :, a + j], start=part == 0, stop=False)
                                last = nc.tensor.matmul(place_ps[:, a + j, :], same_hi[r][:, j, :],
                                                        lo_hot[s][:, a + j, :], start=False, stop=True)
                            last.then_inc(group_placed, 1)

            def spread_unbroken(order):
                pe.wait_ge(diag_made, order + 1)
                nc.tensor.matmul(unbroken_ps, ones[:], diag[:], start=True, stop=True).then_inc(unbroken_read, 1)

            def transpose_ids(order):
                for c, (a, m) in enumerate(ID_SPANS):
                    pe.wait_ge(id_columns_made, order * len(ID_SPANS) + c + 1)
                    nc.tensor.transpose(id_rows_ps[0:m, :], id_columns[:, a:a + m], ident[:]).then_inc(id_rows_T_made, 1)

            def fetch(pass_no, width, beside=None):
                def body(i, s):
                    n = i * RING + s + pass_no * CHUNKS
                    pe.wait_ge(fetched_copied, n + 1)
                    for g in range(HOT_GROUPS):
                        pe.wait_ge(node_hot_made, n * HOT_GROUPS + g + 1)
                        for b in range(HOT_TILES):
                            t = g * HOT_TILES + b
                            for j in range(KP[s]):
                                last = nc.tensor.matmul(fetched_ps[s][j][:, 0:PARTS * width],
                                                        node_hot[g][:, b, j * P:(j + 1) * P], parts[:, t, :, 0:width],
                                                        start=t == 0, stop=t == TILES - 1)
                        last.then_inc(node_hot_used, 1)

                if beside:
                    pe.wait_ge(parts_ready, pass_no + 1)
                    for s in range(RING):
                        body(0, s)
                    with pe.Fori(0, LOOPS - 1) as i:
                        for s in range(RING):
                            beside(i * RING + s, s)
                            body(i + 1, s)
                    for s in range(RING):
                        beside((LOOPS - 1) * RING + s, s)
                    return
                with pe.Fori(0, LOOPS) as i:
                    pe.wait_ge(parts_ready, pass_no + 1)
                    for s in range(RING):
                        body(i, s)

            pe.sem_inc(node_hot_used, HOT_GROUPS)
            transpose_ids(0)

            def product(job, tiles, weight, ready):
                def transposes(g):
                    a, m = TILE_GROUPS[g]
                    ready(g)
                    if not (isinstance(job, int) and job == 0 and g < RING):
                        pe.wait_ge(tiles_T_copied, job * NTG + max(g - RING + 1, 0))
                    for j in range(m):
                        last = nc.tensor.transpose(hT_ps[g % RING][:, j, :], tiles[:, a + j, :], ident[:])
                    last.then_inc(tiles_T_made, 1)

                def products(g):
                    a, m = TILE_GROUPS[g]
                    pe.wait_ge(tiles_T_copied, job * NTG + g + 1)
                    if not (isinstance(job, int) and job == 0 and g < RING):
                        pe.wait_ge(product_read, job * NTG + max(g - RING + 1, 0))
                    for j in range(m):
                        last = nc.tensor.matmul(prod_ps[g % RING][:, j, :], hT[g % RING][:, j, :], weight,
                                                start=True, stop=True)
                    last.then_inc(product_made, 1)

                for g in range(NTG + 1):
                    if g < NTG:
                        transposes(g)
                    if g >= 1:
                        products(g - 1)

            def join(pass_no):
                pe.wait_ge(state_ready, pass_no + 1)
                nc.tensor.transpose(state_T_ps, state[:], ident[:]).then_inc(state_T_made, 1)
                pe.wait_ge(joined_T_made, pass_no + 1)
                nc.tensor.transpose(joined_ps, joined_T[:, 0:P], ident[:]).then_inc(joined_made, 1)

            inputs = lambda n: (lambda g: pe.wait_ge(product_input, (n - 1) * NTG + g + 1))
            pe.wait_ge(weights_loaded, 160)
            pe.wait_ge(node_hot_made, 1)
            count_begin(1)
            fetch(P_SAGE, D, lambda m, s: count_chunk(1, m, s, dhi_hot, dlo_hot))
            count_end(1)
            spread_unbroken(0)
            join(P_SAGE)
            pe.wait_ge(scan_slot_free, CHUNKS + RING)
            product(J_L, H, w_l[:], inputs(1))
            offsets(2)
            transpose_ids(1)
            product(J_R, R, w_r[:], inputs(2))
            product(J_WH, H, w_1[:], inputs(3))
            spread_unbroken(1)
            fetch(P_ATT, WIDE)
            join(P_ATT)
            product(J_CONV, H, w_2[:, 0, :], inputs(4))
            with pe.Fori(0, ROUNDS - 1) as r:
                fetch(r + P_MAX, D)
                join(r + P_MAX)
                product(r + J_CONV + 1, R, w_2[:, bass.ds(r + 1, 1), :].rearrange("p a o -> p (a o)"),
                        lambda g: pe.wait_ge(silu_made, r * NTG + g + 1))
            for pass_no in (P_MAX + ROUNDS - 1, P_GCN_S, P_GCN_D):
                fetch(pass_no, D)
                join(pass_no)
            product(J_GCN, R, w_3[:], inputs(5))

        @block.scalar
        def _(act):
            act.wait_ge(constants_made, 1)
            act.sem_inc(hot_T_copied, RING)
            with act.Fori(0, LOOPS) as i:
                for s in range(RING):
                    n = i * RING + s
                    act.wait_ge(attr_used, n + 1)
                    act.dma_start(attr[s][:].rearrange("p k f -> p (k f)"),
                                  edge_attr.rearrange("(p s) f -> p (s f)", s=STEPS)
                                  [:, bass.ds(n * (K * EDGE_F), K * EDGE_F)])\
                        .then_inc(attr_loaded[s], 16)
                    for g, (a, m) in enumerate(STEP_GROUPS):
                        c, r = n * NSG + g, (s * NSG + g) % RING
                        act.wait_ge(hot_T_made, c + 1)
                        act.wait_ge(group_placed, c + 1)
                        nc.scalar.activation(hi_hot_T[r][:, 0:m, :], hot_T_ps[r][:, 0:m, :], ACT.Copy)\
                            .then_inc(hot_T_copied, 1)

            def transposed(job, g):
                a, m = TILE_GROUPS[g]
                act.wait_ge(tiles_T_made, job * NTG + g + 1)
                if not (isinstance(job, int) and job == 0 and g < RING):
                    act.wait_ge(product_made, job * NTG + max(g - RING + 1, 0))
                nc.scalar.activation(hT[g % RING][:, 0:m, :], hT_ps[g % RING][:, 0:m, :], ACT.Copy)\
                    .then_inc(tiles_T_copied, 1)

            def product(job):
                for g in range(NTG):
                    transposed(job, g)

            def root(n):
                act.wait_ge(squares_summed, n)
                nc.scalar.activation(stat2[:], stat[:], ACT.Sqrt).then_inc(roots_made, 1)

            def load_ids(order, i, s):
                act.dma_start(ids_row[s][:], fetched_ids[order].rearrange("(a c) p -> a (c p)", a=1)
                              [:, bass.ds(i * (sum(KP) * P) + KP_BEFORE[s] * P, KP[s] * P)]
                              .broadcast_to([P, KP[s] * P])).then_inc(ids_loaded[s], 16)

            def copy_fetched(pass_no, order, width, next_order, attend=False):

                def body(i, s, ahead):
                    m = i * RING + s
                    n = m + pass_no * CHUNKS
                    act.wait_ge(node_hot_used, n * HOT_GROUPS + 2 * HOT_GROUPS)
                    act.wait_ge(fetched_summed, n + 1)
                    for j in range(KP[s]):
                        last = nc.scalar.activation(fetched[:, j, 0:PARTS * width], fetched_ps[s][j][:, 0:PARTS * width],
                                                    ACT.Copy)
                    last.then_inc(fetched_copied, 1)
                    if ahead:
                        load_ids(order, i + 1, s)
                    if attend:
                        act.wait_ge(logits_shifted, m + 1)
                        nc.scalar.activation(logit[:], logit[:], ACT.Exp).then_inc(exps_made, 1)

                with act.Fori(0, LOOPS - 1) as i:
                    for s in range(RING):
                        body(i, s, True)
                for s in range(RING):
                    body(LOOPS - 1, s, False)
                    if next_order is not None:
                        load_ids(next_order, 0, s)

            act.sem_inc(fetched_copied, RING)
            root(1)
            act.wait_ge(ids_stored, 16 * len(ID_SPANS))
            for s in range(RING):
                load_ids(0, 0, s)
            copy_fetched(P_SAGE, 0, D, 0)
            product(J_L)
            product(J_R)
            root(2)
            root(3)
            product(J_WH)
            act.wait_ge(ids_stored, 16 * len(ID_SPANS) * 2)
            copy_fetched(P_ATT, 0, WIDE, 1, attend=True)
            for g, (a, m) in enumerate(TILE_GROUPS):
                act.wait_ge(elu_input, g + 1)
                nc.scalar.activation(U[:, a:a + m, :], U[:, a:a + m, :], ACT.Exp).then_inc(elu_exp, 1)
            root(4)
            product(J_CONV)
            with act.Fori(0, ROUNDS - 1) as r:
                copy_fetched(r + P_MAX, 1, D, 1)
                for g in range(NTG + 1):
                    if g < NTG:
                        a, m = TILE_GROUPS[g]
                        act.wait_ge(nodes_read[g], r * (16 * m) + 16 * m * (P_MAX + 1))
                        nc.scalar.activation(R[:, a:a + m, :], R[:, a:a + m, :], ACT.Silu).then_inc(silu_made, 1)
                    if g >= 1:
                        transposed(r + J_CONV + 1, g - 1)
            copy_fetched(P_MAX + ROUNDS - 1, 1, D, 0)
            root(5)
            copy_fetched(P_GCN_S, 0, D, 1)
            copy_fetched(P_GCN_D, 1, D, None)
            root(6)
            for g in range(NTG + 1):
                if g < NTG:
                    transposed(J_GCN, g)
                if g >= 1:
                    a, m = TILE_GROUPS[g - 1]
                    act.wait_ge(gelu_input, g)
                    nc.scalar.activation(U[:, a:a + m, :], U[:, a:a + m, :], ACT.Gelu).then_inc(gelu_made, 1)

        @block.vector
        def _(dve):
            v = nc.vector
            step = Steps(dve, vec)

            step(v.memset(terms[:], 0.0))
            step(v.memset(key_before_i[:], -1))
            dve.sem_inc(zeros_made, 1)
            step(v.memset(key_before_f[:], -1.0))
            step(v.memset(ones[:], 1.0))
            step(v.memset(zeros_b[:], 0.0))
            step(v.memset(joined_T[:], 0.0))
            for a in (src_hi, src_lo):
                step(v.memset(a[:, STEPS:], 0.0))
            step(v.memset(not_first[:], 1.0))
            step(v.memset(not_first[:, :, 0], 0.0))
            dve.wait_ge(iota_made, 2)
            step(v.tensor_copy(iota[:], iota_i[:]))
            step(v.tensor_copy(row[:], row_i[:]))
            step(v.tensor_scalar(ident[:], iota[:], row[:], None, ALU.is_equal))
            step(v.tensor_scalar(ident_b[:], iota[:], row[:], None, ALU.is_equal))
            step(v.tensor_scalar(later[:], iota[:], row[:], None, ALU.is_gt))
            dve.sem_inc(constants_made, 1)
            dve.wait_ge(edges_loaded, 48)

            def split(ids_i, ids_f, hi, lo):
                step(v.tensor_copy(ids_f[:], ids_i[:]))
                step(v.tensor_scalar(sorted_sb[:, :, 0].bitcast(I32), ids_f[:], 1.0 / TILES, -0.48, ALU.mult, ALU.add))
                step(v.tensor_copy(hi[:, 0:STEPS], sorted_sb[:, :, 0].bitcast(I32)))
                step(v.scalar_tensor_tensor(out=lo[:, 0:STEPS], in0=hi[:, 0:STEPS], scalar=-float(TILES), in1=ids_f[:],
                                            op0=ALU.mult, op1=ALU.add))

            split(src_i, key, src_hi, src_lo)

            def one_hot(hot, width, value, n):
                return v.tensor_tensor(hot, iota[:, 0:width].unsqueeze(1).broadcast_to([P, K, width]),
                                       value[:, chunk(n)].unsqueeze(2).broadcast_to([P, K, width]), ALU.is_equal)

            with dve.Fori(0, LOOPS) as i:
                for s in range(RING):
                    n = i * RING + s
                    dve.wait_ge(count_hot_used, n + 1)
                    one_hot(hi_hot[s], P, src_hi, n)
                    one_hot(lo_hot[s], TILES, src_lo, n).then_inc(count_hot_made, 1)
            dve.wait_ge(zeros_stored, 16 * 5)
            split(dst_i, dst_f, dst_hi, dst_lo)

            def bounds(order):
                step(v.tensor_tensor_scan(end[order][:], ones[:, 0:TILES], degree[order][:], 0.0, ALU.mult, ALU.add))
                step(v.tensor_copy(tmp_1[:], end[order][:, TILES - 1:TILES]))
                dve.sem_inc(totals_made, 1)
                dve.wait_ge(offsets_made, order + 1)
                step(v.tensor_copy(tmp_2[:], offset_ps))
                step(v.tensor_scalar(end[order][:], end[order][:], tmp_2[:], None, ALU.add))
                step(v.tensor_tensor(start[order][:], end[order][:], degree[order][:], ALU.subtract))
                step(v.tensor_scalar(has_edges[order][:], degree[order][:], 0.0, None, ALU.is_gt))
                step(v.tensor_scalar(tmp_t[:], end[order][:], -1.0 - ZERO_ROW, None, ALU.add))
                step(v.tensor_tensor(tmp_t[:], tmp_t[:], has_edges[order][:], ALU.mult))
                step(v.tensor_scalar(last_row[order][:], tmp_t[:], float(ZERO_ROW), None, ALU.add))
                dve.sem_inc(ends_made, 1)

            dve.wait_ge(counted, 1)
            step(v.tensor_copy(degree[0][:], count_ps[0]))
            bounds(0)
            step(v.tensor_scalar(tmp_1[:], row[:], float(TILES), float(PAD_EDGES), ALU.mult, ALU.add))
            step(v.tensor_scalar(spare_row[:], iota[:, 0:TILES], tmp_1[:], None, ALU.add))
            step(v.tensor_tensor(tmp_t[:], start[0][:], spare_row[:], ALU.subtract))
            step(v.tensor_tensor(tmp_t[:], tmp_t[:], has_edges[0][:], ALU.mult))
            step(v.tensor_tensor(start_row[:], tmp_t[:], spare_row[:], ALU.add))
            step(v.tensor_scalar(place_next[:], start[0][:], -float(HALF), None, ALU.add))
            dve.wait_ge(weights_loaded, 160)

            def all_hots(s, n):
                one_hot(hi_hot[s], P, src_hi, n)
                one_hot(lo_hot[s], TILES, src_lo, n).then_inc(hot_made, 1)

            dve.sem_inc(tables_made, 1)
            dve.sem_inc(same_masked, RING)
            dve.sem_inc(places_read, 1)
            dve.sem_inc(attr_used, RING)
            all_hots(0, 0)
            with dve.Fori(0, LOOPS) as i:
                step.enter(i, 9 * RING)
                for s in range(RING):
                    n = i * RING + s
                    dve.wait_ge(deltas_made, n + 1)
                    step(v.tensor_copy(delta_ps[:, :, 0], place_next[:]))
                    step(v.tensor_tensor_scan(place_tables[s][:].rearrange("p t k -> p (t k)"),
                                              not_first[:].rearrange("p t k -> p (t k)"),
                                              bank[0][:, 0:TILES * (K + 1)], 0.0, ALU.mult, ALU.add))
                    step(v.tensor_copy(place_next[:], place_tables[s][:, :, K]))
                    step(v.tensor_copy(place_parts[s][:, 0], place_tables[s][:]))
                    step(v.tensor_tensor(place_parts[s][:, 1], place_tables[s][:], place_parts[s][:, 0], ALU.subtract))
                    dve.sem_inc(tables_made, 1)
                    dve.wait_ge(group_placed, n * NSG + RING)
                    all_hots((s + 1) % RING, n + 1)
                    dve.wait_ge(attr_loaded[s], (i + 1) * 16)
                    dve.wait_ge(payload_free, n + 1)
                    step(v.tensor_tensor(attr_products, attr[s][:].unsqueeze(2).broadcast_to([P, K, HEADS, EDGE_F]),
                                         att_w[:, :, 2 * HEAD_D:].unsqueeze(1).broadcast_to([P, K, HEADS, EDGE_F]),
                                         ALU.mult))
                    dve.sem_inc(attr_used, 1)
                    v.tensor_reduce(payload[s][:, :, 2:PAYLOAD], attr_products, AX.X, ALU.add)
                    v.tensor_copy(payload[s][:, :, 0], dst_f[:, chunk(n)])
                    v.tensor_copy(payload[s][:, :, 1], key[:, chunk(n)])
                    for g, (a, m) in enumerate(STEP_GROUPS):
                        c, r = n * NSG + g, (s * NSG + g) % RING
                        dve.wait_ge(same_made, c + 1)
                        dve.wait_ge(group_placed, c + 1)
                        v.tensor_tensor(same_hi[r][:, 0:m, :], same_ps[r][:, 0:m, :],
                                        later[:].unsqueeze(1).broadcast_to([P, m, P]), ALU.mult)\
                            .then_inc(same_masked, 1)
                    dve.wait_ge(group_placed, n * NSG + NSG + RING)
                    step(v.tensor_tensor(place_products, place_ps, lo_hot[s], ALU.mult))
                    dve.sem_inc(places_read, 1)
                    step(v.tensor_reduce(place_sums[:], place_products, AX.X, ALU.add))
                    step(v.tensor_scalar(index_ring[s][:], place_sums[:], float(HALF), None, ALU.add))
                    dve.sem_inc(payload_made, 1)
                step.leave(LOOPS)

            def group_of(array):
                def view(g, over_features=False):
                    a, m = TILE_GROUPS[g]
                    return array[:, a:a + m].unsqueeze(2).broadcast_to([P, m, D]) if over_features else array[:, a:a + m]
                return view

            Xg, Hg, Rg, Ug, stat_g, tmp_g = (group_of(array) for array in (X, H, R, U, stat, tmp_t))

            def normalise(n, update, results):
                for g in range(NTG):
                    if update:
                        update(g)
                    step(v.tensor_reduce(stat_g(g), Xg(g), AX.X, ALU.add))
                    step(v.tensor_scalar(stat_g(g), stat_g(g), 1.0 / D, None, ALU.mult))
                    step(v.tensor_tensor(Hg(g), Xg(g), stat_g(g, True), ALU.subtract))
                    step(v.tensor_tensor(Rg(g), Hg(g), Hg(g), ALU.mult))
                    step(v.tensor_reduce(stat_g(g), Rg(g), AX.X, ALU.add))
                step(v.tensor_scalar(stat[:], stat[:], 1.0 / D, 1e-5, ALU.mult, ALU.add))
                dve.sem_inc(squares_summed, 1)
                dve.wait_ge(roots_made, n)
                step(v.reciprocal(stat[:], stat2[:]))
                for g in range(NTG):
                    step(v.scalar_tensor_tensor(out=Hg(g), in0=Hg(g), scalar=0.0, in1=stat_g(g, True),
                                                op0=ALU.max, op1=ALU.mult))
                    for result in results:
                        dve.sem_inc(result, 1)

            def read_product(job, add):
                for g, (a, m) in enumerate(TILE_GROUPS):
                    dve.wait_ge(product_made, job * NTG + g + 1)
                    to, got = U[:, a:a + m, :], prod_ps[g % RING][:, 0:m, :]
                    (v.tensor_tensor(to, got, add(a, m), ALU.add) if add else v.tensor_copy(to, got))\
                        .then_inc(product_read, 1)
                    yield g

            def drained(generator):
                for _ in generator:
                    pass

            def product_done(job):
                dve.wait_ge(product_read, job * NTG + NTG)

            bias = lambda b: (lambda a, m: b.unsqueeze(1).broadcast_to([P, m, D]))

            dve.wait_ge(x_loaded, 16)
            normalise(1, None, [table_ready, product_input])

            def node_rows_of_steps(order):
                for s in range(RING):
                    step(v.tensor_copy(id_columns[:].rearrange("p (i j) -> p i j", j=sum(KP))
                                       [:, :, KP_BEFORE[s]:KP_BEFORE[s] + KP[s]],
                                       ids[order][:].rearrange("p (i k) -> p i k", k=RING * K)
                                       [:, :, s * K + KG[s]:(s + 1) * K]))
                for c, (a, m) in enumerate(ID_SPANS):
                    n = order * len(ID_SPANS) + c
                    dve.sem_inc(id_columns_made, 1)
                    dve.wait_ge(id_rows_T_made, n + 1)
                    if n:
                        dve.wait_ge(ids_stored, 16 * n)
                    step(v.tensor_copy(id_rows[0:m, :], id_rows_ps[0:m, :]))
                    dve.sem_inc(id_rows_made, 1)

            def split_parts(tiles_, a, rows, rest):
                part = lambda c: parts[:, tiles_, c, a:a + rows.shape[-1]]
                step(v.tensor_copy(part(0), rows))
                step(v.tensor_tensor(rest, rows, part(0), ALU.subtract))
                step(v.tensor_copy(part(1), rest))
                step(v.tensor_tensor(rest, rest, part(1), ALU.subtract))
                step(v.tensor_copy(part(2), rest))

            def new_table(job, add, early):
                def group_parts(g):
                    a, m = TILE_GROUPS[g]
                    split_parts(slice(a, a + m), 0, U[:, a:a + m, :], R[:, a:a + m, :])

                for g in read_product(job, add):
                    dve.wait_ge(product_read, job * NTG + g + 1)
                    dve.sem_inc(table_ready, 1)
                    if g < early:
                        group_parts(g)
                for g in range(early, NTG):
                    group_parts(g)
                dve.sem_inc(parts_ready, 1)

            def runs(order, before):
                v.tensor_tensor(cont[order][:, 1:], key[:, 1:], key[:, 0:STEPS - 1], ALU.is_equal)
                v.tensor_tensor(cont[order][:, 0:1], key[:, 0:1], before, ALU.is_equal)
                step(v.tensor_copy(key0_i[order][:], key[:, 0:1]))

            def fixes(order):
                dve.wait_ge(first_ends_read, 16 * (order + 1))
                step(v.tensor_scalar(tmp_1[:], row[:], float(STEPS), float(STEPS), ALU.mult, ALU.add))
                step(v.tensor_tensor(tmp_2[:], end_of_first[order][:], tmp_1[:], ALU.is_le))
                step(v.tensor_tensor(tmp_2[:], tmp_2[:], cont[order][:, 0:1], ALU.mult))
                step(v.tensor_scalar(tmp_1[:], row[:], float(SPARE), None, ALU.add))
                step(v.scalar_tensor_tensor(out=tmp_3[:], in0=end_of_first[order][:], scalar=-1.0,
                                            in1=tmp_1[:], op0=ALU.add, op1=ALU.subtract))
                step(v.tensor_tensor(tmp_3[:], tmp_3[:], tmp_2[:], ALU.mult))
                step(v.tensor_tensor(fix_row[order][:], tmp_3[:], tmp_1[:], ALU.add))
                step(v.tensor_reduce(tmp_1[:], cont[order][:], AX.X, ALU.min))
                step(v.tensor_scalar(diag[:], ident[:], tmp_1[:], None, ALU.mult))
                dve.sem_inc(diag_made, 1)
                dve.wait_ge(unbroken_read, order + 1)
                step(v.tensor_copy(unbroken[order][:], unbroken_ps))
                if order:
                    step(v.tensor_scalar(unbroken_limit[:], unbroken[1][:], -0.5, None, ALU.add))
                    step(v.tensor_scalar(unbroken_limit[:], unbroken_limit[:], BIG, 2.0, ALU.mult, ALU.mult))

            split_parts(slice(0, TILES), 0, H[:], R[:])
            dve.sem_inc(parts_ready, 1)
            dve.wait_ge(sorted_loaded, 32)
            step(v.tensor_copy(dst_i[:], sorted_sb[:, :, 0]))
            dve.sem_inc(rows_free, RING)
            node_rows_of_steps(0)
            step(v.tensor_scalar(node_id[:], spare_row[:], -float(PAD_EDGES), None, ALU.add))
            step(v.tensor_copy(key[:], sorted_sb[:, :, 1]))
            runs(0, key_before_f[:])
            dve.sem_inc(key0_made, 1)

            def attention(n, s, fill):
                over = lambda a: a[:].unsqueeze(2).broadcast_to([P, K, HEADS])

                def filled(ins):
                    step.begin(ins)
                    fill(1)
                    step.wait()

                filled(v.tensor_tensor(logit[:], gathered[s][:, :, D:WIDE], terms[:, chunk(n), :], ALU.add))
                filled(v.scalar_tensor_tensor(out=logit[:], in0=logit[:], scalar=0.2, in1=logit[:],
                                              op0=ALU.mult, op1=ALU.max))
                filled(v.tensor_reduce(top[:], logit[:], AX.X, ALU.max))
                filled(v.tensor_tensor(logit[:], logit[:], over(top), ALU.subtract))
                dve.sem_inc(logits_shifted, 1)
                fill(2)
                dve.wait_ge(exps_made, n + 1)
                filled(v.tensor_reduce(top[:], logit[:], AX.X, ALU.add))
                filled(v.reciprocal(top[:], top[:]))
                filled(v.tensor_tensor(logit[:], logit[:], over(top), ALU.mult))
                filled(v.tensor_tensor(scanned[s][:].rearrange("p k (h e) -> p k h e", h=HEADS),
                                       gathered[s][:, :, 0:D].rearrange("p k (h e) -> p k h e", h=HEADS),
                                       logit[:].unsqueeze(3).broadcast_to([P, K, HEADS, HEAD_D]), ALU.mult))

            def count_dst(m, s):
                dve.wait_ge(count_hot_used, m + 1 + CHUNKS)
                one_hot(dhi_hot[s], P, dst_hi, m)
                one_hot(dlo_hot[s], TILES, dst_lo, m).then_inc(count_hot_made, 1)

            def hots(pass_no, i, s, rows):
                n = i * RING + s + pass_no * CHUNKS
                for t in rows:
                    g, b = divmod(t, HOT_TILES)
                    if t == 0:
                        dve.wait_ge(ids_loaded[s], (i + 1) * 16 + pass_no * (16 * LOOPS))
                    if b == 0:
                        dve.wait_ge(node_hot_used, n * HOT_GROUPS + g + 1)
                    made = v.tensor_scalar(node_hot[g][:, b, 0:KP[s] * P], ids_row[s][:], node_id[:, t:t + 1],
                                           None, ALU.is_equal)
                    if b == HOT_TILES - 1:
                        made.then_inc(node_hot_made, 1)

            def first_hots(pass_no):
                hots(pass_no, 0, 0, range(TILES))

            def scan_edges(pass_no, order, op, gate, message=None, beside=None, before_join=None, more=True):
                reset, neutral = (ALU.mult, 0.0) if op == ALU.add else (ALU.min, -BIG)
                width = WIDE if message else D

                def body(i, s, ahead):
                    m = i * RING + s
                    n = m + pass_no * CHUNKS

                    def wait_rows(h):
                        each = 16 * len(GATHERS[s][h])
                        dve.wait_ge(rows_gathered[s][h], (i + 1) * each + pass_no * (each * LOOPS))

                    dve.wait_ge(fetched_copied, n + 1 + RING)
                    rows = gathered[s][:, KG[s]:K, 0:width]
                    part = lambda c: fetched[:, 0:KP[s], c * width:(c + 1) * width]
                    step(v.tensor_tensor(rows, part(0), part(1), ALU.add))
                    step(v.tensor_tensor(rows, rows, part(2), ALU.add))
                    dve.sem_inc(fetched_summed, 1)
                    if beside:
                        beside(m, s)
                    wait_rows(0)
                    dve.wait_ge(scan_slot_free, n + 1)
                    hots_made = 0

                    def fill(rows):
                        nonlocal hots_made
                        upto = min(hots_made + rows, TILES)
                        if ahead:
                            hots(pass_no, i + 1, s, range(hots_made, upto))
                        hots_made = upto

                    if message:
                        wait_rows(1)
                        message(m, s, fill)
                        dve.sem_inc(rows_free, 1)
                    rest = TILES - hots_made
                    for k in range(K):
                        before = scanned[s][:, k - 1, :] if k else state[:]
                        row = (scanned if message else gathered)[s][:, k, 0:D]
                        if k == GATHERS[s][1][0] and not message:
                            wait_rows(1)
                        step.wait()
                        step.begin(v.scalar_tensor_tensor(out=scanned[s][:, k, :], in0=before,
                                                          scalar=gate[:, bass.ds(m * K + k, 1)], in1=row,
                                                          op0=reset, op1=op))
                        fill(rest * (k + 1) // K - rest * k // K)
                    step.wait()
                    dve.sem_inc(chunk_scanned, 1)
                    if not message:
                        dve.sem_inc(rows_free, 1)
                    step.begin(v.tensor_copy(state[:], scanned[s][:, K - 1, :]))

                step.begin(v.memset(state[:], neutral))
                for s in range(1, RING):
                    hots(pass_no, 0, s, range(TILES))
                with dve.Fori(0, LOOPS - 1) as i:
                    step.enter(i, RING * (K + 3 + (8 if message else 0)))
                    for s in range(RING):
                        body(i, s, True)
                    step.leave(LOOPS - 1)
                for s in range(RING):
                    body(LOOPS - 1, s, False)
                step.wait()
                if before_join:
                    before_join()
                dve.sem_inc(state_ready, 1)
                dve.wait_ge(state_T_made, pass_no + 1)
                across = unbroken[order] if op == ALU.add else unbroken_limit
                step(v.tensor_tensor_scan(joined_T[:, 1:], across[:], state_T_ps, neutral, reset, op))
                dve.sem_inc(joined_T_made, 1)
                dve.wait_ge(joined_made, pass_no + 1)
                dve.wait_ge(fix_read, (pass_no + 1) * 16)
                step(v.tensor_tensor(fix_rows[:], fix_rows[:], joined_ps, op))
                dve.sem_inc(fix_made, 1)
                if more:
                    first_hots(pass_no + 1)

            def node_group(pass_no, g):
                dve.wait_ge(nodes_read[g], 16 * TILE_GROUPS[g][1] * (pass_no + 1))

            dve.sem_inc(fetched_summed, 1)
            first_hots(P_SAGE)

            def counts_and_fixes():
                dve.wait_ge(counted, 2)
                step(v.tensor_copy(degree[1][:], count_ps[1]))
                fixes(0)

            scan_edges(P_SAGE, 0, ALU.add, cont[0], beside=count_dst, before_join=counts_and_fixes)
            drained(read_product(J_L, bias(bias_l[:])))
            product_done(J_L)
            step(v.tensor_tensor(U[:], U[:], bias_r[:].unsqueeze(1).broadcast_to([P, TILES, D]), ALU.add))
            bounds(1)
            step(v.tensor_copy(key[:], dst_f[:]))
            step(v.tensor_copy(tmp_1[:], key_before_i[:]))
            runs(1, tmp_1[:])
            dve.sem_inc(key0_made, 1)
            step(v.tensor_scalar(limit[:], cont[1][:], -0.5, None, ALU.add))
            step(v.tensor_scalar(limit[:], limit[:], BIG, 2.0, ALU.mult, ALU.mult))
            node_rows_of_steps(1)
            step(v.tensor_scalar(tmp_t[:], degree[0][:], 1.0, None, ALU.max))
            step(v.reciprocal(tmp_t[:], tmp_t[:]))

            def relu_squares(g):
                dve.wait_ge(product_read, J_R * NTG + g + 1)
                step(v.tensor_scalar(Ug(g), Ug(g), 0.0, None, ALU.max))
                step(v.tensor_tensor(squares_g(g), Ug(g), Ug(g), ALU.mult))
                step(v.tensor_reduce(stat_g(g), squares_g(g), AX.X, ALU.add))

            squares_g = group_of(H)
            products_of_means = read_product(J_R, lambda a, m: U[:, a:a + m, :])
            for g in range(NTG):
                node_group(P_SAGE, g)
                step(v.tensor_tensor(Rg(g), Rg(g), tmp_g(g, True), ALU.mult))
                dve.sem_inc(product_input, 1)
                if g >= 2:
                    relu_squares(next(products_of_means))
            for g in products_of_means:
                relu_squares(g)
            dve.sem_inc(squares_summed, 1)
            dve.wait_ge(roots_made, 2)
            norm_g = group_of(tmp_t)
            step(v.tensor_scalar(tmp_t[:], stat2[:], 1e-6, None, ALU.add))
            step(v.reciprocal(tmp_t[:], tmp_t[:]))

            def add_normed(g):
                step(v.tensor_tensor(Ug(g), Ug(g), norm_g(g, True), ALU.mult))
                step(v.tensor_tensor(Xg(g), Xg(g), Ug(g), ALU.add))

            normalise(3, add_normed, [product_input])
            drained(read_product(J_WH, None))
            product_done(J_WH)
            for term, a0, ready in ((src_term, 0, src_terms_ready), (dst_term, HEAD_D, dst_terms_ready)):
                for h in range(HEADS):
                    step(v.tensor_tensor(R[:, :, h * HEAD_D:(h + 1) * HEAD_D], U[:, :, h * HEAD_D:(h + 1) * HEAD_D],
                                         att_w[:, h, a0:a0 + HEAD_D].unsqueeze(1).broadcast_to([P, TILES, HEAD_D]),
                                         ALU.mult))
                step(v.tensor_reduce(term[:], R[:].rearrange("p t (h e) -> p t h e", h=HEADS), AX.X, ALU.add))
                dve.sem_inc(ready, 1)
            split_parts(slice(0, TILES), 0, U[:], R[:])
            split_parts(slice(0, TILES), D, dst_term[:], R[:, :, 0:HEADS])
            dve.sem_inc(parts_ready, 1)
            fixes(1)
            dve.wait_ge(first_terms_read, 16)
            dve.wait_ge(src_terms_loaded, 16)
            step(v.tensor_copy(terms[:, 0, :], first_terms[:]))
            for h in range(HEADS):
                step(v.tensor_tensor_scan(terms[:, :, h], cont[0][:], terms[:, :, h], 0.0, ALU.mult, ALU.add))
            step(v.tensor_tensor(terms[:], terms[:], sorted_sb[:, :, 2:PAYLOAD], ALU.add))
            scan_edges(P_ATT, 0, ALU.add, cont[0], attention)

            def add_elu(g):
                node_group(P_ATT, g)
                step(v.tensor_scalar(Ug(g), Rg(g), 0.0, None, ALU.min))
                dve.sem_inc(elu_input, 1)
                dve.wait_ge(elu_exp, g + 1)
                step(v.tensor_scalar(Ug(g), Ug(g), -1.0, None, ALU.add))
                step(v.scalar_tensor_tensor(out=Rg(g), in0=Rg(g), scalar=0.0, in1=Ug(g), op0=ALU.max, op1=ALU.add))
                step(v.tensor_tensor(Xg(g), Xg(g), Rg(g), ALU.add))

            normalise(4, add_elu, [product_input])
            new_table(J_CONV, bias(bias_2[:, 0, :]), 0)
            with dve.Fori(0, ROUNDS - 1) as r:
                step.enter(r, 1 + CHUNKS * (K + 3) + 2 + 5 * NTG)
                scan_edges(r + P_MAX, 1, ALU.max, limit)
                new_table(r + J_CONV + 1, lambda a, m: bias_2[:, bass.ds(r + 1, 1), :].broadcast_to([P, m, D]),
                          NTG - 3)
                step.leave(ROUNDS - 1)
            scan_edges(P_MAX + ROUNDS - 1, 1, ALU.max, limit)

            def add_rows(g):
                node_group(P_MAX + ROUNDS - 1, g)
                step(v.tensor_tensor(Xg(g), Xg(g), Rg(g), ALU.add))

            normalise(5, add_rows, [table_ready])
            split_parts(slice(0, TILES), 0, H[:], R[:])
            dve.sem_inc(parts_ready, 1)
            scan_edges(P_GCN_S, 0, ALU.add, cont[0])
            for g in range(NTG):
                node_group(P_GCN_S, g)
                step(v.tensor_copy(Ug(g), Rg(g)))
            dve.sem_inc(parts_ready, 1)
            scan_edges(P_GCN_D, 1, ALU.add, cont[1], more=False)
            step(v.tensor_tensor(stat[:], degree[0][:], degree[1][:], ALU.add))
            step(v.tensor_scalar(stat[:], stat[:], 1.0, None, ALU.max))
            dve.sem_inc(squares_summed, 1)
            dve.wait_ge(roots_made, 6)
            step(v.reciprocal(tmp_t[:], stat2[:]))
            for g in range(NTG):
                node_group(P_GCN_D, g)
                step(v.tensor_tensor(Rg(g), Rg(g), Ug(g), ALU.add))
                step(v.tensor_tensor(Rg(g), Rg(g), tmp_g(g, True), ALU.mult))
                dve.sem_inc(product_input, 1)
            products = read_product(J_GCN, bias(bias_3[:]))
            for g in range(NTG + 1):
                if g < NTG:
                    next(products)
                    dve.wait_ge(product_read, J_GCN * NTG + g + 1)
                    step(v.tensor_tensor(Ug(g), Ug(g), Hg(g), ALU.add))
                    dve.sem_inc(gelu_input, 1)
                if g >= 1:
                    dve.wait_ge(gelu_made, g)
                    step(v.tensor_tensor(Xg(g - 1), Xg(g - 1), Ug(g - 1), ALU.add))
                    dve.sem_inc(out_ready, 1)


INPUTS = ["x", "src", "dst", "edge_attr_16", "L0_gnn_Wl", "L0_gnn_Wr", "L1_gnn_W", "L2_gnn_Ws", "L3_gnn_W",
          "L0_gnn_bl", "L0_gnn_br", "L2_gnn_bs", "L3_gnn_b", "L1_gnn_a"]


def kernel(**inputs):
    import numpy as np
    import concourse.bacc as bacc
    from concourse.bass_utils import run_bass_kernel_spmd

    a = {name: np.asarray(inputs[name]) for name in INPUTS}

    def padded(values, rows, fill):
        more = np.full((rows - values.shape[0],) + values.shape[1:], fill, values.dtype)
        return np.concatenate([values, more])

    a["x"] = padded(a["x"], PAD_NODES, 0)
    a["src"] = padded(a["src"], PAD_EDGES, PAD_NODES - 1)
    a["dst"] = padded(a["dst"], PAD_EDGES, PAD_NODES - 1)
    a["edge_attr_16"] = padded(a["edge_attr_16"], PAD_EDGES, 0)
    a["L2_gnn_Ws"] = a["L2_gnn_Ws"].transpose(0, 2, 1)
    a["L3_gnn_W"] = a["L3_gnn_W"].T
    for name in ("L0_gnn_bl", "L0_gnn_br", "L2_gnn_bs", "L3_gnn_b", "L1_gnn_a"):
        a[name] = a[name].reshape(1, -1)

    nc = bacc.Bacc("TRN2", target_bir_lowering=False, num_devices=1)
    arrays, args = {}, []
    for name in INPUTS:
        arrays[f"in_{name}"] = np.ascontiguousarray(a[name])
        args.append(nc.dram_tensor(f"in_{name}", a[name].shape, mybir.dt.from_np(a[name].dtype),
                                   kind="ExternalInput").ap())
    out = nc.dram_tensor("out_0", (PAD_NODES, D), F32, kind="ExternalOutput").ap()
    build(nc, *args, out)
    r = run_bass_kernel_spmd(nc, [arrays], core_ids=[0])
    return r.results[0]["out_0"][:NODES]
```
